# Optimizing a Trainium2 kernel written in Bass

```python
import numpy as np
import jax
import jax.numpy as jnp

def _softmax(x, axis=-1):
    return jax.nn.softmax(x, axis=axis)

def _gelu(x):
    return jax.nn.gelu(x, approximate=True)

def _silu(x):
    return jax.nn.silu(x)

def _sigmoid(x):
    return jax.nn.sigmoid(x)

def _layernorm(x, axis=-1, eps=1e-05):
    m = jnp.mean(x, axis=axis, keepdims=True)
    v = jnp.var(x, axis=axis, keepdims=True)
    return (x - m) / jnp.sqrt(v + eps)

def _scatter_add(tgt, idx, src, axis=0):
    return tgt.at[idx].add(src)

def _segment_sum(src, seg, n):
    return jax.ops.segment_sum(src, seg, n)
kernel_name = 'mk_hybrid_d1_jaxref_r8_eeeca3'

def setup_inputs(seed: int=0):
    np.random.seed(seed)
    _w = jnp.asarray

    def _L0_attn_a_setup():
        import jax, jax.numpy as jnp
        import numpy as np
        D_MODEL = 128
        N_HEADS = 16
        HEAD_DIM = D_MODEL // N_HEADS
        LORA_RANK = 16
        LORA_SCALING = 1.0 / LORA_RANK

        def lora_linear(x, w, a, b):
            return x @ w.T + LORA_SCALING * (x @ a.T @ b.T)
        key = jax.random.key(seed)
        ks = jax.random.split(key, 14)
        B, S = (4, 256)

        def w(k, shape, scale=0.02):
            return jax.random.normal(k, shape, dtype=jnp.float32) * scale
        inp = {'x': jax.random.normal(ks[0], (B, S, D_MODEL), dtype=jnp.float32), 'wq': w(ks[1], (D_MODEL, D_MODEL)), 'aq': w(ks[2], (LORA_RANK, D_MODEL)), 'bq': w(ks[3], (D_MODEL, LORA_RANK)), 'wk': w(ks[4], (D_MODEL, D_MODEL)), 'ak': w(ks[5], (LORA_RANK, D_MODEL)), 'bk': w(ks[6], (D_MODEL, LORA_RANK)), 'wv': w(ks[7], (D_MODEL, D_MODEL)), 'av': w(ks[8], (LORA_RANK, D_MODEL)), 'bv': w(ks[9], (D_MODEL, LORA_RANK)), 'wo': w(ks[10], (D_MODEL, D_MODEL)), 'ao': w(ks[11], (LORA_RANK, D_MODEL)), 'bo': w(ks[12], (D_MODEL, LORA_RANK))}
        return inp
    _L0_attn_a_in = _L0_attn_a_setup()

    def _L0_attn_b_setup():
        import jax, jax.numpy as jnp
        import numpy as np
        import math
        D_MODEL = 128
        N_HEADS = 16
        LATENT = 32
        key = jax.random.key(seed)
        ks = jax.random.split(key, 9)
        B, T, C, L = (2, 256, D_MODEL, LATENT)
        s = 0.02
        return {'x': jax.random.normal(ks[0], (B, T, C), dtype=jnp.float32), 'Wq': jax.random.normal(ks[1], (C, C), dtype=jnp.float32) * s, 'bq': jnp.zeros((C,), dtype=jnp.float32), 'Wkd': jax.random.normal(ks[2], (C, 2 * L), dtype=jnp.float32) * s, 'bkd': jnp.zeros((2 * L,), dtype=jnp.float32), 'Wku': jax.random.normal(ks[3], (L, 2 * C), dtype=jnp.float32) * s, 'bku': jnp.zeros((2 * C,), dtype=jnp.float32), 'Wo': jax.random.normal(ks[4], (C, C), dtype=jnp.float32) * s, 'bo': jnp.zeros((C,), dtype=jnp.float32)}
    _L0_attn_b_in = _L0_attn_b_setup()

    def _L0_ffn_setup():
        import jax, jax.numpy as jnp
        import numpy as np
        B, T, D = (4, 256, 128)
        FF = 512
        E = 8
        TOP_K = 2
        key = jax.random.key(seed)
        k1, k2, k3, k4 = jax.random.split(key, 4)
        x = jax.random.normal(k1, (B, T, D), dtype=jnp.float32)
        router_w = jax.random.normal(k2, (E, D), dtype=jnp.float32) * 0.02
        w1 = jax.random.normal(k3, (E, FF, D), dtype=jnp.float32) * 0.02
        w2 = jax.random.normal(k4, (E, D, FF), dtype=jnp.float32) * 0.02
        return {'x': x, 'router_w': router_w, 'w1': w1, 'w2': w2}
    _L0_ffn_in = _L0_ffn_setup()
    _d = {'L0_attn_a_x': _L0_attn_a_in['x'], 'L0_attn_a_wq': _L0_attn_a_in['wq'], 'L0_attn_a_aq': _L0_attn_a_in['aq'], 'L0_attn_a_bq': _L0_attn_a_in['bq'], 'L0_attn_a_wk': _L0_attn_a_in['wk'], 'L0_attn_a_ak': _L0_attn_a_in['ak'], 'L0_attn_a_bk': _L0_attn_a_in['bk'], 'L0_attn_a_wv': _L0_attn_a_in['wv'], 'L0_attn_a_av': _L0_attn_a_in['av'], 'L0_attn_a_bv': _L0_attn_a_in['bv'], 'L0_attn_a_wo': _L0_attn_a_in['wo'], 'L0_attn_a_ao': _L0_attn_a_in['ao'], 'L0_attn_a_bo': _L0_attn_a_in['bo'], 'L0_attn_b_Wq': _L0_attn_b_in['Wq'], 'L0_attn_b_bq': _L0_attn_b_in['bq'], 'L0_attn_b_Wkd': _L0_attn_b_in['Wkd'], 'L0_attn_b_bkd': _L0_attn_b_in['bkd'], 'L0_attn_b_Wku': _L0_attn_b_in['Wku'], 'L0_attn_b_bku': _L0_attn_b_in['bku'], 'L0_attn_b_Wo': _L0_attn_b_in['Wo'], 'L0_attn_b_bo': _L0_attn_b_in['bo'], 'L0_ffn_router_w': _L0_ffn_in['router_w'], 'L0_ffn_w1': _L0_ffn_in['w1'], 'L0_ffn_w2': _L0_ffn_in['w2']}
    _x0 = _d['L0_attn_a_x']
    _d['L0_attn_a_x'] = jax.random.normal(jax.random.fold_in(jax.random.key(seed), 1), (4, 1024, 128), dtype=_x0.dtype)
    del _x0
    return _d

def reference(L0_attn_a_x, L0_attn_a_wq, L0_attn_a_aq, L0_attn_a_bq, L0_attn_a_wk, L0_attn_a_ak, L0_attn_a_bk, L0_attn_a_wv, L0_attn_a_av, L0_attn_a_bv, L0_attn_a_wo, L0_attn_a_ao, L0_attn_a_bo, L0_attn_b_Wq, L0_attn_b_bq, L0_attn_b_Wkd, L0_attn_b_bkd, L0_attn_b_Wku, L0_attn_b_bku, L0_attn_b_Wo, L0_attn_b_bo, L0_ffn_router_w, L0_ffn_w1, L0_ffn_w2):

    def _L0_attn_a_ref(x, wq, aq, bq, wk, ak, bk, wv, av, bv, wo, ao, bo):
        import jax, jax.numpy as jnp
        import numpy as np
        D_MODEL = 128
        N_HEADS = 16
        HEAD_DIM = D_MODEL // N_HEADS
        LORA_RANK = 16
        LORA_SCALING = 1.0 / LORA_RANK

        def lora_linear(x, w, a, b):
            return x @ w.T + LORA_SCALING * (x @ a.T @ b.T)
        B, S, _ = x.shape

        def split_heads(t):
            return t.reshape(B, S, N_HEADS, HEAD_DIM).transpose(0, 2, 1, 3)
        q = split_heads(lora_linear(x, wq, aq, bq))
        k = split_heads(lora_linear(x, wk, ak, bk))
        v = split_heads(lora_linear(x, wv, av, bv))
        scores = jnp.einsum('bhqd,bhkd->bhqk', q, k) / jnp.sqrt(jnp.float32(HEAD_DIM))
        causal = jnp.tril(jnp.ones((S, S), dtype=bool))
        scores = jnp.where(causal, scores, -jnp.inf)
        attn = jax.nn.softmax(scores, axis=-1)
        ctx = jnp.einsum('bhqk,bhkd->bhqd', attn, v)
        ctx = ctx.transpose(0, 2, 1, 3).reshape(B, S, D_MODEL)
        return lora_linear(ctx, wo, ao, bo)

    def _L0_attn_b_ref(x, Wq, bq, Wkd, bkd, Wku, bku, Wo, bo):
        import jax, jax.numpy as jnp
        import numpy as np
        import math
        D_MODEL = 128
        N_HEADS = 16
        LATENT = 32
        B, T, C = x.shape
        H = N_HEADS
        D = C // H
        L = LATENT
        q = (x @ Wq + bq).reshape(B, T, H, D)
        kv_latent = jax.nn.gelu(x @ Wkd + bkd, approximate=False)
        lat = kv_latent[..., :L] + kv_latent[..., L:]
        kv = lat @ Wku + bku
        k = kv[..., :C].reshape(B, T, H, D)
        v = kv[..., C:].reshape(B, T, H, D)
        scale = 1.0 / math.sqrt(D)
        attn = jnp.einsum('bqhd,bkhd->bhqk', q, k) * scale
        causal = jnp.tril(jnp.ones((T, T), dtype=bool))
        attn = jnp.where(causal, attn, -jnp.inf)
        attn = jax.nn.softmax(attn, axis=-1)
        out = jnp.einsum('bhqk,bkhd->bqhd', attn, v).reshape(B, T, C)
        return out @ Wo + bo

    def _L0_ffn_ref(x, router_w, w1, w2):
        import jax, jax.numpy as jnp
        import numpy as np
        B, T, D = (4, 256, 128)
        FF = 512
        E = 8
        TOP_K = 2
        Bx, Tx, Dx = x.shape
        N = Bx * Tx
        xf = x.reshape(N, Dx)
        logits = xf @ router_w.T
        top_vals, top_idx = jax.lax.top_k(logits, TOP_K)
        gate = jax.nn.softmax(top_vals.astype(jnp.float32), axis=-1).astype(x.dtype)
        comb = jnp.zeros((N, E), dtype=x.dtype).at[jnp.arange(N)[:, None], top_idx].add(gate)
        out = jnp.zeros((N, Dx), dtype=x.dtype)
        for e in range(E):
            h = jax.nn.gelu(xf @ w1[e].T, approximate=False)
            out = out + comb[:, e:e + 1] * (h @ w2[e].T)
        return out.reshape(Bx, Tx, Dx)
    x = L0_attn_a_x
    x = x + _L0_attn_a_ref(_layernorm(x, axis=-1), L0_attn_a_wq, L0_attn_a_aq, L0_attn_a_bq, L0_attn_a_wk, L0_attn_a_ak, L0_attn_a_bk, L0_attn_a_wv, L0_attn_a_av, L0_attn_a_bv, L0_attn_a_wo, L0_attn_a_ao, L0_attn_a_bo)
    x = x + _L0_ffn_ref(_layernorm(x, axis=-1), L0_ffn_router_w, L0_ffn_w1, L0_ffn_w2)
    x = x + _L0_attn_b_ref(_layernorm(x, axis=-1), L0_attn_b_Wq, L0_attn_b_bq, L0_attn_b_Wkd, L0_attn_b_bkd, L0_attn_b_Wku, L0_attn_b_bku, L0_attn_b_Wo, L0_attn_b_bo)
    x = x + _L0_ffn_ref(_layernorm(x, axis=-1), L0_ffn_router_w, L0_ffn_w1, L0_ffn_w2)
    return x

_drawn_inputs = setup_inputs


def setup_inputs(seed=0):
    import zlib

    import numpy as np

    out = dict(_drawn_inputs(seed))
    spreads = {'L0_attn_b_bq': (0.0, 0.8),
     'L0_attn_b_bkd': (0.0, 0.8),
     'L0_attn_b_bku': (0.0, 0.322),
     'L0_attn_b_bo': (0.0, 0.1)}
    factors = {'L0_attn_a_wq': 8.0,
     'L0_attn_a_aq': 8.0,
     'L0_attn_a_bq': 8.0,
     'L0_attn_a_wk': 8.0,
     'L0_attn_a_ak': 8.0,
     'L0_attn_a_bk': 8.0,
     'L0_attn_a_wv': 8.0,
     'L0_attn_a_av': 8.0,
     'L0_attn_a_bv': 8.0,
     'L0_attn_a_wo': 8.0,
     'L0_attn_a_ao': 8.0,
     'L0_attn_a_bo': 8.0,
     'L0_attn_b_Wq': 8.0,
     'L0_attn_b_Wkd': 8.0,
     'L0_attn_b_Wku': 8.0}
    for name, (base, spread) in spreads.items():
        noise = np.random.default_rng([zlib.crc32(name.encode()), seed]).standard_normal(out[name].shape)
        drawn = base * np.exp(spread * noise) if base else spread * noise
        out[name] = jnp.asarray(drawn.astype(out[name].dtype))
    for name, factor in factors.items():
        out[name] = (out[name] * factor).astype(out[name].dtype)
    return out
```

```python
from contextlib import ExitStack

import concourse.bass as bass
from concourse import mybir

ALU = mybir.AluOpType
ACT = mybir.ActivationFunctionType
AX = mybir.AxisListType
F32 = mybir.dt.float32
BF16 = mybir.dt.bfloat16
U32 = mybir.dt.uint32

P = 128
D = 128
B = 4
S = 1024
NT = B * S
TILES = NT // P
H = 16
HD = D // H
EPS = 1e-5
NEG = -1e30

HG = 4
GROUPS = B * (H // HG)
QB = S // P
CH = 512
PARTS = 3
ROWS = PARTS * PARTS * HD
MROW = 96
VW = 32

E_N = 8
FF = 512
FC = FF // P


UNITS = [(0, 0), (0, 3), (0, 2), (0, 1),
         (1, 0), (1, 1), (1, 2), (1, 3), (1, 7), (1, 6), (1, 5), (1, 4)]
NU = len(UNITS)
NDIAG = sum(j >= 4 * c for c, j in UNITS)
LAST = {c: max(u for u, (cc, _) in enumerate(UNITS) if cc == c) for c in (0, 1)}
PBUF = 4
LAG = 2


def unit_cols(u):
    c, j = UNITS[u]
    q0 = max(P * j, CH * c)
    return q0, CH * (c + 1) - q0


def max_steps():
    steps = []
    for i in range(QB):
        keys = P * (i + 1)
        first = min(keys, CH)
        per = CH // first if CH % first == 0 else 1
        for h in range(0, HG, per):
            steps.append((i, h, per, 0, first, 0))
        if keys > CH:
            rest = keys - CH
            per = {P: 4, 2 * P: 2}.get(rest, 1)
            for h in range(0, HG, per):
                steps.append((i, h, per, CH, rest, 1))
    return steps


STEPS = max_steps()
NSTEP = len(STEPS)


def spread():
    total = sum(per * n for _, _, per, _, n, _ in STEPS)
    cols = [unit_cols(u)[1] for u in range(NU)]
    upto = sum(cols[:MT_UNIT])
    plan, s, done, run = [[] for _ in range(NU)], 0, 0, 0
    for u in range(MT_UNIT):
        run += cols[u]
        while s < NSTEP and done + STEPS[s][2] * STEPS[s][4] / 2 <= total * run / upto + 1e-6:
            done += STEPS[s][2] * STEPS[s][4]
            plan[u].append(s)
            s += 1
    plan[MT_UNIT - 1] += list(range(s, NSTEP))
    return plan


MT_UNIT = 10
PLAN = spread()
assert NSTEP % 2 == 0 and sum(map(len, PLAN)) == NSTEP and NU % PBUF == 0


def layer_norm(nc, tag, x, xn, xnT, ident):
    with ExitStack() as ctx:
        sb = lambda n, s, d: ctx.enter_context(nc.sbuf_tensor(f"{tag}_{n}", s, d))
        sem = lambda n: ctx.enter_context(nc.semaphore(f"{tag}_{n}"))
        stats = sb("stats", [P, TILES, 6], F32)
        mean = sb("mean", [P, TILES], F32)
        half = sb("half", [P, TILES], F32)
        sq = sb("sq", [P, TILES], F32)
        var = sb("var", [P, TILES], F32)
        std = sb("std", [P, TILES], F32)
        rstd = sb("rstd", [P, TILES], F32)
        bank = [ctx.enter_context(nc.psum_tensor(f"{tag}_bank{i}", [P, CH], F32)) for i in range(2)]
        stats_done, small, std_done = sem("stats_done"), sem("small"), sem("std_done")
        xn_ready, turned, copied = sem("xn_ready"), sem("turned"), sem("copied")
        block = ctx.enter_context(nc.Block())

        @block.vector
        def _(dve):
            with dve.Fori(0, TILES // 4) as i:
                for t, k in ((4 * i, k) for k in range(4)):
                    nc.vector.bn_stats(stats[:, t + k, :], x[:, t + k, :]).then_inc(stats_done, 1)
            dve.wait_ge(stats_done, TILES)
            me, mo, ve, vo = (stats[:, :, k] for k in (1, 4, 2, 5))
            nc.vector.tensor_tensor(mean[:], me, mo, ALU.add).then_inc(small, 1)
            nc.vector.tensor_tensor(half[:], me, mo, ALU.subtract).then_inc(small, 1)
            nc.vector.tensor_tensor(var[:], ve, vo, ALU.add).then_inc(small, 1)
            dve.wait_ge(small, 3)
            nc.vector.tensor_scalar(mean[:], mean[:], 0.5, None, ALU.mult).then_inc(small, 1)
            nc.vector.scalar_tensor_tensor(out=sq[:], in0=half[:], scalar=0.25, in1=half[:],
                                           op0=ALU.mult, op1=ALU.mult).then_inc(small, 1)
            nc.vector.tensor_scalar(var[:], var[:], 1.0 / D, EPS, ALU.mult, ALU.add).then_inc(small, 1)
            dve.wait_ge(small, 6)
            nc.vector.tensor_tensor(var[:], var[:], sq[:], ALU.add).then_inc(small, 1)
            dve.wait_ge(std_done, 1)
            nc.vector.reciprocal(rstd[:], std[:]).then_inc(small, 1)
            dve.wait_ge(small, 8)
            with dve.Fori(0, TILES // 4) as i:
                for t, k in ((4 * i, k) for k in range(4)):
                    nc.vector.tensor_scalar(xn[:, t + k, :], x[:, t + k, :], mean[:, bass.ds(t + k, 1)],
                                            rstd[:, bass.ds(t + k, 1)], ALU.subtract,
                                            ALU.mult).then_inc(xn_ready, 1)

        @block.tensor
        def _(pe):
            for g in range(TILES // 4):
                pe.wait_ge(xn_ready, 4 * (g + 1))
                if g >= 2:
                    pe.wait_ge(copied, g - 1)
                for k in range(4):
                    last = nc.tensor.transpose(bank[g % 2][:, k * P:(k + 1) * P], xn[:, 4 * g + k, :],
                                               ident[:])
                last.then_inc(turned, 1)

        @block.scalar
        def _(act):
            act.wait_ge(small, 7)
            nc.scalar.activation(std[:], var[:], ACT.Sqrt).then_inc(std_done, 1)
            for g in range(TILES // 4):
                act.wait_ge(turned, g + 1)
                nc.scalar.activation(xnT[:, g * CH:(g + 1) * CH], bank[g % 2][:], ACT.Copy).then_inc(copied, 1)


def project_a(nc, tag, w, xnT, v_sb, q_dram, k_dram):
    project(nc, tag, xnT, v_sb, q_dram, k_dram, w["q"], w["k"], w["v"], None, None, None, None)


def project(nc, tag, xnT, v_sb, q_dram, k_dram, wq, wk, wv, bq, bk, bv, latent):
    N = NT // CH
    with ExitStack() as ctx:
        sb = lambda n, s, d: ctx.enter_context(nc.sbuf_tensor(f"{tag}_{n}", s, d))
        sem = lambda n: ctx.enter_context(nc.semaphore(f"{tag}_{n}"))
        ps = lambda n: [ctx.enter_context(nc.psum_tensor(f"{tag}_{n}{i}", [P, CH], F32)) for i in range(2)]
        qk_bank, v_bank, l_bank = ps("qk"), ps("v"), ps("l")
        parts = [sb(f"parts{i}", [P, PARTS, CH], BF16) for i in range(2)]
        rest = [sb(f"rest{i}", [P, CH], F32) for i in range(2)]
        gl = [sb(f"gl{i}", [64, CH], F32) for i in range(2)] if latent else None
        qk_ready, first_done, rest_done, second_done = sem("qk_ready"), sem("first"), sem("rest"), sem("second")
        third_done, stored, v_ready, v_copied = sem("third"), [sem("stored0"), sem("stored1")], sem("v_ready"), sem("v_copied")
        l_ready, l_done = sem("l_ready"), sem("l_done")
        block = ctx.enter_context(nc.Block())

        @block.tensor
        def _(pe):
            for c in range(N):
                src = xnT[:, c * CH:(c + 1) * CH]
                if latent:
                    if c >= 2:
                        pe.wait_ge(l_done, c - 1)
                    nc.tensor.matmul(l_bank[c % 2][0:64, :], latent["wkd"][:], src, start=True,
                                     stop=True).then_inc(l_ready, 1)
                for s in range(2):
                    n = 2 * c + s
                    if n >= 2:
                        pe.wait_ge(first_done, n - 1)
                        pe.wait_ge(rest_done, n - 1)
                    if s and latent:
                        pe.wait_ge(l_done, c + 1)
                        nc.tensor.matmul(qk_bank[n % 2][:], wk, gl[c % 2][:], start=True,
                                         stop=True).then_inc(qk_ready, 1)
                    else:
                        nc.tensor.matmul(qk_bank[n % 2][:], wk if s else wq, src, start=True,
                                         stop=True).then_inc(qk_ready, 1)
                if c >= 2:
                    pe.wait_ge(v_copied, c - 1)
                for k in range(4):
                    left = gl[c % 2][:, k * P:(k + 1) * P] if latent else xnT[:, c * CH + k * P:c * CH + (k + 1) * P]
                    last = nc.tensor.matmul(v_bank[c % 2][:, k * P:(k + 1) * P], left, wv, start=True, stop=True)
                last.then_inc(v_ready, 1)

        @block.scalar
        def _(act):
            for c in range(N):
                if latent:
                    act.wait_ge(l_ready, c + 1)
                    if c >= 2:
                        act.wait_ge(v_ready, c - 1)
                    nc.scalar.activation(gl[c % 2][:], l_bank[c % 2][0:64, :], ACT.Gelu,
                                         bias=latent["bkd"][:, 0:1]).then_inc(l_done, 1)
                for s in range(2):
                    n = 2 * c + s
                    act.wait_ge(qk_ready, n + 1)
                    if n >= 2:
                        act.wait_ge(stored[n % 2], 16 * PARTS * (n // 2))
                    b = bk if s else bq
                    if b is None:
                        nc.scalar.activation(parts[n % 2][:, 0, :], qk_bank[n % 2][:], ACT.Copy).then_inc(first_done, 1)
                    else:
                        nc.scalar.activation(parts[n % 2][:, 0, :], qk_bank[n % 2][:], ACT.Identity,
                                             bias=b).then_inc(first_done, 1)
                    act.wait_ge(rest_done, n + 1)
                    nc.scalar.activation(parts[n % 2][:, 1, :], rest[n % 2][:], ACT.Copy).then_inc(second_done, 1)

        @block.vector
        def _(dve):
            for c in range(N):
                for s in range(2):
                    n = 2 * c + s
                    b = bk if s else bq
                    dve.wait_ge(first_done, n + 1)
                    if n >= 2:
                        dve.wait_ge(third_done, n - 1)
                    nc.vector.scalar_tensor_tensor(out=rest[n % 2][:], in0=qk_bank[n % 2][:],
                                                   scalar=0.0 if b is None else b, in1=parts[n % 2][:, 0, :],
                                                   op0=ALU.add, op1=ALU.subtract).then_inc(rest_done, 1)
                dve.wait_ge(v_ready, c + 1)
                seq, half = divmod(c, S // CH)
                groups = v_sb[:, seq * (H // HG):(seq + 1) * (H // HG), 4 * half:4 * half + 4, :]
                dst = groups.rearrange("p g k w -> p k g w")
                src = v_bank[c % 2][:].rearrange("p (k g w) -> p k g w", k=4, w=HG * HD)
                if bv is None:
                    nc.vector.tensor_copy(dst, src).then_inc(v_copied, 1)
                else:
                    nc.vector.tensor_tensor(dst, src, bv[:].rearrange("p (g w) -> p g w", w=HG * HD).unsqueeze(1).broadcast_to([P, 4, H // HG, HG * HD]),
                                            ALU.add).then_inc(v_copied, 1)

        @block.gpsimd
        def _(pool):
            for n in range(2 * N):
                pool.wait_ge(second_done, n + 1)
                nc.gpsimd.tensor_tensor(parts[n % 2][:, 2, :], rest[n % 2][:], parts[n % 2][:, 1, :],
                                        ALU.subtract).then_inc(third_done, 1)

        @block.sync
        def _(sp):
            for n in range(2 * N):
                c, s = divmod(n, 2)
                sp.wait_ge(third_done, n + 1)
                dram = k_dram if s else q_dram
                for a in range(PARTS):
                    seq, half = divmod(c, S // CH)
                    dst = bass.AP(dram.tensor, (seq * H * PARTS + a) * HD * S + half * CH,
                                  [[PARTS * HD * S, H], [S, HD], [1, CH]])
                    sp.dma_start(dst, parts[n % 2][:, a, :]).then_inc(stored[n % 2], 16)
            for i in range(2):
                sp.wait_ge(stored[i], 16 * PARTS * N)


def attention(nc, tag, v_sb, ctx_sb, q_dram, k_dram, k):
    SCALE = float(HD) ** -0.5
    with ExitStack() as ctx:
        sb = lambda n, s, d: ctx.enter_context(nc.sbuf_tensor(f"{tag}_{n}", s, d))
        sem = lambda n: ctx.enter_context(nc.semaphore(f"{tag}_{n}"))
        ps = lambda n, s: ctx.enter_context(nc.psum_tensor(f"{tag}_{n}", s, F32))
        qT = [sb(f"qT{i}", [P, HG, S], BF16) for i in range(2)]
        kT = [sb(f"kT{i}", [P, HG, S], BF16) for i in range(2)]
        v = [sb(f"v{i}", [P, QB, HG, VW], F32) for i in range(2)]
        prob = [sb(f"prob{i}", [P, HG, CH], F32) for i in range(PBUF)]
        mx = sb("mx", [P, HG, QB], F32)
        mx2 = sb("mx2", [P, HG, QB // 2], F32)
        mneg = sb("mneg", [HG * QB, PARTS, P], BF16)
        mrest = sb("mrest", [HG * QB, P], F32)
        oT = sb("oT", [P, CH], F32)
        rec = sb("rec", [P, 4, HG], F32)
        st = [ps(f"st{i}", [P, 2, CH], F32) if False else ctx.enter_context(nc.psum_tensor(f"{tag}_st{i}", [P, 2, CH], F32)) for i in range(2)]
        sm = [ctx.enter_context(nc.psum_tensor(f"{tag}_sm{i}", [P, CH], F32)) for i in range(2)]
        pv = ctx.enter_context(nc.psum_tensor(f"{tag}_pv", [P, CH], F32))
        misc = ctx.enter_context(nc.psum_tensor(f"{tag}_misc", [P, CH], F32))

        padded = sem("padded")
        zeroed = sem("zeroed")
        lo_loaded = [sem(f"lo_loaded{i}") for i in range(2)]
        hi_loaded = [sem(f"hi_loaded{i}") for i in range(2)]
        v_set = sem("v_set")
        sm_ready, max_done = sem("sm_ready"), sem("max_done")
        mx_ready = sem("mx_ready")
        m_turned = sem("m_turned")
        m_chain = sem("m_chain")
        m_loaded = sem("m_loaded")
        st_ready, exp_done, sel_done, pv_done = sem("st_ready"), sem("exp_done"), sem("sel_done"), sem("pv_done")
        o_copied, o_turned, rec_done, o_done = sem("o_copied"), sem("o_turned"), sem("rec_done"), sem("o_done")
        mx2_done = sem("mx2_done")
        block = ctx.enter_context(nc.Block())

        NL = PARTS * (1 + PARTS) * 16

        def groups(eng, body):
            body(0, 0, 0, True, False)
            with eng.Fori(0, GROUPS // 2 - 1) as i:
                body(2 * i + 1, i, 1, False, False)
                body(2 * i + 2, i + 1, 0, False, False)
            body(GROUPS - 1, GROUPS // 2 - 1, 1, False, True)

        @block.sync
        def _(sp):
            def load(g, par, half):
                at = g * (HG * PARTS * HD * S) + half * CH
                done = (hi_loaded if half else lo_loaded)[par]
                cols = slice(half * CH, (half + 1) * CH)
                head = [PARTS * HD * S, HG]
                for c in range(PARTS):
                    r = c * PARTS * HD
                    sp.dma_start(qT[par][r:r + PARTS * HD, :, cols],
                                 bass.AP(q_dram.tensor, at, [[S, PARTS * HD], head, [1, CH]])).then_inc(done, 16)
                    for a in range(PARTS):
                        sp.dma_start(kT[par][r + a * HD:r + (a + 1) * HD, :, cols],
                                     bass.AP(k_dram.tensor, at + c * (HD * S), [[S, HD], head, [1, CH]])
                                     ).then_inc(done, 16)

            def rows(g, par):
                sp.wait_ge(m_chain, 4 * g + 4)
                for a in range(PARTS):
                    sp.dma_start(qT[par][MROW + a:MROW + a + 1, :, :].rearrange("o h (i q) -> o (h i) q", q=P),
                                 mneg[:, a, :]).then_inc(m_loaded, 16)

            sp.wait_ge(padded, 6)
            load(0, 0, 0)
            load(0, 0, 1)
            load(1, 1, 0)
            load(1, 1, 1)
            rows(0, 0)

            def step(g, par):
                sp.wait_ge(st_ready, 2 * NU * g + 2 * (UNITS.index((1, 3)) + 1))
                load(g + 2, par, 0)
                rows(g + 1, 1 - par)
                sp.wait_ge(st_ready, 2 * NU * (g + 1))
                load(g + 2, par, 1)

            with sp.Fori(0, GROUPS // 2 - 1) as i:
                step(2 * i, 0)
                step(2 * i + 1, 1)
            rows(GROUPS - 1, 1)
            sp.wait_ge(m_loaded, GROUPS * PARTS * 16)

        @block.gpsimd
        def _(pool):
            for i in range(2):
                nc.gpsimd.memset(v[i][:], 0.0).then_inc(v_set, 1)
            pool.wait_ge(v_set, 2)
            nc.gpsimd.memset(v[0][:, :, :, HD:HD + 1], 1.0).then_inc(zeroed, 1)
            nc.gpsimd.memset(v[1][:, :, :, HD:HD + 1], 1.0).then_inc(zeroed, 1)

            def values(g, par):
                nc.gpsimd.tensor_copy(v[par][:, :, :, 0:HD],
                                      v_sb[:, g, :, :].rearrange("p t (h d) -> p t h d", d=HD)).then_inc(v_set, 1)

            values(0, 0)
            fill = pool.alloc_register(f"{tag}_fill")
            pool.reg_mov(fill, 0)

            def body(g, nth, par, first, last):
                n = 0
                for u, (c, j) in enumerate(UNITS):
                    if u == 6 and not last:
                        if not first:
                            pool.wait_ge(pv_done, NU * g)
                        values(g + 1, 1 - par)
                    if j >= 4 * c:
                        pool.wait_ge(exp_done, 2 * NU * g + 2 * u + 2)
                        pool.reg_mul(fill, fill, 2)
                        diag = prob[u % PBUF][:, :, 0:P]
                        nc.gpsimd.affine_select(out=diag, in_=diag, compare_op=ALU.is_ge, fill=fill, base=0,
                                                pattern=[[0, HG], [1, P]], channel_multiplier=-1
                                                ).then_inc(sel_done, 1)

            groups(pool, body)

        @block.scalar
        def _(act):
            def body(g, nth, par, first, last):
                for u in range(NU):
                    _, n = unit_cols(u)
                    if not (first and u < PBUF):
                        act.wait_ge(pv_done, NU * g + u - PBUF + 1)
                    for pair in range(2):
                        act.wait_ge(st_ready, 2 * NU * g + 2 * u + pair + 1)
                        nc.scalar.activation(prob[u % PBUF][:, 2 * pair:2 * pair + 2, 0:n],
                                             st[pair][:, :, 0:n], ACT.Exp, scale=SCALE).then_inc(exp_done, 1)

            groups(act, body)

        def after(u):
            w = u - LAG
            return (0, w) if w >= 0 else (1, w + NU)

        @block.tensor
        def _(pe):
            def scores_max(g, par, s, first_group):
                i, h0, per, k0, n, _ = STEPS[s]
                if not (first_group and s < 2):
                    pe.wait_ge(max_done, NSTEP * g + s - 1)
                bank = sm[s % 2]
                for h in range(h0, h0 + per):
                    out = bank[:, (h - h0) * n:(h - h0 + 1) * n]
                    diag = k0 + n == P * (i + 1)
                    last = nc.tensor.matmul(out, qT[par][0:MROW, h, i * P:(i + 1) * P],
                                            kT[par][0:MROW, h, k0:k0 + n], start=True, stop=True)
                    if diag:
                        last = nc.tensor.matmul(out[:, n - P:n], k["ident_bf"][:], k["mask"][:],
                                                start=False, stop=True, skip_group_check=True)
                last.then_inc(sm_ready, 1)

            def turn_max(g):
                pe.wait_ge(mx_ready, g + 1)
                nc.tensor.transpose(misc[0:HG * QB, 0:P], mx[:].rearrange("p h i -> p (h i)"),
                                    k["ident"][:]).then_inc(m_turned, 1)

            def product(g, par, u):
                c, j = UNITS[u]
                q0, n = unit_cols(u)
                off = q0 - c * CH
                if j >= 4 * c:
                    d = sum(jj >= 4 * cc for cc, jj in UNITS[:u + 1])
                    pe.wait_ge(sel_done, NDIAG * g + d)
                else:
                    pe.wait_ge(exp_done, 2 * NU * g + 2 * u + 2)
                for h in range(HG):
                    last = nc.tensor.matmul(pv[VW * h:VW * (h + 1), off:off + n], v[par][:, j, h, :],
                                            prob[u % PBUF][:, h, 0:n], start=(j == 0), stop=True,
                                            skip_group_check=True)
                last.then_inc(pv_done, 1)

            def turn_out(g, c):
                pe.wait_ge(o_copied, 2 * g + c + 1)
                for i in range(4):
                    last = nc.tensor.transpose(misc[:, i * P:(i + 1) * P], oT[:, i * P:(i + 1) * P], k["ident"][:])
                last.then_inc(o_turned, 1)

            pe.wait_ge(padded, 6)
            pe.wait_ge(lo_loaded[0], NL)
            pe.wait_ge(hi_loaded[0], NL)
            for s in range(NSTEP):
                scores_max(0, 0, s, True)
            turn_max(0)

            def body(g, nth, par, first, last):
                pe.wait_ge(m_loaded, 16 * PARTS * (g + 1))
                for u, (c, j) in enumerate(UNITS):
                    q0, n = unit_cols(u)
                    for pair in range(2):
                        if not (first and u == 0):
                            pe.wait_ge(exp_done, 2 * NU * g + 2 * u + pair - 1)
                        for h in range(2):
                            hh = 2 * pair + h
                            mm = nc.tensor.matmul(st[pair][:, h, 0:n], kT[par][0:MROW + PARTS, hh, j * P:(j + 1) * P],
                                                  qT[par][0:MROW + PARTS, hh, q0:q0 + n], start=True, stop=True)
                        mm.then_inc(st_ready, 1)
                    if not last:
                        if u == 0:
                            pe.wait_ge(lo_loaded[1 - par], NL * (nth + par + 1))
                        for s in PLAN[u]:
                            if k_needs_hi(s) and (s == 0 or not k_needs_hi(s - 1)):
                                pe.wait_ge(hi_loaded[1 - par], NL * (nth + par + 1))
                            scores_max(g + 1, 1 - par, s, False)
                        if u == MT_UNIT:
                            turn_max(g + 1)
                    back, w = after(u)
                    if not (first and back):
                        if w == 0:
                            pe.wait_ge(v_set, 2 + (g - back) + 1)
                        if w == 0 or w == LAST[0] + 1:
                            if not (w == 0 and first):
                                pe.wait_ge(o_copied, 2 * (g - back) + (0 if w == 0 else 1))
                        product(g - back, (1 - par) if back else par, w)
                    x = (u - LAG - 1) % NU
                    xb = 1 if u - LAG - 1 < 0 else 0
                    for cc in (0, 1):
                        if x == LAST[cc] and not (first and xb):
                            turn_out(g - xb, cc)
                if last:
                    for w in range(NU - LAG, NU):
                        product(g, par, w)
                    turn_out(g, 1)

            groups(pe, body)

        @block.vector
        def _(dve):
            def row_max(g, s):
                i, h0, per, k0, n, piece = STEPS[s]
                dve.wait_ge(sm_ready, NSTEP * g + s + 1)
                dst = mx2[:, h0:h0 + per, i - 4] if piece else mx[:, h0:h0 + per, i]
                nc.vector.tensor_reduce(dst, sm[s % 2][:, 0:per * n].rearrange("p (h k) -> p h k", k=n),
                                        AX.X, ALU.max).then_inc(max_done, 1)

            def join_max(g):
                dve.wait_ge(max_done, NSTEP * (g + 1))
                nc.vector.tensor_tensor(mx[:, :, 4:QB], mx[:, :, 4:QB], mx2[:], ALU.max).then_inc(mx_ready, 1)

            def cut_max(g):
                dve.wait_ge(m_turned, g + 1)
                if not (isinstance(g, int) and g == 0):
                    dve.wait_ge(m_loaded, 16 * PARTS * g)
                src = misc[0:HG * QB, 0:P]
                nc.vector.tensor_scalar(mneg[:, 0, :], src, -1.0, None, ALU.mult).then_inc(m_chain, 1)
                dve.wait_ge(m_chain, 4 * g + 1)
                nc.vector.scalar_tensor_tensor(out=mrest[:], in0=src, scalar=-1.0, in1=mneg[:, 0, :],
                                               op0=ALU.mult, op1=ALU.subtract).then_inc(m_chain, 1)
                dve.wait_ge(m_chain, 4 * g + 2)
                nc.vector.tensor_copy(mneg[:, 1, :], mrest[:]).then_inc(m_chain, 1)
                dve.wait_ge(m_chain, 4 * g + 3)
                nc.vector.tensor_tensor(mneg[:, 2, :], mrest[:], mneg[:, 1, :], ALU.subtract).then_inc(m_chain, 1)

            def copy_out(g, c):
                dve.wait_ge(pv_done, NU * g + LAST[c] + 1)
                if not (isinstance(g, int) and g == 0 and c == 0):
                    dve.wait_ge(o_turned, 2 * g + c)
                nc.vector.tensor_copy(oT[:], pv[:]).then_inc(o_copied, 1)

            def norm_out(g, c):
                dve.wait_ge(o_turned, 2 * g + c + 1)
                o = misc[:].rearrange("p (i h w) -> p i h w", i=4, w=VW)
                nc.vector.reciprocal(rec[:], o[:, :, :, HD]).then_inc(rec_done, 1)
                dve.wait_ge(rec_done, 2 * g + c + 1)
                dst = ctx_sb[:, g, 4 * c:4 * c + 4, :]
                nc.vector.tensor_tensor(dst.rearrange("p i (h d) -> p i h d", d=HD), o[:, :, :, 0:HD],
                                        rec[:].unsqueeze(3).broadcast_to([P, 4, HG, HD]),
                                        ALU.mult).then_inc(o_done, 1)

            for i in range(2):
                nc.vector.memset(qT[i][64:96, :, :], 0.0).then_inc(padded, 1)
                nc.vector.memset(kT[i][64:96, :, :], 0.0).then_inc(padded, 1)
                nc.vector.memset(kT[i][MROW:MROW + PARTS, :, :], 1.0).then_inc(padded, 1)
            for s in range(NSTEP):
                row_max(0, s)
            join_max(0)
            cut_max(0)

            def body(g, nth, par, first, last):
                for u in range(NU):
                    if not last:
                        for s in PLAN[u]:
                            row_max(g + 1, s)
                        if PLAN[u] and PLAN[u][-1] == NSTEP - 1:
                            join_max(g + 1)
                        if u == MT_UNIT:
                            cut_max(g + 1)
                    back, w = after(u)
                    for cc in (0, 1):
                        if w == LAST[cc] and not (first and back):
                            copy_out(g - back, cc)
                    x = (u - LAG - 1) % NU
                    xb = 1 if u - LAG - 1 < 0 else 0
                    for cc in (0, 1):
                        if x == LAST[cc] and not (first and xb):
                            norm_out(g - xb, cc)
                if last:
                    copy_out(g, 1)
                    norm_out(g, 1)

            groups(dve, body)


def k_needs_hi(s):
    return STEPS[s][0] >= 4


def output_projection(nc, tag, ctx_sb, x, wo, bo, ident):
    N = TILES // 4
    with ExitStack() as ctx:
        sem = lambda n: ctx.enter_context(nc.semaphore(f"{tag}_{n}"))
        ps = lambda n: [ctx.enter_context(nc.psum_tensor(f"{tag}_{n}{i}", [P, CH], F32)) for i in range(2)]
        t_bank, o_bank = ps("t"), ps("o")
        cT = [ctx.enter_context(nc.sbuf_tensor(f"{tag}_cT{i}", [P, CH], F32)) for i in range(2)]
        rows = [ctx.enter_context(nc.sbuf_tensor(f"{tag}_rows{i}", [P, 4, D], F32)) for i in range(2)]
        gathered = sem("gathered")
        turned, copied, made, added, biased = sem("turned"), sem("copied"), sem("made"), sem("added"), sem("biased")
        block = ctx.enter_context(nc.Block())

        @block.tensor
        def _(pe):
            for n in range(N + 1):
                if n < N:
                    pe.wait_ge(gathered, n + 1)
                    if n >= 2:
                        pe.wait_ge(copied, n - 1)
                    for i in range(4):
                        last = nc.tensor.transpose(t_bank[n % 2][:, i * P:(i + 1) * P], rows[n % 2][:, i, :],
                                                   ident[:])
                    last.then_inc(turned, 1)
                if n >= 1:
                    m = n - 1
                    pe.wait_ge(copied, m + 1)
                    if m >= 2:
                        pe.wait_ge(added, m - 1)
                    for i in range(4):
                        last = nc.tensor.matmul(o_bank[m % 2][:, i * P:(i + 1) * P], cT[m % 2][:, i * P:(i + 1) * P],
                                                wo, start=True, stop=True)
                    last.then_inc(made, 1)

        @block.scalar
        def _(act):
            for n in range(N):
                act.wait_ge(turned, n + 1)
                if n >= 2:
                    act.wait_ge(made, n - 1)
                nc.scalar.activation(cT[n % 2][:], t_bank[n % 2][:], ACT.Copy).then_inc(copied, 1)

        @block.gpsimd
        def _(pool):
            for n in range(N):
                if n >= 2:
                    pool.wait_ge(turned, n - 1)
                seq, half = divmod(n, S // CH)
                groups = ctx_sb[:, seq * (H // HG):(seq + 1) * (H // HG), 4 * half:4 * half + 4, :]
                nc.gpsimd.tensor_copy(rows[n % 2][:].rearrange("p k (g w) -> p k g w", w=HG * HD),
                                      groups.rearrange("p g k w -> p k g w")).then_inc(gathered, 1)
                if bo is not None:
                    for t in range(4 * n, 4 * n + 4):
                        nc.gpsimd.tensor_tensor(x[:, t, :], x[:, t, :], bo[:], ALU.add).then_inc(biased, 1)

        @block.vector
        def _(dve):
            for n in range(N):
                dve.wait_ge(made, n + 1)
                if bo is not None:
                    dve.wait_ge(biased, 4 * n + 4)
                xs = x[:, 4 * n:4 * n + 4, :]
                nc.vector.tensor_tensor(xs, o_bank[n % 2][:].rearrange("p (i d) -> p i d", d=D), xs,
                                        ALU.add).then_inc(added, 1)


def route(nc, tag, xnT, router, comb, expert_no):
    with ExitStack() as ctx:
        sb = lambda n, s, d: ctx.enter_context(nc.sbuf_tensor(f"{tag}_{n}", s, d))
        sem = lambda n: ctx.enter_context(nc.semaphore(f"{tag}_{n}"))
        bank = ctx.enter_context(nc.psum_tensor(f"{tag}_bank", [P, TILES, E_N], F32))
        logits = sb("logits", [P, TILES, E_N], F32)
        top = sb("top", [P, TILES, 8], F32)
        at = sb("at", [P, TILES, 8], U32)
        atf = sb("atf", [P, TILES, 2], F32)
        gate = sb("gate", [P, TILES, 2], F32)
        den = sb("den", [P, TILES], F32)
        hot = sb("hot", [P, 2, TILES, E_N], F32)
        made, got, tops, exp_done, small = sem("made"), sem("got"), sem("tops"), sem("exp_done"), sem("small")
        block = ctx.enter_context(nc.Block())

        @block.tensor
        def _(pe):
            for t in range(TILES):
                last = nc.tensor.matmul(bank[:, t, :], xnT[:, t * P:(t + 1) * P], router, start=True, stop=True)
            last.then_inc(made, 1)

        @block.scalar
        def _(act):
            act.wait_ge(small, 1)
            nc.scalar.activation(gate[:, :, 1], den[:], ACT.Exp).then_inc(exp_done, 1)

        @block.vector
        def _(dve):
            dve.wait_ge(made, 1)
            nc.vector.tensor_copy(logits[:], bank[:]).then_inc(got, 1)
            dve.wait_ge(got, 1)
            for t in range(TILES):
                nc.vector.max(top[:, t, :], logits[:, t, :]).then_inc(tops, 1)
            dve.wait_ge(tops, TILES)
            for t in range(TILES):
                nc.vector.max_index(at[:, t, :], top[:, t, :], logits[:, t, :]).then_inc(tops, 1)
            nc.vector.tensor_tensor(den[:], top[:, :, 1], top[:, :, 0], ALU.subtract).then_inc(small, 1)
            dve.wait_ge(tops, 2 * TILES)
            nc.vector.tensor_copy(atf[:], at[:, :, 0:2]).then_inc(small, 1)
            dve.wait_ge(exp_done, 1)
            nc.vector.tensor_scalar(den[:], gate[:, :, 1], 1.0, None, ALU.add).then_inc(small, 1)
            dve.wait_ge(small, 3)
            nc.vector.reciprocal(gate[:, :, 0], den[:]).then_inc(small, 1)
            dve.wait_ge(small, 4)
            nc.vector.tensor_tensor(gate[:, :, 1], gate[:, :, 1], gate[:, :, 0], ALU.mult).then_inc(small, 1)
            for n in range(2):
                nc.vector.tensor_tensor(hot[:, n, :, :], expert_no[:].unsqueeze(1).broadcast_to([P, TILES, E_N]),
                                        atf[:, :, n:n + 1].broadcast_to([P, TILES, E_N]), ALU.is_equal).then_inc(small, 1)
            dve.wait_ge(small, 7)
            for n in range(2):
                nc.vector.tensor_tensor(hot[:, n, :, :], hot[:, n, :, :],
                                        gate[:, :, n:n + 1].broadcast_to([P, TILES, E_N]), ALU.mult).then_inc(small, 1)
            dve.wait_ge(small, 9)
            nc.vector.tensor_tensor(comb[:], hot[:, 0, :, :], hot[:, 1, :, :], ALU.add).then_inc(small, 1)


def experts(nc, tag, x, xnT, comb, w1, w2):
    N = NT // CH
    with ExitStack() as ctx:
        sem = lambda n: ctx.enter_context(nc.semaphore(f"{tag}_{n}"))
        h_bank = [ctx.enter_context(nc.psum_tensor(f"{tag}_h{i}", [P, 2, CH], F32)) for i in range(2)]
        y_bank = [ctx.enter_context(nc.psum_tensor(f"{tag}_y{i}", [P, CH], F32)) for i in range(2)]
        hs = [ctx.enter_context(nc.sbuf_tensor(f"{tag}_hs{i}", [P, FC, CH], F32)) for i in range(2)]
        xc = ctx.enter_context(nc.sbuf_tensor(f"{tag}_xc", [P, 4, D], F32))
        cc = ctx.enter_context(nc.sbuf_tensor(f"{tag}_cc", [P, 4, E_N], F32))
        h_ready, h_done, y_ready, y_done, got, put = (sem(n) for n in ("h_ready", "h_done", "y_ready", "y_done", "got", "put"))
        block = ctx.enter_context(nc.Block())

        @block.tensor
        def _(pe):
            def up(c, e, first):
                for half in range(2):
                    if not (first and e == 0):
                        pe.wait_ge(h_done, 2 * E_N * c + 2 * e + half - 1)
                    for f in range(2):
                        ff = 2 * half + f
                        last = nc.tensor.matmul(h_bank[half][:, f, :], w1[:, e, ff * P:(ff + 1) * P],
                                                xnT[:, bass.ds(c * CH, CH)], start=True, stop=True)
                    last.then_inc(h_ready, 1)

            def down(c, e, first):
                pe.wait_ge(h_done, 2 * E_N * c + 2 * e + 2)
                if not (first and e < 2):
                    pe.wait_ge(y_done, 4 * (E_N * c + e - 1))
                for t in range(4):
                    for ff in range(FC):
                        last = nc.tensor.matmul(y_bank[e % 2][:, t * D:(t + 1) * D], hs[e % 2][:, ff, t * P:(t + 1) * P],
                                                w2[:, e, ff, :], start=(ff == 0), stop=(ff == FC - 1))
                last.then_inc(y_ready, 1)

            def body(c, first):
                for e in range(E_N):
                    up(c, e, first)
                    if e:
                        down(c, e - 1, first)
                down(c, E_N - 1, first)

            body(0, True)
            with pe.Fori(1, N) as c:
                body(c, False)

        @block.scalar
        def _(act):
            def body(c, first):
                for e in range(E_N):
                    if not (first and e < 2):
                        act.wait_ge(y_ready, E_N * c + e - 1)
                    for half in range(2):
                        act.wait_ge(h_ready, 2 * E_N * c + 2 * e + half + 1)
                        nc.scalar.activation(hs[e % 2][:, 2 * half:2 * half + 2, :], h_bank[half][:],
                                             ACT.Gelu).then_inc(h_done, 1)

            body(0, True)
            with act.Fori(1, N) as c:
                body(c, False)

        @block.vector
        def _(dve):
            def body(c):
                nc.vector.tensor_copy(xc[:], x[:, bass.ds(4 * c, 4), :]).then_inc(got, 1)
                nc.vector.tensor_copy(cc[:], comb[:, bass.ds(4 * c, 4), :]).then_inc(got, 1)
                dve.wait_ge(got, 2 * c + 2)
                for e in range(E_N):
                    dve.wait_ge(y_ready, E_N * c + e + 1)
                    if e:
                        dve.wait_ge(y_done, 4 * (E_N * c + e))
                    for t in range(4):
                        nc.vector.scalar_tensor_tensor(out=xc[:, t, :], in0=y_bank[e % 2][:, t * D:(t + 1) * D],
                                                       scalar=cc[:, t, e:e + 1], in1=xc[:, t, :], op0=ALU.mult,
                                                       op1=ALU.add).then_inc(y_done, 1)
                dve.wait_ge(y_done, 4 * E_N * (c + 1))
                nc.vector.tensor_scalar(x[:, bass.ds(4 * c, 4), :], xc[:], 1.0, None, ALU.mult).then_inc(put, 1)
                dve.wait_ge(put, c + 1)

            with dve.Fori(0, N) as c:
                body(c)


def hybrid_block(nc, a, out):
    with ExitStack() as ctx:
        sb = lambda n, s, d=F32: ctx.enter_context(nc.sbuf_tensor(n, s, d))
        x = sb("x", [P, TILES, D])
        xn = sb("xn", [P, TILES, D])
        xnT = sb("xnT", [P, NT])
        ident = sb("ident", [P, P])
        ident_bf = sb("ident_bf", [P, P], BF16)
        mask = sb("mask", [P, P], BF16)
        expert_no = sb("expert_no", [P, E_N])
        comb = sb("comb", [P, TILES, E_N])
        w1 = sb("w1", [P, E_N, FF])
        w2 = sb("w2", [P, E_N, FC, D])
        router = sb("router", [P, E_N])
        wA = {n: sb(f"wA_{n}", [P, D]) for n in "qkvo"}
        lora_a = {n: sb(f"lora_a_{n}", [16, D]) for n in "qkvo"}
        lora_b = {n: sb(f"lora_b_{n}", [16, D]) for n in "qkvo"}
        b_wq, b_wo = sb("b_wq", [P, D]), sb("b_wo", [P, D])
        b_wkd, b_wku = sb("b_wkd", [P, 64]), sb("b_wku", [64, 2 * D])
        b_bq, b_bk, b_bkd = sb("b_bq", [P, 1]), sb("b_bk", [P, 1]), sb("b_bkd", [64, 1])
        b_bv, b_bo = sb("b_bv", [P, D]), sb("b_bo", [P, D])
        q_dram = nc.dram_tensor("q_parts", (B, H, PARTS, HD, S), BF16).ap()
        k_dram = nc.dram_tensor("k_parts", (B, H, PARTS, HD, S), BF16).ap()
        by_group = xn[:].rearrange("p t d -> p (t d)").rearrange("p (g t w) -> p g t w", g=GROUPS, t=QB)
        consts = {"ident": ident, "ident_bf": ident_bf, "mask": mask}

        with ExitStack() as c2:
            sem = lambda n: c2.enter_context(nc.semaphore(n))
            x_in, w_in, c0, folded, lora_done = sem("x_in"), sem("w_in"), sem("c0"), sem("folded"), sem("lora_done")
            bank = c2.enter_context(nc.psum_tensor("fold", [P, 4, D], F32))
            block = c2.enter_context(nc.Block())

            @block.sync
            def _(sp):
                n = 0
                for c in range(B):
                    sp.dma_start(x[:, c * QB:(c + 1) * QB, :],
                                 a["x"][c].rearrange("(t p) d -> p t d", p=P)).then_inc(x_in, 16)
                sp.wait_ge(x_in, 16 * (B + 13))

            @block.scalar
            def _(act):
                n = 0
                for m in "qkvo":
                    for dst, src in ((wA[m], a["wT_" + m]), (lora_a[m], a["la_" + m]), (lora_b[m], a["lb_" + m])):
                        act.dma_start(dst[:], src).then_inc(w_in, 16)
                        n += 1
                act.dma_start(w1[:], a["w1"]).then_inc(x_in, 16)
                act.dma_start(w2[:], a["w2"]).then_inc(x_in, 16)
                bias = a["bku"]
                for dst, src in ((router[:], a["router"]), (b_wq[:], a["b_wq"]), (b_wo[:], a["b_wo"]),
                                 (b_wkd[:], a["b_wkd"]), (b_wku[0:32, :], a["b_wku"]), (b_wku[32:64, :], a["b_wku"]),
                                 (b_bq[:], a["bq"].unsqueeze(1)), (b_bk[:], bias[0:D].unsqueeze(1)),
                                 (b_bkd[:], a["bkd"].unsqueeze(1)), (b_bv[:], bias[D:2 * D].partition_broadcast(P)),
                                 (b_bo[:], a["bo"].partition_broadcast(P))):
                    act.dma_start(dst, src).then_inc(x_in, 16)
                act.wait_ge(x_in, 16 * (B + 13))

            @block.gpsimd
            def _(pool):
                nc.gpsimd.memset(ident[:], 0.0)
                nc.gpsimd.memset(mask[:], 0.0).then_inc(c0, 1)
                nc.gpsimd.iota(expert_no[:], pattern=[[1, E_N]], base=0, channel_multiplier=0,
                               allow_small_or_imprecise_dtypes=True).then_inc(c0, 1)
                pool.wait_ge(c0, 1)
                nc.gpsimd.affine_select(out=ident[:], in_=ident[:], compare_op=ALU.not_equal, fill=1.0, base=0,
                                        pattern=[[-1, P]], channel_multiplier=1).then_inc(c0, 1)
                nc.gpsimd.affine_select(out=mask[:], in_=mask[:], compare_op=ALU.is_ge, fill=NEG, base=0,
                                        pattern=[[-1, P]], channel_multiplier=1).then_inc(c0, 1)
                pool.wait_ge(c0, 4)
                nc.gpsimd.tensor_copy(ident_bf[:], ident[:]).then_inc(c0, 1)

            @block.tensor
            def _(pe):
                pe.wait_ge(w_in, 16 * 12)
                for n, m in enumerate("qkvo"):
                    last = nc.tensor.matmul(bank[:, n, :], lora_a[m][:], lora_b[m][:], start=True, stop=True)
                last.then_inc(lora_done, 1)

            @block.vector
            def _(dve):
                dve.wait_ge(lora_done, 1)
                for n, m in enumerate("qkvo"):
                    nc.vector.scalar_tensor_tensor(out=wA[m][:], in0=bank[:, n, :], scalar=1.0 / 16, in1=wA[m][:],
                                                   op0=ALU.mult, op1=ALU.add).then_inc(folded, 1)

        with nc.sbuf_tensor("v_sb", [P, GROUPS, QB, HG * HD], F32) as v_sb:
            layer_norm(nc, "ln1", x, xn, xnT, ident)
            project(nc, "pa", xnT, v_sb, q_dram, k_dram, wA["q"][:], wA["k"][:], wA["v"][:], None, None, None, None)
            attention(nc, "aa", v_sb, by_group, q_dram, k_dram, consts)
            output_projection(nc, "oa", by_group, x, wA["o"][:], None, ident)
        layer_norm(nc, "ln2", x, xn, xnT, ident)
        route(nc, "ra", xnT, router[:], comb, expert_no)
        experts(nc, "ea", x, xnT, comb, w1, w2)
        with nc.sbuf_tensor("v_sb2", [P, GROUPS, QB, HG * HD], F32) as v_sb:
            layer_norm(nc, "ln3", x, xn, xnT, ident)
            project(nc, "pb", xnT, v_sb, q_dram, k_dram, b_wq[:], b_wku[:, 0:D], b_wku[:, D:2 * D],
                    b_bq[:, 0:1], b_bk[:, 0:1], b_bv, {"wkd": b_wkd, "bkd": b_bkd})
            attention(nc, "ab", v_sb, by_group, q_dram, k_dram, consts)
            output_projection(nc, "ob", by_group, x, b_wo[:], b_bo, ident)
        layer_norm(nc, "ln4", x, xn, xnT, ident)
        route(nc, "rb", xnT, router[:], comb, expert_no)
        experts(nc, "eb", x, xnT, comb, w1, w2)

        with nc.semaphore("out_done") as out_done, nc.Block() as block:
            @block.sync
            def _(sp):
                for c in range(B):
                    sp.dma_start(out[c].rearrange("(t p) d -> p t d", p=P),
                                 x[:, c * QB:(c + 1) * QB, :]).then_inc(out_done, 16)
                sp.wait_ge(out_done, 16 * B)


def kernel(**inputs):
    import numpy as np
    import concourse.bacc as bacc
    from concourse.bass_utils import run_bass_kernel_spmd

    def get(n):
        return np.asarray(inputs[n])

    w1 = get("L0_ffn_w1")
    w2 = get("L0_ffn_w2")
    arrays = {"x": get("L0_attn_a_x")}
    for m in "qkvo":
        arrays["wT_" + m] = get(f"L0_attn_a_w{m}").T
        arrays["la_" + m] = get(f"L0_attn_a_a{m}")
        arrays["lb_" + m] = get(f"L0_attn_a_b{m}").T
    arrays.update(
        w1=w1.transpose(2, 0, 1),
        w2=w2.reshape(w2.shape[0], w2.shape[1], 4, 128).transpose(3, 0, 2, 1),
        router=get("L0_ffn_router_w").T,
        b_wq=get("L0_attn_b_Wq"), b_wo=get("L0_attn_b_Wo"), b_wkd=get("L0_attn_b_Wkd"), b_wku=get("L0_attn_b_Wku"),
        bq=get("L0_attn_b_bq"), bkd=get("L0_attn_b_bkd"), bku=get("L0_attn_b_bku"), bo=get("L0_attn_b_bo"),
    )
    nc = bacc.Bacc("TRN2", target_bir_lowering=False, num_devices=1)
    fed, a = {}, {}
    for name, value in arrays.items():
        value = np.ascontiguousarray(value)
        fed[f"in_{name}"] = value
        a[name] = nc.dram_tensor(f"in_{name}", value.shape, mybir.dt.from_np(value.dtype), kind="ExternalInput").ap()
    out = nc.dram_tensor("out", (B, S, D), F32, kind="ExternalOutput").ap()
    hybrid_block(nc, a, out)
    r = run_bass_kernel_spmd(nc, [fed], core_ids=[0])
    return r.results[0]["out"]
```

```python
from contextlib import ExitStack

import concourse.bass as bass
from concourse import mybir

ALU = mybir.AluOpType
ACT = mybir.ActivationFunctionType
AX = mybir.AxisListType
F32 = mybir.dt.float32
BF16 = mybir.dt.bfloat16
U32 = mybir.dt.uint32

P = 128
D = 128
B = 4
S = 1024
NT = B * S
TILES = NT // P
H = 16
HD = D // H
EPS = 1e-5
NEG = -1e30

HG = 4
GROUPS = B * (H // HG)
QB = S // P
CH = 512
PARTS = 3
ROWS = PARTS * PARTS * HD
MROW = 96
VW = 32

E_N = 8
FF = 512
FC = FF // P
PAIRS = 2 * TILES
UNROLL = 8
XTILES = -(-((PAIRS * P + E_N * (P - 1)) // P) // UNROLL) * UNROLL


UNITS = [(0, 0), (0, 3), (0, 2), (0, 1),
         (1, 0), (1, 1), (1, 2), (1, 3), (1, 7), (1, 6), (1, 5), (1, 4)]
NU = len(UNITS)
NDIAG = sum(j >= 4 * c for c, j in UNITS)
LAST = {c: max(u for u, (cc, _) in enumerate(UNITS) if cc == c) for c in (0, 1)}
PBUF = 4
LAG = 2


def unit_cols(u):
    c, j = UNITS[u]
    q0 = max(P * j, CH * c)
    return q0, CH * (c + 1) - q0


def max_steps():
    steps = []
    for i in range(QB):
        keys = P * (i + 1)
        first = min(keys, CH)
        per = CH // first if CH % first == 0 else 1
        for h in range(0, HG, per):
            steps.append((i, h, per, 0, first, 0))
        if keys > CH:
            rest = keys - CH
            per = {P: 4, 2 * P: 2}.get(rest, 1)
            for h in range(0, HG, per):
                steps.append((i, h, per, CH, rest, 1))
    return steps


STEPS = max_steps()
NSTEP = len(STEPS)


RING = 3
HALF_STEPS = sum(i < QB // 2 for i, *_ in STEPS)
FIRST_HI = HALF_STEPS


def plan():
    cols = [unit_cols(u)[1] for u in range(NU)]
    cost = [per * keys for _, _, per, _, keys, _ in STEPS]
    order, s, done = [], 0, 0
    for u in range(NU):
        goal = sum(cost) * sum(cols[:u + 1]) / sum(cols)
        steps = []
        while s < NSTEP and done + cost[s] / 2 <= goal + 1e-6 or (u == NU - 1 and s < NSTEP):
            done += cost[s]
            steps.append(("step", s, 0))
            s += 1
        atoms = [("scores", 0, 0), ("scores", 1, 0), ("product", 0, 0)]
        starts = [0.0, 0.25, 0.5]
        mixed = sorted([(f, 0, n, a) for n, (f, a) in enumerate(zip(starts, atoms))]
                       + [((n + 0.5) / len(steps), 1, n, a) for n, a in enumerate(steps)])
        mixed = [a for *_, a in mixed]
        if u == 1:
            mixed.insert(1, ("max", 1, 0))
        if u > 1 and any(("step", HALF_STEPS - 1, 0) in x for x in order) and \
                not any(("max", 0, 1) in x for x in order):
            mixed.insert(len(mixed) - 1, ("max", 0, 1))
        if u == LAST[1] + LAG - NU + 1:
            mixed.append(("out", 1, 1))
        if u == LAST[0] + LAG + 1:
            mixed.append(("out", 0, 0))
        order.append(mixed)
    return order


ORDER = plan()
START = [("step", s, 0) for s in range(HALF_STEPS + 3)] + [("max", 0, 1)] \
    + [("step", s, 0) for s in range(HALF_STEPS + 3, NSTEP)]
PER_GROUP = sum(w in ("step", "max", "out") for u in ORDER for w, _, _ in u)
assert NU % PBUF == 0 and PER_GROUP % RING == 0 and PER_GROUP == NSTEP + 4


def skipped(what, y, first, last):
    return (first and what == "out" and y == 1) or (last and what == "step") or (last and what == "max" and y == 1)


def ring_start(first):
    return len(START) % RING if first else (len(START) + PER_GROUP - 1) % RING


def ring_base(g, first):
    return (len(START) if first else len(START) + PER_GROUP * g - 1), 0


def index_in_group(item, first, last=False):
    flat = [i for u in ORDER for i in u if i[0] in ("step", "max", "out") and not skipped(i[0], i[2], first, last)]
    return flat.index(item)


HALF_STEPS_AT = {f: index_in_group(("step", HALF_STEPS - 1, 0), f) for f in (True, False)}


def out_index(g, c, first, last):
    if c == 1:
        return ring_base(g + 1, False)[0] + index_in_group(("out", 1, 1), False, last)
    return ring_base(g, first)[0] + index_in_group(("out", 0, 0), first, last)


def layer_norm(nc, tag, x, xn, xnT, ident, spent):
    with ExitStack() as ctx:
        sb = lambda n, s, d: ctx.enter_context(nc.sbuf_tensor(f"{tag}_{n}", s, d))
        sem = lambda n: ctx.enter_context(nc.semaphore(f"{tag}_{n}"))
        stats = sb("stats", [P, TILES, 6], F32)
        mean = sb("mean", [P, TILES], F32)
        half = sb("half", [P, TILES], F32)
        sq = sb("sq", [P, TILES], F32)
        var = sb("var", [P, TILES], F32)
        std = sb("std", [P, TILES], F32)
        rstd = sb("rstd", [P, TILES], F32)
        bank = [ctx.enter_context(nc.psum_tensor(f"{tag}_bank{i}", [P, CH], F32)) for i in range(2)]
        stats_done, small, std_done = sem("stats_done"), sem("small"), sem("std_done")
        xn_ready, turned, copied = sem("xn_ready"), sem("turned"), sem("copied")
        spent += [stats_done, small, std_done, xn_ready, turned, copied]
        block = ctx.enter_context(nc.Block())

        @block.vector
        def _(dve):
            with dve.Fori(0, TILES // 4) as i:
                for t, k in ((4 * i, k) for k in range(4)):
                    nc.vector.bn_stats(stats[:, t + k, :], x[:, t + k, :]).then_inc(stats_done, 1)
            dve.wait_ge(stats_done, TILES)
            me, mo, ve, vo = (stats[:, :, k] for k in (1, 4, 2, 5))
            nc.vector.tensor_tensor(mean[:], me, mo, ALU.add).then_inc(small, 1)
            nc.vector.tensor_tensor(half[:], me, mo, ALU.subtract).then_inc(small, 1)
            nc.vector.tensor_tensor(var[:], ve, vo, ALU.add).then_inc(small, 1)
            dve.wait_ge(small, 3)
            nc.vector.tensor_scalar(mean[:], mean[:], 0.5, None, ALU.mult).then_inc(small, 1)
            nc.vector.scalar_tensor_tensor(out=sq[:], in0=half[:], scalar=0.25, in1=half[:],
                                           op0=ALU.mult, op1=ALU.mult).then_inc(small, 1)
            nc.vector.tensor_scalar(var[:], var[:], 1.0 / D, EPS, ALU.mult, ALU.add).then_inc(small, 1)
            dve.wait_ge(small, 6)
            nc.vector.tensor_tensor(var[:], var[:], sq[:], ALU.add).then_inc(small, 1)
            dve.wait_ge(std_done, 1)
            nc.vector.reciprocal(rstd[:], std[:]).then_inc(small, 1)
            dve.wait_ge(small, 8)
            with dve.Fori(0, TILES // 4) as i:
                for t, k in ((4 * i, k) for k in range(4)):
                    nc.vector.tensor_scalar(xn[:, t + k, :], x[:, t + k, :], mean[:, bass.ds(t + k, 1)],
                                            rstd[:, bass.ds(t + k, 1)], ALU.subtract,
                                            ALU.mult).then_inc(xn_ready, 1)

        @block.tensor
        def _(pe):
            for g in range(TILES // 4):
                pe.wait_ge(xn_ready, 4 * (g + 1))
                if g >= 2:
                    pe.wait_ge(copied, g - 1)
                for k in range(4):
                    last = nc.tensor.transpose(bank[g % 2][:, k * P:(k + 1) * P], xn[:, 4 * g + k, :],
                                               ident[:])
                last.then_inc(turned, 1)

        @block.scalar
        def _(act):
            act.wait_ge(small, 7)
            nc.scalar.activation(std[:], var[:], ACT.Sqrt).then_inc(std_done, 1)
            for g in range(TILES // 4):
                act.wait_ge(turned, g + 1)
                nc.scalar.activation(xnT[:, g * CH:(g + 1) * CH], bank[g % 2][:], ACT.Copy).then_inc(copied, 1)


K_STORES = [(0, 0, 3, 0), (1, 1, 2, 0), (1, 0, 1, 2), (2, 2, 1, 0), (2, 0, 2, 1)]
STORES = (1, len(K_STORES))


def project(nc, tag, xnT, v_sb, q_dram, k_dram, wq, wk, wv, bq, bk, bv, latent, spent):
    N = NT // CH
    with ExitStack() as ctx:
        sb = lambda n, s, d: ctx.enter_context(nc.sbuf_tensor(f"{tag}_{n}", s, d))
        sem = lambda n: ctx.enter_context(nc.semaphore(f"{tag}_{n}"))
        ps = lambda n: [ctx.enter_context(nc.psum_tensor(f"{tag}_{n}{i}", [P, CH], F32)) for i in range(2)]
        qk_bank, v_bank, l_bank = ps("qk"), ps("v"), ps("l")
        parts = [sb(f"parts{i}", [P, PARTS, CH], BF16) for i in range(4)]
        rest = [sb(f"rest{i}", [P, CH], F32) for i in range(2)]
        gl = [sb(f"gl{i}", [64, CH], F32) for i in range(2)] if latent else None
        qk_ready, first_done, rest_done, second_done = sem("qk_ready"), sem("first"), sem("rest"), sem("second")
        third_done, stored, v_ready, v_copied = sem("third"), [[sem(f"stored{s}_{i}") for i in range(2)] for s in range(2)], sem("v_ready"), sem("v_copied")
        l_ready, l_done = sem("l_ready"), sem("l_done")
        spent += [qk_ready, first_done, rest_done, second_done, third_done, *stored[0], *stored[1], v_ready, v_copied, l_ready, l_done]
        block = ctx.enter_context(nc.Block())

        @block.tensor
        def _(pe):
            for c in range(N):
                src = xnT[:, c * CH:(c + 1) * CH]
                if latent:
                    if c >= 2:
                        pe.wait_ge(l_done, c - 1)
                    nc.tensor.matmul(l_bank[c % 2][0:64, :], latent["wkd"][:], src, start=True,
                                     stop=True).then_inc(l_ready, 1)
                for s in range(2):
                    n = 2 * c + s
                    if n >= 2:
                        pe.wait_ge(first_done, n - 1)
                        pe.wait_ge(rest_done, n - 1)
                    if s and latent:
                        pe.wait_ge(l_done, c + 1)
                        nc.tensor.matmul(qk_bank[n % 2][:], wk, gl[c % 2][:], start=True,
                                         stop=True).then_inc(qk_ready, 1)
                    else:
                        nc.tensor.matmul(qk_bank[n % 2][:], wk if s else wq, src, start=True,
                                         stop=True).then_inc(qk_ready, 1)
                if c >= 2:
                    pe.wait_ge(v_copied, c - 1)
                for k in range(4):
                    left = gl[c % 2][:, k * P:(k + 1) * P] if latent else xnT[:, c * CH + k * P:c * CH + (k + 1) * P]
                    last = nc.tensor.matmul(v_bank[c % 2][:, k * P:(k + 1) * P], left, wv, start=True, stop=True)
                last.then_inc(v_ready, 1)

        @block.scalar
        def _(act):
            for c in range(N):
                if latent:
                    act.wait_ge(l_ready, c + 1)
                    if c >= 2:
                        act.wait_ge(v_ready, c - 1)
                    nc.scalar.activation(gl[c % 2][:], l_bank[c % 2][0:64, :], ACT.Gelu,
                                         bias=latent["bkd"][:, 0:1]).then_inc(l_done, 1)
                for s in range(2):
                    n = 2 * c + s
                    act.wait_ge(qk_ready, n + 1)
                    if c >= 2:
                        act.wait_ge(stored[s][c % 2], 16 * STORES[s] * (c // 2))
                    b = bk if s else bq
                    if b is None:
                        nc.scalar.activation(parts[n % 4][:, 0, :], qk_bank[n % 2][:], ACT.Copy).then_inc(first_done, 1)
                    else:
                        nc.scalar.activation(parts[n % 4][:, 0, :], qk_bank[n % 2][:], ACT.Identity,
                                             bias=b).then_inc(first_done, 1)
                    act.wait_ge(rest_done, n + 1)
                    nc.scalar.activation(parts[n % 4][:, 1, :], rest[n % 2][:], ACT.Copy).then_inc(second_done, 1)

        @block.vector
        def _(dve):
            for c in range(N):
                for s in range(2):
                    n = 2 * c + s
                    b = bk if s else bq
                    dve.wait_ge(first_done, n + 1)
                    if n >= 2:
                        dve.wait_ge(third_done, n - 1)
                    nc.vector.scalar_tensor_tensor(out=rest[n % 2][:], in0=qk_bank[n % 2][:],
                                                   scalar=0.0 if b is None else b, in1=parts[n % 4][:, 0, :],
                                                   op0=ALU.add, op1=ALU.subtract).then_inc(rest_done, 1)
                dve.wait_ge(v_ready, c + 1)
                seq, half = divmod(c, S // CH)
                groups = v_sb[:, seq * (H // HG):(seq + 1) * (H // HG), 4 * half:4 * half + 4, :]
                dst = groups.rearrange("p g k w -> p k g w")
                src = v_bank[c % 2][:].rearrange("p (k g w) -> p k g w", k=4, w=HG * HD)
                if bv is None:
                    nc.vector.tensor_copy(dst, src).then_inc(v_copied, 1)
                else:
                    nc.vector.tensor_tensor(dst, src, bv[:].rearrange("p (g w) -> p g w", w=HG * HD).unsqueeze(1).broadcast_to([P, 4, H // HG, HG * HD]),
                                            ALU.add).then_inc(v_copied, 1)

        @block.gpsimd
        def _(pool):
            for n in range(2 * N):
                pool.wait_ge(second_done, n + 1)
                nc.gpsimd.tensor_tensor(parts[n % 4][:, 2, :], rest[n % 2][:], parts[n % 4][:, 1, :],
                                        ALU.subtract).then_inc(third_done, 1)

        @block.sync
        def _(sp):
            for c in range(N):
                seq, half = divmod(c, S // CH)
                cols = slice(half * CH, (half + 1) * CH)
                sp.wait_ge(third_done, 2 * c + 1)
                sp.dma_start(q_dram[seq, :, :, cols], parts[2 * c % 4][:]).then_inc(stored[0][c % 2], 16)
                sp.wait_ge(third_done, 2 * c + 2)
                for x, part, n, place in K_STORES:
                    sp.dma_start(k_dram[x, seq, :, place:place + n, cols],
                                 parts[(2 * c + 1) % 4][:, part:part + n, :]).then_inc(stored[1][c % 2], 16)
            for s in range(2):
                for i in range(2):
                    sp.wait_ge(stored[s][i], 16 * STORES[s] * (N // 2))


def attention(nc, tag, v_sb, ctx_sb, q_dram, k_dram, k, spent):
    SCALE = float(HD) ** -0.5
    with ExitStack() as ctx:
        sb = lambda n, s, d: ctx.enter_context(nc.sbuf_tensor(f"{tag}_{n}", s, d))
        ps = lambda n, s: ctx.enter_context(nc.psum_tensor(f"{tag}_{n}", s, F32))
        sem = lambda n: ctx.enter_context(nc.semaphore(f"{tag}_{n}"))
        qT, kT, v = k["qT"], k["kT"], k["v"]
        prob = [sb(f"prob{i}", [P, HG, CH], F32) for i in range(PBUF)]
        mx = [sb(f"mx{i}", [P, HG, QB // 2], F32) for i in range(2)]
        mx2 = sb("mx2", [P, HG, QB // 2], F32)
        mneg = sb("mneg", [HG * QB // 2, PARTS, P], BF16)
        mrest = sb("mrest", [HG * QB // 2, P], F32)
        oT = sb("oT", [P, CH], F32)
        rec = sb("rec", [P, 4, HG], F32)
        st = [ps(f"st{i}", [P, 2, CH]) for i in range(2)]
        ring = [ps(f"ring{i}", [P, CH]) for i in range(RING)]
        pv = ps("pv", [P, CH])

        lo_loaded = [sem(f"lo_loaded{i}") for i in range(2)]
        hi_loaded = [sem(f"hi_loaded{i}") for i in range(2)]
        v_set = sem("v_set")
        ring_ready, ring_free = sem("ring_ready"), sem("ring_free")
        mx_joined = sem("mx_joined")
        m_chain = sem("m_chain")
        m_cut, m_loaded = sem("m_cut"), sem("m_loaded")
        st_ready, exp_done, sel_done, pv_done = sem("st_ready"), sem("exp_done"), sem("sel_done"), sem("pv_done")
        o_copied, rec_done = sem("o_copied"), sem("rec_done")
        block = ctx.enter_context(nc.Block())

        NL = 2 * PARTS * 16

        def groups(eng, body):
            body(0, 0, 0, True, False)
            with eng.Fori(0, GROUPS // 2 - 1) as i:
                body(2 * i + 1, i, 1, False, False)
                body(2 * i + 2, i + 1, 0, False, False)
            body(GROUPS - 1, GROUPS // 2 - 1, 1, False, True)

        @block.sync
        def _(sp):
            def load(g, par, half):
                done = (hi_loaded if half else lo_loaded)[par]
                n = PARTS * HD
                for x in range(PARTS):
                    for dst, dram, first in ((qT[par][x * n:(x + 1) * n, half, :, :], q_dram, 0),
                                             (kT[par][x * n:(x + 1) * n, :, half * CH:(half + 1) * CH], k_dram,
                                              x * NT * D * PARTS)):
                        sp.dma_start(dst, bass.AP(dram.tensor, first + g * (HG * n * S) + half * CH,
                                                  [[S, n], [n * S, HG], [1, CH]])).then_inc(done, 16)

            def send(par, half):
                for a in range(PARTS):
                    dst = qT[par][MROW + a:MROW + a + 1, half, :, :]
                    sp.dma_start(dst.rearrange("o h (i q) -> o (h i) q", q=P),
                                 mneg[:, a, :]).then_inc(m_loaded, 16)

            load(0, 0, 0)
            load(0, 0, 1)
            load(1, 1, 0)
            load(1, 1, 1)
            sp.wait_ge(m_cut, 1)
            send(0, 0)

            def step(g, par):
                sp.wait_ge(m_cut, 2 * g + 2)
                send(par, 1)
                sp.wait_ge(m_cut, 2 * g + 3)
                send(1 - par, 0)
                sp.wait_ge(st_ready, 2 * NU * g + 2 * (UNITS.index((1, 3)) + 1))
                load(g + 2, par, 0)
                sp.wait_ge(st_ready, 2 * NU * (g + 1))
                load(g + 2, par, 1)

            with sp.Fori(0, GROUPS // 2 - 1) as i:
                step(2 * i, 0)
                step(2 * i + 1, 1)
            for g in (GROUPS - 2, GROUPS - 1):
                sp.wait_ge(m_cut, 2 * g + 2)
                send(g % 2, 1)
                if g == GROUPS - 2:
                    sp.wait_ge(m_cut, 2 * g + 3)
                    send(1, 0)
            sp.wait_ge(m_loaded, 2 * GROUPS * PARTS * 16)

        @block.gpsimd
        def _(pool):
            for s in spent:
                nc.gpsimd.sem_clear(s)
            spent.clear()
            def values(g, par):
                nc.gpsimd.tensor_copy(v[par][:, :, :, 0:HD],
                                      v_sb[:, g, :, :].rearrange("p t (h d) -> p t h d", d=HD)).then_inc(v_set, 1)

            values(0, 0)
            fill = pool.alloc_register(f"{tag}_fill")
            pool.reg_mov(fill, 0)

            def body(g, nth, par, first, last):
                for u, (c, j) in enumerate(UNITS):
                    if u == 6 and not last:
                        if not first:
                            pool.wait_ge(pv_done, NU * g)
                        values(g + 1, 1 - par)
                    if j >= 4 * c:
                        pool.wait_ge(exp_done, 2 * NU * g + 2 * u + 2)
                        pool.reg_mul(fill, fill, 2)
                        diag = prob[u % PBUF][:, :, 0:P]
                        nc.gpsimd.affine_select(out=diag, in_=diag, compare_op=ALU.is_ge, fill=fill, base=0,
                                                pattern=[[0, HG], [1, P]], channel_multiplier=-1
                                                ).then_inc(sel_done, 1)

            groups(pool, body)

        @block.scalar
        def _(act):
            def copy_out(g, c, first, last):
                act.wait_ge(pv_done, NU * g + LAST[c] + 1)
                if c:
                    act.wait_ge(ring_free, out_index(g, 0, first, last) + 1)
                elif not first:
                    act.wait_ge(ring_free, out_index(g - 1, 1, False, last) + 1)
                nc.scalar.activation(oT[:], pv[:], ACT.Copy).then_inc(o_copied, 1)

            def body(g, nth, par, first, last):
                for u in range(NU):
                    _, n = unit_cols(u)
                    if not (first and u < PBUF):
                        act.wait_ge(pv_done, NU * g + u - PBUF + 1)
                    for pair in range(2):
                        act.wait_ge(st_ready, 2 * NU * g + 2 * u + pair + 1)
                        nc.scalar.activation(prob[u % PBUF][:, 2 * pair:2 * pair + 2, 0:n],
                                             st[pair][:, :, 0:n], ACT.Exp, scale=SCALE).then_inc(exp_done, 1)
                    if u == LAST[0] + LAG:
                        copy_out(g, 0, first, last)
                    if u == LAST[1] + LAG - NU and not first:
                        copy_out(g - 1, 1, False, False)
                if last:
                    copy_out(g, 1, first, last)

            groups(act, body)

        @block.tensor
        def _(pe):
            def ring_wait(n, at):
                if not (isinstance(n, int) and n < RING):
                    pe.wait_ge(ring_free, n - RING + 1)

            def scores_max(g, par, s, n, bank):
                i, h0, per, k0, keys, _ = STEPS[s]
                ring_wait(n, bank)
                for h in range(h0, h0 + per):
                    out = ring[bank][:, (h - h0) * keys:(h - h0 + 1) * keys]
                    last = nc.tensor.matmul(out, qT[par][0:MROW, i // 4, h, i % 4 * P:(i % 4 + 1) * P],
                                            kT[par][0:MROW, h, k0:k0 + keys], start=True, stop=True)
                    if k0 + keys == P * (i + 1):
                        last = nc.tensor.matmul(out[:, keys - P:keys], k["ident_bf"][:], k["mask"][:],
                                                start=False, stop=True, skip_group_check=True)
                last.then_inc(ring_ready, 1)

            def turn_max(g, half, n, bank, done):
                ring_wait(n, bank)
                if half:
                    pe.wait_ge(mx_joined, g + 1)
                else:
                    pe.wait_ge(ring_free, done)
                nc.tensor.transpose(ring[bank][0:HG * QB // 2, 0:P], mx[half][:].rearrange("p h i -> p (h i)"),
                                    k["ident"][:]).then_inc(ring_ready, 1)

            def turn_out(g, c, n, bank):
                ring_wait(n, bank)
                pe.wait_ge(o_copied, 2 * g + c + 1)
                for i in range(4):
                    last = nc.tensor.transpose(ring[bank][:, i * P:(i + 1) * P], oT[:, i * P:(i + 1) * P], k["ident"][:])
                last.then_inc(ring_ready, 1)

            def scores(g, par, u, pair, first):
                c, j = UNITS[u]
                q0, n = unit_cols(u)
                if not (first and u == 0):
                    pe.wait_ge(exp_done, 2 * NU * g + 2 * u + pair - 1)
                for h in range(2):
                    hh = 2 * pair + h
                    mm = nc.tensor.matmul(st[pair][:, h, 0:n], kT[par][0:MROW + PARTS, hh, j * P:(j + 1) * P],
                                          qT[par][0:MROW + PARTS, c, hh, q0 - c * CH:q0 - c * CH + n], start=True, stop=True)
                mm.then_inc(st_ready, 1)

            def product(g, par, u, very_first):
                c, j = UNITS[u]
                q0, n = unit_cols(u)
                off = q0 - c * CH
                if u == 0:
                    pe.wait_ge(v_set, g + 1)
                if u in (0, LAST[0] + 1) and not very_first:
                    pe.wait_ge(o_copied, 2 * g + (u > 0))
                if j >= 4 * c:
                    d = sum(jj >= 4 * cc for cc, jj in UNITS[:u + 1])
                    pe.wait_ge(sel_done, NDIAG * g + d)
                else:
                    pe.wait_ge(exp_done, 2 * NU * g + 2 * u + 2)
                for h in range(HG):
                    last = nc.tensor.matmul(pv[VW * h:VW * (h + 1), off:off + n], v[par][:, j, h, :],
                                            prob[u % PBUF][:, h, 0:n], start=(j == 0), stop=True,
                                            skip_group_check=True)
                last.then_inc(pv_done, 1)

            pe.wait_ge(lo_loaded[0], NL)
            pe.wait_ge(hi_loaded[0], NL)
            for n, (what, x, _) in enumerate(START):
                if what == "step":
                    scores_max(0, 0, x, n, n % RING)
                else:
                    turn_max(0, 0, n, n % RING, HALF_STEPS)

            def body(g, nth, par, first, last):
                base, at = ring_base(g, first)
                for u, (c, j) in enumerate(UNITS):
                    if u == 0:
                        pe.wait_ge(m_loaded, 16 * PARTS * (2 * g + 1))
                        if not last:
                            pe.wait_ge(lo_loaded[1 - par], NL * (nth + par + 1))
                    if u == LAST[0] + 1:
                        pe.wait_ge(m_loaded, 16 * PARTS * (2 * g + 2))
                    for what, x, y in ORDER[u]:
                        if what == "scores":
                            scores(g, par, u, x, first)
                        elif what == "product":
                            back = u < LAG
                            if not (first and back):
                                product(g - back, (1 - par) if back else par, (u - LAG) % NU, first and u == LAG)
                        elif not skipped(what, y, first, last):
                            n, bank = base + at, (ring_start(first) + at) % RING
                            if what == "step":
                                if x == FIRST_HI:
                                    pe.wait_ge(hi_loaded[1 - par], NL * (nth + par + 1))
                                scores_max(g + 1, 1 - par, x, n, bank)
                            elif what == "max":
                                turn_max(g + 1 - x, x, n, bank, base + HALF_STEPS_AT[first] + 1)
                            elif what == "out":
                                turn_out(g - y, x, n, bank)
                            at += 1
                if last:
                    for w in range(NU - LAG, NU):
                        product(g, par, w, False)
                    turn_out(g, 1, base + at, (ring_start(first) + at) % RING)

            groups(pe, body)

        @block.vector
        def _(dve):
            def row_max(s, n, bank):
                i, h0, per, _, keys, piece = STEPS[s]
                dve.wait_ge(ring_ready, n + 1)
                half = i // (QB // 2)
                dst = (mx2 if piece else mx[half])[:, h0:h0 + per, i % (QB // 2)]
                nc.vector.tensor_reduce(dst, ring[bank][:, 0:per * keys].rearrange("p (h k) -> p h k", k=keys),
                                        AX.X, ALU.max).then_inc(ring_free, 1)

            def join_max(n):
                dve.wait_ge(ring_free, n + 1)
                nc.vector.tensor_tensor(mx[1][:], mx[1][:], mx2[:], ALU.max).then_inc(mx_joined, 1)

            def cut_max(k, n, bank):
                dve.wait_ge(ring_ready, n + 1)
                if not (isinstance(k, int) and k == 0):
                    dve.wait_ge(m_loaded, 16 * PARTS * k)
                src = ring[bank][0:HG * QB // 2, 0:P]
                nc.vector.tensor_scalar(mneg[:, 0, :], src, -1.0, None, ALU.mult).then_inc(m_chain, 1)
                dve.wait_ge(m_chain, 2 * k + 1)
                nc.vector.scalar_tensor_tensor(out=mrest[:], in0=src, scalar=-1.0, in1=mneg[:, 0, :],
                                               op0=ALU.mult, op1=ALU.subtract).then_inc(ring_free, 1)
                dve.wait_ge(ring_free, n + 1)
                nc.vector.tensor_copy(mneg[:, 1, :], mrest[:]).then_inc(m_chain, 1)
                dve.wait_ge(m_chain, 2 * k + 2)
                nc.vector.tensor_tensor(mneg[:, 2, :], mrest[:], mneg[:, 1, :], ALU.subtract).then_inc(m_cut, 1)

            def norm_out(g, c, n, bank):
                dve.wait_ge(ring_ready, n + 1)
                o = ring[bank][:].rearrange("p (i h w) -> p i h w", i=4, w=VW)
                nc.vector.reciprocal(rec[:], o[:, :, :, HD]).then_inc(rec_done, 1)
                dve.wait_ge(rec_done, 2 * g + c + 1)
                dst = ctx_sb[:, g, 4 * c:4 * c + 4, :]
                nc.vector.tensor_tensor(dst.rearrange("p i (h d) -> p i h d", d=HD), o[:, :, :, 0:HD],
                                        rec[:].unsqueeze(3).broadcast_to([P, 4, HG, HD]),
                                        ALU.mult).then_inc(ring_free, 1)

            for n, (what, x, _) in enumerate(START):
                if what == "step":
                    row_max(x, n, n % RING)
                    if x == NSTEP - 1:
                        join_max(n)
                else:
                    cut_max(0, n, n % RING)

            def body(g, nth, par, first, last):
                base, at = ring_base(g, first)
                for u in range(NU):
                    for what, x, y in ORDER[u]:
                        if what in ("scores", "product") or skipped(what, y, first, last):
                            continue
                        n, bank = base + at, (ring_start(first) + at) % RING
                        if what == "step":
                            row_max(x, n, bank)
                            if x == NSTEP - 1:
                                join_max(n)
                        elif what == "max":
                            cut_max(2 * (g + 1 - x) + x, n, bank)
                        elif what == "out":
                            norm_out(g - y, x, n, bank)
                        at += 1
                if last:
                    norm_out(g, 1, base + at, (ring_start(first) + at) % RING)

            groups(dve, body)


def output_projection(nc, tag, ctx_sb, x, wo, bo, ident):
    N = TILES // 4
    with ExitStack() as ctx:
        sem = lambda n: ctx.enter_context(nc.semaphore(f"{tag}_{n}"))
        ps = lambda n: [ctx.enter_context(nc.psum_tensor(f"{tag}_{n}{i}", [P, CH], F32)) for i in range(2)]
        t_bank, o_bank = ps("t"), ps("o")
        cT = [ctx.enter_context(nc.sbuf_tensor(f"{tag}_cT{i}", [P, CH], F32)) for i in range(2)]
        rows = [ctx.enter_context(nc.sbuf_tensor(f"{tag}_rows{i}", [P, 4, D], F32)) for i in range(2)]
        gathered = sem("gathered")
        turned, copied, made, added, biased = sem("turned"), sem("copied"), sem("made"), sem("added"), sem("biased")
        block = ctx.enter_context(nc.Block())

        @block.tensor
        def _(pe):
            for n in range(N + 1):
                if n < N:
                    pe.wait_ge(gathered, n + 1)
                    if n >= 2:
                        pe.wait_ge(copied, n - 1)
                    for i in range(4):
                        last = nc.tensor.transpose(t_bank[n % 2][:, i * P:(i + 1) * P], rows[n % 2][:, i, :],
                                                   ident[:])
                    last.then_inc(turned, 1)
                if n >= 1:
                    m = n - 1
                    pe.wait_ge(copied, m + 1)
                    if m >= 2:
                        pe.wait_ge(added, m - 1)
                    for i in range(4):
                        last = nc.tensor.matmul(o_bank[m % 2][:, i * P:(i + 1) * P], cT[m % 2][:, i * P:(i + 1) * P],
                                                wo, start=True, stop=True)
                    last.then_inc(made, 1)

        @block.scalar
        def _(act):
            for n in range(N):
                act.wait_ge(turned, n + 1)
                if n >= 2:
                    act.wait_ge(made, n - 1)
                nc.scalar.activation(cT[n % 2][:], t_bank[n % 2][:], ACT.Copy).then_inc(copied, 1)

        @block.gpsimd
        def _(pool):
            for n in range(N):
                if n >= 2:
                    pool.wait_ge(turned, n - 1)
                seq, half = divmod(n, S // CH)
                groups = ctx_sb[:, seq * (H // HG):(seq + 1) * (H // HG), 4 * half:4 * half + 4, :]
                nc.gpsimd.tensor_copy(rows[n % 2][:].rearrange("p k (g w) -> p k g w", w=HG * HD),
                                      groups.rearrange("p g k w -> p k g w")).then_inc(gathered, 1)
                if bo is not None:
                    for t in range(4 * n, 4 * n + 4):
                        nc.gpsimd.tensor_tensor(x[:, t, :], x[:, t, :], bo[:], ALU.add).then_inc(biased, 1)

        @block.vector
        def _(dve):
            for n in range(N):
                dve.wait_ge(made, n + 1)
                if bo is not None:
                    dve.wait_ge(biased, 4 * n + 4)
                xs = x[:, 4 * n:4 * n + 4, :]
                nc.vector.tensor_tensor(xs, o_bank[n % 2][:].rearrange("p (i d) -> p i d", d=D), xs,
                                        ALU.add).then_inc(added, 1)


def route(nc, tag, xn, xnT, xn_dram, router, k, gate, take, give, tile_expert):
    with ExitStack() as ctx:
        sb = lambda n, s, d=F32: ctx.enter_context(nc.sbuf_tensor(f"{tag}_{n}", s, d))
        ps = lambda n, s: ctx.enter_context(nc.psum_tensor(f"{tag}_{n}", s, F32))
        sem = lambda n: ctx.enter_context(nc.semaphore(f"{tag}_{n}"))
        bank = ps("bank", [P, TILES, E_N])
        before = ps("before", [P, E_N, PAIRS])
        total = ps("total", [P, E_N, PAIRS])
        inverse = ps("inverse", [P, XTILES])
        logits = sb("logits", [P, TILES, E_N])
        top = sb("top", [P, TILES, 8])
        at = sb("at", [P, TILES, 8], U32)
        atf = sb("atf", [P, 2, TILES])
        den = sb("den", [P, TILES])
        hot = sb("hot", [P, E_N, PAIRS], BF16)
        run = sb("run", [P, E_N, PAIRS])
        pos = sb("pos", [P, E_N, PAIRS])
        sel = sb("sel", [P, E_N, PAIRS])
        count = sb("count", [P, E_N])
        more = sb("more", [P, E_N, TILES])
        ntile, end, shift = sb("ntile", [P, E_N]), sb("end", [P, E_N]), sb("shift", [P, E_N])
        past = sb("past", [1, XTILES, E_N])
        texp = sb("texp", [1, XTILES])
        slot = sb("slot", [P, PAIRS], U32)
        slot_tile_u, slot_row_u = sb("slot_tile_u", [P, PAIRS], U32), sb("slot_row_u", [P, PAIRS], U32)
        slot_tile, slot_row = sb("slot_tile", [P, PAIRS]), sb("slot_row", [P, PAIRS])
        NB, SHARE = 8, 4
        row_hot = [sb(f"row_hot{i}", [P, P]) for i in range(NB)]
        tile_hot = [sb(f"tile_hot{i}", [P, XTILES]) for i in range(NB)]
        spare, pair0, wrap = sb("spare", [P, XTILES]), sb("pair0", [P, XTILES]), sb("wrap", [P, XTILES])
        made, got, tops, exp_done, small = sem("made"), sem("got"), sem("tops"), sem("exp_done"), sem("small")
        hot_done, counted = sem("hot_done"), sem("counted")
        placed = sem("placed")
        rows_hot, tiles_hot, mixed = sem("rows_hot"), sem("tiles_hot"), sem("mixed")
        pool_hot = sem("pool_hot")
        xn_out = sem("xn_out")
        block = ctx.enter_context(nc.Block())

        @block.sync
        def _(sp):
            for c in range(B):
                sp.dma_start(xn_dram[c * S:(c + 1) * S, :].rearrange("(t p) d -> p t d", p=P),
                             xn[:, c * QB:(c + 1) * QB, :]).then_inc(xn_out, 16)
            sp.wait_ge(xn_out, 16 * B)

        @block.tensor
        def _(pe):
            for t in range(TILES):
                last = nc.tensor.matmul(bank[:, t, :], xnT[:, t * P:(t + 1) * P], router, start=True, stop=True)
            last.then_inc(made, 1)
            pe.wait_ge(hot_done, 1)
            nc.tensor.matmul(before[:], k["earlier"][:], hot[:], start=True, stop=True).then_inc(counted, 1)
            nc.tensor.matmul(total[:], k["all_ones"][:], hot[:], start=True, stop=True).then_inc(counted, 1)
            for n in range(PAIRS):
                pe.wait_ge(rows_hot, n + 1)
                if n % SHARE:
                    pe.wait_ge(tiles_hot, n - n // SHARE)
                else:
                    pe.wait_ge(pool_hot, n // SHARE + 1)
                nc.tensor.matmul(inverse[:], row_hot[n % NB][:], tile_hot[n % NB][:], start=(n == 0),
                                 stop=(n == PAIRS - 1)).then_inc(mixed, 1)

        @block.scalar
        def _(act):
            act.wait_ge(small, 1)
            nc.scalar.activation(gate[:, 1, :], den[:], ACT.Exp).then_inc(exp_done, 1)

        @block.gpsimd
        def _(pool):
            pool.wait_ge(placed, 2)
            for n in range(0, PAIRS, SHARE):
                if n >= NB:
                    pool.wait_ge(mixed, n - NB + 1)
                nc.gpsimd.tensor_scalar(tile_hot[n % NB][:], k["count_up"][:, 0:XTILES], slot_tile[:, n:n + 1],
                                        k["pair_no"][:, n:n + 1], ALU.is_equal, ALU.mult).then_inc(pool_hot, 1)

        @block.vector
        def _(dve):
            tick = [0]

            def after(ins):
                tick[0] += 1
                ins.then_inc(small, 1)

            dve.wait_ge(made, 1)
            nc.vector.tensor_copy(logits[:], bank[:]).then_inc(got, 1)
            dve.wait_ge(got, 1)
            for t in range(TILES):
                nc.vector.max(top[:, t, :], logits[:, t, :]).then_inc(tops, 1)
            dve.wait_ge(tops, TILES)
            for t in range(TILES):
                nc.vector.max_index(at[:, t, :], top[:, t, :], logits[:, t, :]).then_inc(tops, 1)
            nc.vector.tensor_tensor(den[:], top[:, :, 1], top[:, :, 0], ALU.subtract).then_inc(small, 1)
            dve.wait_ge(tops, 2 * TILES)
            nc.vector.tensor_copy(atf[:].rearrange("p k t -> p t k"), at[:, :, 0:2]).then_inc(small, 1)
            dve.wait_ge(small, 2)
            nc.vector.tensor_tensor(hot[:], atf[:].rearrange("p k t -> p (k t)").unsqueeze(1).broadcast_to([P, E_N, PAIRS]),
                                    k["count_up"][:, 0:E_N].unsqueeze(2).broadcast_to([P, E_N, PAIRS]),
                                    ALU.is_equal).then_inc(hot_done, 1)
            dve.wait_ge(exp_done, 1)
            nc.vector.tensor_scalar(den[:], gate[:, 1, :], 1.0, None, ALU.add).then_inc(small, 1)
            dve.wait_ge(small, 3)
            nc.vector.reciprocal(gate[:, 0, :], den[:]).then_inc(small, 1)
            dve.wait_ge(small, 4)
            nc.vector.tensor_tensor(gate[:, 1, :], gate[:, 1, :], gate[:, 0, :], ALU.mult).then_inc(small, 1)
            dve.wait_ge(counted, 2)
            flat = lambda m: m[:].rearrange("p e n -> p (e n)")
            nc.vector.tensor_tensor_scan(flat(run), k["ones_row"][:], flat(total), 0.0, ALU.mult,
                                         ALU.add).then_inc(small, 1)
            dve.wait_ge(small, 6)
            nc.vector.tensor_tensor(run[:], run[:], total[:], ALU.subtract).then_inc(small, 1)
            dve.wait_ge(small, 7)
            nc.vector.tensor_tensor(pos[:], run[:], before[:], ALU.add).then_inc(small, 1)
            nc.vector.tensor_reduce(count[:], total[:], AX.X, ALU.add).then_inc(small, 1)
            dve.wait_ge(small, 9)
            nc.vector.tensor_tensor(more[:], count[:].unsqueeze(2).broadcast_to([P, E_N, TILES]),
                                    k["by_tile"][:].unsqueeze(1).broadcast_to([P, E_N, TILES]),
                                    ALU.is_gt).then_inc(small, 1)
            dve.wait_ge(small, 10)
            nc.vector.tensor_reduce(ntile[:], more[:], AX.X, ALU.add).then_inc(small, 1)
            dve.wait_ge(small, 11)
            nc.vector.tensor_tensor_scan(end[:], k["ones_row"][:, 0:E_N], ntile[:], 0.0, ALU.mult,
                                         ALU.add).then_inc(small, 1)
            dve.wait_ge(small, 12)
            nc.vector.tensor_tensor(shift[:], end[:], ntile[:], ALU.subtract).then_inc(small, 1)
            dve.wait_ge(small, 13)
            nc.vector.scalar_tensor_tensor(out=shift[:], in0=shift[:], scalar=float(P), in1=run[:, :, 0],
                                           op0=ALU.mult, op1=ALU.subtract).then_inc(small, 1)
            dve.wait_ge(small, 14)
            nc.vector.tensor_tensor(pos[:], pos[:], shift[:].unsqueeze(2).broadcast_to([P, E_N, PAIRS]),
                                    ALU.add).then_inc(small, 1)
            dve.wait_ge(small, 15)
            nc.vector.tensor_tensor(sel[:], pos[:], hot[:], ALU.mult).then_inc(small, 1)
            dve.wait_ge(small, 16)
            nc.vector.tensor_reduce(slot_tile[:], sel[:].rearrange("p e n -> p n e"), AX.X, ALU.add).then_inc(small, 1)
            dve.wait_ge(small, 17)
            nc.vector.tensor_copy(slot[:], slot_tile[:]).then_inc(small, 1)
            dve.wait_ge(small, 18)
            nc.vector.tensor_scalar(slot_tile_u[:], slot[:], 7, None, ALU.logical_shift_right).then_inc(small, 1)
            nc.vector.tensor_scalar(slot_row_u[:], slot[:], P - 1, None, ALU.bitwise_and).then_inc(small, 1)
            dve.wait_ge(small, 20)
            nc.vector.tensor_copy(slot_tile[:], slot_tile_u[:]).then_inc(placed, 1)
            nc.vector.tensor_copy(slot_row[:], slot_row_u[:]).then_inc(placed, 1)
            dve.wait_ge(placed, 2)
            for n in range(PAIRS):
                if n >= NB:
                    dve.wait_ge(mixed, n - NB + 1)
                nc.vector.tensor_scalar(row_hot[n % NB][:], k["count_up"][:], slot_row[:, n:n + 1], None,
                                        ALU.is_equal).then_inc(rows_hot, 1)
                if n % SHARE:
                    nc.vector.tensor_scalar(tile_hot[n % NB][:], k["count_up"][:, 0:XTILES], slot_tile[:, n:n + 1],
                                            k["pair_no"][:, n:n + 1], ALU.is_equal, ALU.mult).then_inc(tiles_hot, 1)
            nc.vector.tensor_tensor(past[:], k["count_up"][0:1, 0:XTILES].unsqueeze(2).broadcast_to([1, XTILES, E_N]),
                                    end[0:1, :].unsqueeze(1).broadcast_to([1, XTILES, E_N]),
                                    ALU.is_ge).then_inc(small, 1)
            dve.wait_ge(small, 21)
            nc.vector.tensor_reduce(texp[:], past[:], AX.X, ALU.add).then_inc(small, 1)
            dve.wait_ge(small, 22)
            nc.vector.tensor_scalar(tile_expert[:], texp[:], float(E_N - 1), None, ALU.min).then_inc(small, 1)
            dve.wait_ge(mixed, PAIRS)
            nc.vector.scalar_tensor_tensor(out=spare[:], in0=inverse[:], scalar=0.0, in1=k["spare_row"][:],
                                           op0=ALU.is_equal, op1=ALU.mult).then_inc(small, 1)
            nc.vector.tensor_scalar(pair0[:], inverse[:], -1.0, 0.0, ALU.add, ALU.max).then_inc(small, 1)
            dve.wait_ge(small, 25)
            nc.vector.scalar_tensor_tensor(out=give[:], in0=inverse[:], scalar=-1.0, in1=spare[:], op0=ALU.add,
                                           op1=ALU.add).then_inc(small, 1)
            nc.vector.tensor_scalar(wrap[:], pair0[:], float(NT), float(NT), ALU.is_ge, ALU.mult).then_inc(small, 1)
            dve.wait_ge(small, 27)
            nc.vector.tensor_tensor(take[:], pair0[:], wrap[:], ALU.subtract).then_inc(small, 1)


def experts(nc, tag, xn_dram, y_dram, take, give, tile_expert, w1, w2, experts_in, ident, gathered, put, turn_no):
    XB, YB = len(gathered), len(put)
    N = XTILES // UNROLL
    G0, P0 = 2 * N * turn_no, N * turn_no
    with ExitStack() as ctx:
        sb = lambda n, s, d=F32: ctx.enter_context(nc.sbuf_tensor(f"{tag}_{n}", s, d))
        sem = lambda n: ctx.enter_context(nc.semaphore(f"{tag}_{n}"))
        ps = lambda n: [ctx.enter_context(nc.psum_tensor(f"{tag}_{n}{i}", [P, CH], F32)) for i in range(2)]
        t_bank, h_bank, y_bank = ps("t"), ps("h"), ps("y")
        xg = [sb(f"xg{i}", [P, D]) for i in range(XB)]
        xT = [sb(f"xT{i}", [P, P]) for i in range(2)]
        w1e = [sb(f"w1e{i}", [P, FF]) for i in range(2)]
        hs = [sb(f"hs{i}", [P, FC, P]) for i in range(2)]
        yo = [sb(f"yo{i}", [P, D]) for i in range(YB)]
        take4 = [sb(f"take4_{i}", [P, 4], U32) for i in range(2)]
        give4 = [sb(f"give4_{i}", [P, 4], U32) for i in range(2)]
        indexed, turned, xT_ready, w_ready = sem("indexed"), sem("turned"), sem("xT_ready"), sem("w_ready")
        passed = sem("passed")
        h_made, h_ready, y_made, y_ready = sem("h_made"), sem("h_ready"), sem("y_made"), sem("y_ready")
        block = ctx.enter_context(nc.Block())

        @block.gpsimd
        def _(pool):
            def take_waits():
                pool.sem_inc(passed, 1)

            def gather(j, r):
                t = UNROLL * j + r
                if not (isinstance(j, int) and t < XB):
                    pool.wait_ge(turned, t - XB + 1)
                take_waits()
                pool.indirect_dma_start(xg[r % XB][:], None, xn_dram,
                                        bass.IndirectOffsetOnAxis(take4[r // 4][:, r % 4:r % 4 + 1], 0)
                                        ).then_inc(gathered[r % XB], 16)

            def scatter(j, r):
                pool.wait_ge(y_ready, UNROLL * j + r + 1)
                take_waits()
                pool.indirect_dma_start(y_dram, bass.IndirectOffsetOnAxis(give4[r // 4][:, r % 4:r % 4 + 1], 0),
                                        yo[r][:], None).then_inc(put[r], 16)

            def give_index(j, half, first):
                if not first:
                    for r in range(4 * half, 4 * half + 4):
                        pool.wait_ge(put[r], 16 * (j + P0))
                    take_waits()
                nc.gpsimd.tensor_copy(give4[half][:], give[:, bass.ds(UNROLL * j + 4 * half, 4)]).then_inc(indexed, 1)

            def body(j, first, second):
                for r in range(UNROLL):
                    if r % 4 == 0:
                        nc.gpsimd.tensor_copy(take4[r // 4][:], take[:, bass.ds(UNROLL * j + r, 4)]).then_inc(indexed, 1)
                        if not first:
                            give_index(j - 1, r // 4, second)
                        pool.wait_ge(indexed, (r // 4 + 1) if first else 4 * j - 2 + 2 * (r // 4 + 1))
                    gather(j, r)
                    if not first:
                        scatter(j - 1, r)

            body(0, True, False)
            body(1, False, True)
            with pool.Fori(2, N) as j:
                body(j, False, False)
            for r in range(UNROLL):
                if r % 4 == 0:
                    give_index(N - 1, r // 4, False)
                    pool.wait_ge(indexed, 4 * N - 2 + r // 4 + 1)
                scatter(N - 1, r)
            for r in range(UNROLL):
                pool.wait_ge(put[r], 16 * (N + P0))

        @block.tensor
        def _(pe):
            def turn(j, r):
                t = UNROLL * j + r
                if not (isinstance(j, int) and t < 2):
                    pe.wait_ge(xT_ready, t - 1)
                pe.wait_ge(gathered[r % XB], 16 * (2 * j + r // XB + 1 + G0))
                nc.tensor.transpose(t_bank[r % 2][:, 0:P], xg[r % XB][:], ident[:]).then_inc(turned, 1)

            def up(t, r):
                pe.wait_ge(xT_ready, t + 1)
                pe.wait_ge(w_ready, t + 1)
                if not (isinstance(t, int) and t < 2):
                    pe.wait_ge(h_ready, t - 1)
                for f in range(FC):
                    last = nc.tensor.matmul(h_bank[r % 2][:, f * P:(f + 1) * P], w1e[r % 2][:, f * P:(f + 1) * P],
                                            xT[r % 2][:], start=True, stop=True)
                last.then_inc(h_made, 1)

            def down(t, r, e):
                pe.wait_ge(h_ready, t + 1)
                if not (isinstance(t, int) and t < 2):
                    pe.wait_ge(y_ready, t - 1)
                for f in range(FC):
                    last = nc.tensor.matmul(y_bank[r % 2][:, 0:D], hs[r % 2][:, f, :], w2[:, bass.ds(e, 1), f, :],
                                            start=(f == 0), stop=(f == FC - 1))
                last.then_inc(y_made, 1)

            def expert(t):
                return pe.value_load(tile_expert[0:1, bass.ds(t, 1)], min_val=0, max_val=E_N - 1)

            def body(j, first):
                if first:
                    pe.wait_ge(experts_in, 32)
                for r in range(UNROLL):
                    t = UNROLL * j + r
                    turn(j, r)
                    if not (first and r < 1):
                        up(t - 1, r - 1)
                    if not (first and r < 2):
                        down(t - 2, r, expert(t - 2))

            body(0, True)
            with pe.Fori(1, N) as j:
                body(j, False)
            up(XTILES - 1, 1)
            down(XTILES - 2, 0, expert(XTILES - 2))
            down(XTILES - 1, 1, expert(XTILES - 1))

        @block.vector
        def _(dve):
            def body(j, first):
                if first:
                    dve.wait_ge(experts_in, 32)
                for r in range(UNROLL):
                    t = UNROLL * j + r
                    if not (first and r < 2):
                        dve.wait_ge(h_made, t - 1)
                    e = dve.value_load(tile_expert[0:1, bass.ds(t, 1)], min_val=0, max_val=E_N - 1)
                    nc.vector.tensor_scalar(w1e[r % 2][:], w1[:, bass.ds(e, 1), :].rearrange("p e f -> p (e f)"), 1.0, None,
                                            ALU.mult).then_inc(w_ready, 1)
                    dve.wait_ge(turned, t + 1)
                    nc.vector.tensor_copy(xT[r % 2][:], t_bank[r % 2][:, 0:P]).then_inc(xT_ready, 1)

            body(0, True)
            with dve.Fori(1, N) as j:
                body(j, False)

        @block.scalar
        def _(act):
            def gelu(t, r):
                act.wait_ge(h_made, t + 1)
                if not (isinstance(t, int) and t < 2):
                    act.wait_ge(y_made, t - 1)
                nc.scalar.activation(hs[r % 2][:].rearrange("p f s -> p (f s)"), h_bank[r % 2][:],
                                     ACT.Gelu).then_inc(h_ready, 1)

            def results(j, r, first):
                act.wait_ge(y_made, UNROLL * j + r + 1)
                if not first:
                    act.wait_ge(put[r], 16 * (j + P0))
                nc.scalar.activation(yo[r][:], y_bank[r % 2][:, 0:D], ACT.Copy).then_inc(y_ready, 1)

            def body(j, first, second):
                for r in range(UNROLL):
                    gelu(UNROLL * j + r, r)
                    if r:
                        results(j, r - 1, first)
                    elif not first:
                        results(j - 1, UNROLL - 1, second)

            body(0, True, False)
            body(1, False, True)
            with act.Fori(2, N) as j:
                body(j, False, False)
            results(N - 1, UNROLL - 1, False)


def combine(nc, tag, x, gate, y_dram):
    N, YB = TILES // 4, 3
    with ExitStack() as ctx:
        sem = lambda n: ctx.enter_context(nc.semaphore(f"{tag}_{n}"))
        y = [ctx.enter_context(nc.sbuf_tensor(f"{tag}_y{i}", [P, 2, 4, D], F32)) for i in range(YB)]
        loaded, first_done, added = [sem(f"loaded{i}") for i in range(YB)], sem("first_done"), sem("added")
        block = ctx.enter_context(nc.Block())

        def load(eng, k):
            for c in range(N):
                if c >= YB:
                    eng.wait_ge(added, 4 * (c - YB + 1))
                row = k * NT + c * 4 * P
                eng.dma_start(y[c % YB][:, k, :, :],
                              y_dram[row:row + 4 * P, :].rearrange("(t p) d -> p t d", p=P)).then_inc(loaded[c % YB], 16)

        @block.sync
        def _(sp):
            load(sp, 0)

        @block.scalar
        def _(act):
            load(act, 1)

        @block.vector
        def _(dve):
            for c in range(N):
                dve.wait_ge(loaded[c % YB], 32 * (c // YB + 1))
                for k, done in ((0, first_done), (1, added)):
                    if k:
                        dve.wait_ge(first_done, 4 * (c + 1))
                    for i in range(4):
                        t = 4 * c + i
                        nc.vector.scalar_tensor_tensor(out=x[:, t, :], in0=y[c % YB][:, k, i, :],
                                                       scalar=gate[:, k, t:t + 1], in1=x[:, t, :], op0=ALU.mult,
                                                       op1=ALU.add).then_inc(done, 1)


def hybrid_block(nc, a, out):
    with ExitStack() as ctx:
        sb = lambda n, s, d=F32: ctx.enter_context(nc.sbuf_tensor(n, s, d))
        x = sb("x", [P, TILES, D])
        xn = sb("xn", [P, TILES, D])
        xnT = sb("xnT", [P, NT])
        ident = sb("ident", [P, P])
        ident_bf = sb("ident_bf", [P, P], BF16)
        mask = sb("mask", [P, P], BF16)
        earlier = sb("earlier", [P, P], BF16)
        all_ones = sb("all_ones", [P, P], BF16)
        count_up = sb("count_up", [P, P])
        by_tile = sb("by_tile", [P, TILES])
        pair_no = sb("pair_no", [P, PAIRS])
        spare_row = sb("spare_row", [P, XTILES])
        ones_row = sb("ones_row", [P, E_N * PAIRS])
        gate = sb("gate", [P, 2, TILES])
        take, give = sb("take", [P, XTILES], U32), sb("give", [P, XTILES], U32)
        tile_expert = sb("tile_expert", [1, XTILES], mybir.dt.int32)
        w1 = sb("w1", [P, E_N, FF])
        w2 = sb("w2", [P, E_N, FC, D])
        router = sb("router", [P, E_N])
        wA = {n: sb(f"wA_{n}", [P, D]) for n in "qkvo"}
        lora_a = {n: sb(f"lora_a_{n}", [16, D]) for n in "qkvo"}
        lora_b = {n: sb(f"lora_b_{n}", [16, D]) for n in "qkvo"}
        b_wq, b_wo = sb("b_wq", [P, D]), sb("b_wo", [P, D])
        b_wkd, b_wku = sb("b_wkd", [P, 64]), sb("b_wku", [64, 2 * D])
        b_bq, b_bk, b_bkd = sb("b_bq", [P, 1]), sb("b_bk", [P, 1]), sb("b_bkd", [64, 1])
        b_bv, b_bo = sb("b_bv", [P, D]), sb("b_bo", [P, D])
        q_dram = nc.dram_tensor("q_parts", (B, D, PARTS, S), BF16).ap()
        k_dram = nc.dram_tensor("k_parts", (PARTS, B, D, PARTS, S), BF16).ap()
        by_group = xn[:].rearrange("p t d -> p (t d)").rearrange("p (g t w) -> p g t w", g=GROUPS, t=QB)
        qT = [sb(f"qT{i}", [P, 2, HG, CH], BF16) for i in range(2)]
        kT = [sb(f"kT{i}", [P, HG, S], BF16) for i in range(2)]
        v = [sb(f"v{i}", [P, QB, HG, VW]) for i in range(2)]
        xn_dram = nc.dram_tensor("xn_rows", (NT, D), F32).ap()
        y_dram = nc.dram_tensor("expert_rows", (2 * NT + XTILES * P, D), F32).ap()
        experts_in = ctx.enter_context(nc.semaphore("experts_in"))
        gathered = [ctx.enter_context(nc.semaphore(f"gathered{i}")) for i in range(4)]
        put = [ctx.enter_context(nc.semaphore(f"put{i}")) for i in range(UNROLL)]
        consts = {"ident": ident, "ident_bf": ident_bf, "mask": mask, "earlier": earlier, "all_ones": all_ones,
                  "count_up": count_up, "by_tile": by_tile, "pair_no": pair_no, "spare_row": spare_row,
                  "ones_row": ones_row, "qT": qT, "kT": kT, "v": v}

        with ExitStack() as c2:
            sem = lambda n: c2.enter_context(nc.semaphore(n))
            x_in, w_in, c0, folded, lora_done = sem("x_in"), sem("w_in"), sem("c0"), sem("folded"), sem("lora_done")
            c1, padded = sem("c1"), sem("padded")
            spent = [x_in, w_in, c0, c1, padded, folded, lora_done]
            bank = c2.enter_context(nc.psum_tensor("fold", [P, 4, D], F32))
            block = c2.enter_context(nc.Block())

            @block.sync
            def _(sp):
                n = 0
                for c in range(B):
                    sp.dma_start(x[:, c * QB:(c + 1) * QB, :],
                                 a["x"][c].rearrange("(t p) d -> p t d", p=P)).then_inc(x_in, 16)
                sp.wait_ge(x_in, 16 * (B + 11))

            @block.scalar
            def _(act):
                n = 0
                for m in "qkvo":
                    for dst, src in ((wA[m], a["wT_" + m]), (lora_a[m], a["la_" + m]), (lora_b[m], a["lb_" + m])):
                        act.dma_start(dst[:], src).then_inc(w_in, 16)
                        n += 1
                bias = a["bku"]
                for dst, src in ((router[:], a["router"]), (b_wq[:], a["b_wq"]), (b_wo[:], a["b_wo"]),
                                 (b_wkd[:], a["b_wkd"]), (b_wku[0:32, :], a["b_wku"]), (b_wku[32:64, :], a["b_wku"]),
                                 (b_bq[:], a["bq"].unsqueeze(1)), (b_bk[:], bias[0:D].unsqueeze(1)),
                                 (b_bkd[:], a["bkd"].unsqueeze(1)), (b_bv[:], bias[D:2 * D].partition_broadcast(P)),
                                 (b_bo[:], a["bo"].partition_broadcast(P))):
                    act.dma_start(dst, src).then_inc(x_in, 16)
                act.dma_start(w1[:], a["w1"]).then_inc(experts_in, 16)
                act.dma_start(w2[:], a["w2"]).then_inc(experts_in, 16)
                act.wait_ge(x_in, 16 * (B + 11))

            @block.gpsimd
            def _(pool):
                nc.gpsimd.memset(ident[:], 0.0)
                nc.gpsimd.memset(mask[:], 0.0).then_inc(c0, 1)
                for dst, step, n, base, by_row in ((count_up, 1, P, 0, 0), (by_tile, P, TILES, 0, 0),
                                                   (pair_no, P, PAIRS, 1, 1), (spare_row, P, XTILES, 2 * NT + 1, 1)):
                    nc.gpsimd.iota(dst[:], pattern=[[step, n]], base=base, channel_multiplier=by_row,
                                   allow_small_or_imprecise_dtypes=True).then_inc(c1, 1)
                nc.gpsimd.memset(ones_row[:], 1.0).then_inc(c1, 1)
                nc.gpsimd.memset(all_ones[:], 1.0).then_inc(c1, 1)
                nc.gpsimd.memset(earlier[:], 1.0).then_inc(c1, 1)
                pool.wait_ge(c1, 7)
                nc.gpsimd.affine_select(out=earlier[:], in_=earlier[:], compare_op=ALU.is_gt, fill=0.0, base=0,
                                        pattern=[[1, P]], channel_multiplier=-1).then_inc(c1, 1)
                pool.wait_ge(c0, 1)
                nc.gpsimd.affine_select(out=ident[:], in_=ident[:], compare_op=ALU.not_equal, fill=1.0, base=0,
                                        pattern=[[-1, P]], channel_multiplier=1).then_inc(c0, 1)
                nc.gpsimd.affine_select(out=mask[:], in_=mask[:], compare_op=ALU.is_ge, fill=NEG, base=0,
                                        pattern=[[-1, P]], channel_multiplier=1).then_inc(c0, 1)
                pool.wait_ge(c0, 3)
                nc.gpsimd.tensor_copy(ident_bf[:], ident[:]).then_inc(c0, 1)

            @block.tensor
            def _(pe):
                pe.wait_ge(w_in, 16 * 12)
                for n, m in enumerate("qkvo"):
                    last = nc.tensor.matmul(bank[:, n, :], lora_a[m][:], lora_b[m][:], start=True, stop=True)
                last.then_inc(lora_done, 1)

            @block.vector
            def _(dve):
                for i in range(2):
                    nc.vector.memset(qT[i][64:96, :, :, :], 0.0).then_inc(padded, 1)
                    nc.vector.memset(kT[i][64:96, :, :], 0.0).then_inc(padded, 1)
                    nc.vector.memset(kT[i][MROW:MROW + PARTS, :, :], 1.0).then_inc(padded, 1)
                    nc.vector.memset(v[i][:, :, :, HD:HD + 1], 1.0).then_inc(padded, 1)
                    nc.vector.memset(v[i][:, :, :, HD + 1:VW], 0.0).then_inc(padded, 1)
                dve.wait_ge(lora_done, 1)
                for n, m in enumerate("qkvo"):
                    nc.vector.scalar_tensor_tensor(out=wA[m][:], in0=bank[:, n, :], scalar=1.0 / 16, in1=wA[m][:],
                                                   op0=ALU.mult, op1=ALU.add).then_inc(folded, 1)

        with nc.sbuf_tensor("v_sb", [P, GROUPS, QB, HG * HD], F32) as v_sb:
            layer_norm(nc, "ln1", x, xn, xnT, ident, spent)
            project(nc, "pa", xnT, v_sb, q_dram, k_dram, wA["q"][:], wA["k"][:], wA["v"][:], None, None, None, None, spent)
            attention(nc, "aa", v_sb, by_group, q_dram, k_dram, consts, spent)
            output_projection(nc, "oa", by_group, x, wA["o"][:], None, ident)
        layer_norm(nc, "ln2", x, xn, xnT, ident, spent)
        route(nc, "ra", xn, xnT, xn_dram, router[:], consts, gate, take, give, tile_expert)
        experts(nc, "ea", xn_dram, y_dram, take, give, tile_expert, w1, w2, experts_in, ident, gathered, put, 0)
        combine(nc, "cea", x, gate, y_dram)
        with nc.sbuf_tensor("v_sb2", [P, GROUPS, QB, HG * HD], F32) as v_sb:
            layer_norm(nc, "ln3", x, xn, xnT, ident, spent)
            project(nc, "pb", xnT, v_sb, q_dram, k_dram, b_wq[:], b_wku[:, 0:D], b_wku[:, D:2 * D],
                    b_bq[:, 0:1], b_bk[:, 0:1], b_bv, {"wkd": b_wkd, "bkd": b_bkd}, spent)
            attention(nc, "ab", v_sb, by_group, q_dram, k_dram, consts, spent)
            output_projection(nc, "ob", by_group, x, b_wo[:], b_bo, ident)
        layer_norm(nc, "ln4", x, xn, xnT, ident, spent)
        route(nc, "rb", xn, xnT, xn_dram, router[:], consts, gate, take, give, tile_expert)
        experts(nc, "eb", xn_dram, y_dram, take, give, tile_expert, w1, w2, experts_in, ident, gathered, put, 1)
        combine(nc, "ceb", x, gate, y_dram)

        with nc.semaphore("out_done") as out_done, nc.Block() as block:
            @block.sync
            def _(sp):
                for c in range(B):
                    sp.dma_start(out[c].rearrange("(t p) d -> p t d", p=P),
                                 x[:, c * QB:(c + 1) * QB, :]).then_inc(out_done, 16)
                sp.wait_ge(out_done, 16 * B)


def kernel(**inputs):
    import numpy as np
    import concourse.bacc as bacc
    from concourse.bass_utils import run_bass_kernel_spmd

    def get(n):
        return np.asarray(inputs[n])

    w1 = get("L0_ffn_w1")
    w2 = get("L0_ffn_w2")
    arrays = {"x": get("L0_attn_a_x")}
    for m in "qkvo":
        arrays["wT_" + m] = get(f"L0_attn_a_w{m}").T
        arrays["la_" + m] = get(f"L0_attn_a_a{m}")
        arrays["lb_" + m] = get(f"L0_attn_a_b{m}").T
    arrays.update(
        w1=w1.transpose(2, 0, 1),
        w2=w2.reshape(w2.shape[0], w2.shape[1], 4, 128).transpose(3, 0, 2, 1),
        router=get("L0_ffn_router_w").T,
        b_wq=get("L0_attn_b_Wq"), b_wo=get("L0_attn_b_Wo"), b_wkd=get("L0_attn_b_Wkd"), b_wku=get("L0_attn_b_Wku"),
        bq=get("L0_attn_b_bq"), bkd=get("L0_attn_b_bkd"), bku=get("L0_attn_b_bku"), bo=get("L0_attn_b_bo"),
    )
    nc = bacc.Bacc("TRN2", target_bir_lowering=False, num_devices=1)
    fed, a = {}, {}
    for name, value in arrays.items():
        value = np.ascontiguousarray(value)
        fed[f"in_{name}"] = value
        a[name] = nc.dram_tensor(f"in_{name}", value.shape, mybir.dt.from_np(value.dtype), kind="ExternalInput").ap()
    out = nc.dram_tensor("out", (B, S, D), F32, kind="ExternalOutput").ap()
    hybrid_block(nc, a, out)
    r = run_bass_kernel_spmd(nc, [fed], core_ids=[0])
    return r.results[0]["out"]
```

```python
from contextlib import ExitStack

import concourse.bass as bass
from concourse import mybir

ALU = mybir.AluOpType
ACT = mybir.ActivationFunctionType
AX = mybir.AxisListType
F32 = mybir.dt.float32
BF16 = mybir.dt.bfloat16
U32 = mybir.dt.uint32
I32 = mybir.dt.int32

P = 128
D = 128
B = 4
S = 1024
NT = B * S
TILES = NT // P
H = 16
HD = D // H
EPS = 1e-5
NEG = -1e30

HG = 4
GROUPS = B * (H // HG)
QB = S // P
CH = 512
PARTS = 3
ROWS = PARTS * PARTS * HD
MROW = 96
VW = 32

E_N = 8
FF = 512
FC = FF // P
PAIRS = 2 * TILES
STEP = 8
UNROLL = 8
XTILES = -(-((PAIRS * P + E_N * (P - 1)) // P) // UNROLL) * UNROLL


UNITS = [(0, 0), (0, 3), (0, 2), (0, 1),
         (1, 0), (1, 1), (1, 2), (1, 3), (1, 7), (1, 6), (1, 5), (1, 4)]
NU = len(UNITS)
NDIAG = sum(j >= 4 * c for c, j in UNITS)
LAST = {c: max(u for u, (cc, _) in enumerate(UNITS) if cc == c) for c in (0, 1)}
PBUF = 4
LAG = 2


def unit_cols(u):
    c, j = UNITS[u]
    q0 = max(P * j, CH * c)
    return q0, CH * (c + 1) - q0


def max_steps():
    steps = []
    for i in range(QB):
        keys = P * (i + 1)
        first = min(keys, CH)
        per = CH // first if CH % first == 0 else 1
        for h in range(0, HG, per):
            steps.append((i, h, per, 0, first, 0))
        if keys > CH:
            rest = keys - CH
            per = {P: 4, 2 * P: 2}.get(rest, 1)
            for h in range(0, HG, per):
                steps.append((i, h, per, CH, rest, 1))
    return steps


STEPS = max_steps()
NSTEP = len(STEPS)


RING = 3
HALF_STEPS = sum(i < QB // 2 for i, *_ in STEPS)
FIRST_HI = HALF_STEPS


def plan():
    cols = [unit_cols(u)[1] for u in range(NU)]
    cost = [per * keys for _, _, per, _, keys, _ in STEPS]
    order, s, done = [], 0, 0
    for u in range(NU):
        goal = sum(cost) * sum(cols[:u + 1]) / sum(cols)
        steps = []
        while s < NSTEP and done + cost[s] / 2 <= goal + 1e-6 or (u == NU - 1 and s < NSTEP):
            done += cost[s]
            steps.append(("step", s, 0))
            s += 1
        atoms = [("scores", 0, 0), ("scores", 1, 0), ("product", 0, 0)]
        starts = [0.0, 0.25, 0.5]
        mixed = sorted([(f, 0, n, a) for n, (f, a) in enumerate(zip(starts, atoms))]
                       + [((n + 0.5) / len(steps), 1, n, a) for n, a in enumerate(steps)])
        mixed = [a for *_, a in mixed]
        if u == 1:
            mixed.insert(1, ("max", 1, 0))
        if u > 1 and any(("step", HALF_STEPS - 1, 0) in x for x in order) and \
                not any(("max", 0, 1) in x for x in order):
            mixed.insert(len(mixed) - 1, ("max", 0, 1))
        if u == LAST[1] + LAG - NU + 1:
            mixed.append(("out", 1, 1))
        if u == LAST[0] + LAG + 1:
            mixed.append(("out", 0, 0))
        order.append(mixed)
    return order


ORDER = plan()
START = [("step", s, 0) for s in range(HALF_STEPS + 3)] + [("max", 0, 1)] \
    + [("step", s, 0) for s in range(HALF_STEPS + 3, NSTEP)]
PER_GROUP = sum(w in ("step", "max", "out") for u in ORDER for w, _, _ in u)
assert NU % PBUF == 0 and PER_GROUP % RING == 0 and PER_GROUP == NSTEP + 4


def skipped(what, y, first, last):
    return (first and what == "out" and y == 1) or (last and what == "step") or (last and what == "max" and y == 1)


def ring_start(first):
    return len(START) % RING if first else (len(START) + PER_GROUP - 1) % RING


def ring_base(g, first):
    return (len(START) if first else len(START) + PER_GROUP * g - 1), 0


def index_in_group(item, first, last=False):
    flat = [i for u in ORDER for i in u if i[0] in ("step", "max", "out") and not skipped(i[0], i[2], first, last)]
    return flat.index(item)


HALF_STEPS_AT = {f: index_in_group(("step", HALF_STEPS - 1, 0), f) for f in (True, False)}


def out_index(g, c, first, last):
    if c == 1:
        return ring_base(g + 1, False)[0] + index_in_group(("out", 1, 1), False, last)
    return ring_base(g, first)[0] + index_in_group(("out", 0, 0), first, last)


NEWTON = 3
POOL_TILES = 1
NORM_STEPS = 11 + 3 * NEWTON


class Norm:

    def __init__(self, nc, ctx, tag, x, xn, xnT, ident):
        sb = lambda n, s: ctx.enter_context(nc.sbuf_tensor(f"{tag}_{n}", s, F32))
        sem = lambda n: ctx.enter_context(nc.semaphore(f"{tag}_{n}"))
        self.nc, self.x, self.xn, self.xnT, self.ident = nc, x, xn, xnT, ident
        self.stats = sb("stats", [P, TILES, 6])
        self.mv = sb("mv", [P, TILES, 2])
        self.rstd = sb("rstd", [P, TILES])
        self.v, self.w = sb("v", [P, 4]), sb("w", [P, 4])
        self.bits = ctx.enter_context(nc.sbuf_tensor(f"{tag}_bits", [P, 4], I32))
        self.bank = [ctx.enter_context(nc.psum_tensor(f"{tag}_xT{i}", [P, CH], F32)) for i in range(2)]
        self.steps, self.xn_ready, self.xn_pool = sem("norm_steps"), sem("xn_ready"), sem("xn_pool")
        self.turned, self.copied = sem("turned"), sem("copied")
        self.sems = [self.steps, self.xn_ready, self.xn_pool, self.turned, self.copied]

    def normalise(self, dve, c, between=lambda i: None):
        nc, tiles = self.nc, range(4 * c, 4 * c + 4)
        for t in tiles:
            nc.vector.bn_stats(self.stats[:, t, :], self.x[:, t, :]).then_inc(self.steps, 1)
        dve.wait_ge(self.steps, NORM_STEPS * c + 4)
        for t in tiles:
            nc.vector.bn_aggr(self.mv[:, t, :], self.stats[:, t, :]).then_inc(self.steps, 1)
        dve.wait_ge(self.steps, NORM_STEPS * c + 8)
        v, y, w = self.v[:], self.rstd[:, 4 * c:4 * c + 4], self.w[:]
        nc.vector.tensor_scalar(v, self.mv[:, 4 * c:4 * c + 4, 1], EPS, None, ALU.add).then_inc(self.steps, 1)
        between(0)
        dve.wait_ge(self.steps, NORM_STEPS * c + 9)
        nc.vector.tensor_scalar(self.bits[:], v.bitcast(I32), 1, None, ALU.logical_shift_right).then_inc(self.steps, 1)
        between(1)
        dve.wait_ge(self.steps, NORM_STEPS * c + 10)
        nc.vector.tensor_scalar(y.bitcast(I32), self.bits[:], -1.0, float(0x5F3759DF), ALU.mult,
                                ALU.add).then_inc(self.steps, 1)
        for i in range(NEWTON):
            done = NORM_STEPS * c + 11 + 3 * i
            between(3 * i + 2)
            dve.wait_ge(self.steps, done)
            nc.vector.tensor_tensor(w, y, y, ALU.mult).then_inc(self.steps, 1)
            between(3 * i + 3)
            dve.wait_ge(self.steps, done + 1)
            nc.vector.scalar_tensor_tensor(out=w, in0=w, scalar=-0.5, in1=v, op0=ALU.mult,
                                           op1=ALU.mult).then_inc(self.steps, 1)
            between(3 * i + 4)
            dve.wait_ge(self.steps, done + 2)
            nc.vector.scalar_tensor_tensor(out=y, in0=w, scalar=1.5, in1=y, op0=ALU.add,
                                           op1=ALU.mult).then_inc(self.steps, 1)
        between(3 * NEWTON + 2)
        dve.wait_ge(self.steps, NORM_STEPS * (c + 1))
        self.scale(nc.vector, c, range(4 - POOL_TILES), self.xn_ready)

    def scale(self, engine, c, tiles, done):
        for t in (4 * c + i for i in tiles):
            engine.tensor_scalar(self.xn[:, t, :], self.x[:, t, :], self.mv[:, t, 0:1], self.rstd[:, t:t + 1],
                                 ALU.subtract, ALU.mult).then_inc(done, 1)

    def help(self, pool, c):
        pool.wait_ge(self.steps, NORM_STEPS * (c + 1))
        self.scale(self.nc.gpsimd, c, range(4 - POOL_TILES, 4), self.xn_pool)

    def wait_xn(self, eng, chunks):
        eng.wait_ge(self.xn_ready, (4 - POOL_TILES) * chunks)
        eng.wait_ge(self.xn_pool, POOL_TILES * chunks)

    def turn(self, pe, c):
        nc = self.nc
        self.wait_xn(pe, c + 1)
        if c >= 2:
            pe.wait_ge(self.copied, c - 1)
        for i in range(4):
            last = nc.tensor.transpose(self.bank[c % 2][:, i * P:(i + 1) * P], self.xn[:, 4 * c + i, :], self.ident[:])
        last.then_inc(self.turned, 1)

    def copy(self, act, c):
        act.wait_ge(self.turned, c + 1)
        self.nc.scalar.activation(self.xnT[:, c * CH:(c + 1) * CH], self.bank[c % 2][:], ACT.Copy).then_inc(self.copied, 1)


class Adder:

    def __init__(self, nc, ctx, tag, x, gate, y_dram, buffers):
        self.buffers = buffers
        sem = lambda n: ctx.enter_context(nc.semaphore(f"{tag}_{n}"))
        self.nc, self.x, self.gate, self.y_dram = nc, x, gate, y_dram
        self.y = [ctx.enter_context(nc.sbuf_tensor(f"{tag}_y{i}", [P, 2, 4, D], F32)) for i in range(self.buffers)]
        self.loaded = [sem(f"y_loaded{i}") for i in range(self.buffers)]
        self.scaled, self.first_added, self.added = sem("scaled"), sem("first_added"), sem("added")
        self.sems = [*self.loaded, self.scaled, self.first_added, self.added]

    def load(self, eng, c):
        if c >= self.buffers:
            eng.wait_ge(self.added, 4 * (c - self.buffers + 1))
        for k in range(2):
            row = k * NT + c * 4 * P
            eng.dma_start(self.y[c % self.buffers][:, k, :, :], self.y_dram[row:row + 4 * P, :].rearrange(
                "(t p) d -> p t d", p=P)).then_inc(self.loaded[c % self.buffers], 16)

    def scale(self, act, c):
        act.wait_ge(self.loaded[c % self.buffers], 32 * (c // self.buffers + 1))
        y = self.y[c % self.buffers]
        for i in range(4):
            self.nc.scalar.activation(y[:, 0, i, :], y[:, 0, i, :], ACT.Copy,
                                      scale=self.gate[:, 0, 4 * c + i:4 * c + i + 1]).then_inc(self.scaled, 1)

    def add_first(self, pool, c):
        pool.wait_ge(self.scaled, 4 * (c + 1))
        tiles = self.x[:, 4 * c:4 * c + 4, :]
        self.nc.gpsimd.tensor_tensor(tiles, tiles, self.y[c % self.buffers][:, 0, :, :], ALU.add).then_inc(self.first_added, 1)

    def add_second(self, dve, c, i):
        t = 4 * c + i
        if i == 0:
            dve.wait_ge(self.first_added, c + 1)
        self.nc.vector.scalar_tensor_tensor(out=self.x[:, t, :], in0=self.y[c % self.buffers][:, 1, i, :],
                                            scalar=self.gate[:, 1, t:t + 1], in1=self.x[:, t, :], op0=ALU.mult,
                                            op1=ALU.add).then_inc(self.added, 1)


K_STORES = [(0, 0, 3, 0), (1, 1, 2, 0), (1, 0, 1, 2), (2, 2, 1, 0), (2, 0, 2, 1)]
STORES = (1, len(K_STORES))


def load_group(nc, sp, k, loaded, q_dram, k_dram, g, par, half):
    qT, kT = k["qT"][par], k["kT"][par]
    n = PARTS * HD
    for x in range(PARTS):
        for dst, dram, first in ((qT[x * n:(x + 1) * n, half, :, :], q_dram, 0),
                                 (kT[x * n:(x + 1) * n, :, half * CH:(half + 1) * CH], k_dram, x * NT * D * PARTS)):
            sp.dma_start(dst, bass.AP(dram.tensor, first + g * (HG * n * S) + half * CH,
                                      [[S, n], [n * S, HG], [1, CH]])).then_inc(loaded[half][par], 16)


def project(nc, tag, x, xn, xnT, ident, x_in, results, v_sb, q_dram, k_dram, k, loaded, wq, wk,
            wv, bq, bk, bv, latent, spent):
    N = NT // CH
    with ExitStack() as ctx:
        sb = lambda n, s, d: ctx.enter_context(nc.sbuf_tensor(f"{tag}_{n}", s, d))
        sem = lambda n: ctx.enter_context(nc.semaphore(f"{tag}_{n}"))
        ps = lambda n: [ctx.enter_context(nc.psum_tensor(f"{tag}_{n}{i}", [P, CH], F32)) for i in range(2)]
        qk_bank, v_bank, l_bank = ps("qk"), ps("v"), ps("l")
        parts = [sb(f"parts{i}", [P, PARTS, CH], BF16) for i in range(4)]
        rest = [sb(f"rest{i}", [P, CH], F32) for i in range(2)]
        gl = [sb(f"gl{i}", [64, CH], F32) for i in range(2)] if latent else None
        norm = Norm(nc, ctx, tag, x, xn, xnT, ident)
        adder = Adder(nc, ctx, tag, x, *results, buffers=4) if results else None
        qk_ready, first_done, rest_done, second_done = sem("qk_ready"), sem("first"), sem("rest"), sem("second")
        third_done, v_ready, v_copied = sem("third"), sem("v_ready"), sem("v_copied")
        stored = [[sem(f"stored{s}_{i}") for i in range(2)] for s in range(2)]
        l_ready, l_done = sem("l_ready"), sem("l_done")
        spent += norm.sems + (adder.sems if adder else [])
        spent += [qk_ready, first_done, rest_done, second_done, third_done, *stored[0], *stored[1],
                  v_ready, v_copied, l_ready, l_done]
        block = ctx.enter_context(nc.Block())

        def by_head_group(c):
            seq, half = divmod(c, S // CH)
            groups = v_sb[:, seq * (H // HG):(seq + 1) * (H // HG), 4 * half:4 * half + 4, :]
            return (groups.rearrange("p g k w -> p k g w"),
                    v_bank[c % 2][:].rearrange("p (k g w) -> p k g w", k=4, w=HG * HD))

        @block.tensor
        def _(pe):
            norm.turn(pe, 0)
            for c in range(N):
                pe.wait_ge(norm.copied, c + 1)
                src = xnT[:, c * CH:(c + 1) * CH]
                if latent:
                    if c >= 2:
                        pe.wait_ge(l_done, c - 1)
                    nc.tensor.matmul(l_bank[c % 2][0:64, :], latent["wkd"][:], src, start=True,
                                     stop=True).then_inc(l_ready, 1)
                for s in range(2):
                    n = 2 * c + s
                    if n >= 2:
                        pe.wait_ge(first_done, n - 1)
                        pe.wait_ge(rest_done, n - 1)
                    if s and latent:
                        pe.wait_ge(l_done, c + 1)
                        nc.tensor.matmul(qk_bank[n % 2][:], wk, gl[c % 2][:], start=True,
                                         stop=True).then_inc(qk_ready, 1)
                    else:
                        nc.tensor.matmul(qk_bank[n % 2][:], wk if s else wq, src, start=True,
                                         stop=True).then_inc(qk_ready, 1)
                if c >= 2:
                    pe.wait_ge(v_copied, c - 1)
                for k in range(4):
                    left = gl[c % 2][:, k * P:(k + 1) * P] if latent else xnT[:, c * CH + k * P:c * CH + (k + 1) * P]
                    last = nc.tensor.matmul(v_bank[c % 2][:, k * P:(k + 1) * P], left, wv, start=True, stop=True)
                last.then_inc(v_ready, 1)
                if c + 1 < N:
                    norm.turn(pe, c + 1)

        @block.scalar
        def _(act):
            if adder:
                adder.scale(act, 0)
                adder.scale(act, 1)
            norm.copy(act, 0)
            for c in range(N):
                if adder and c + 2 < N:
                    adder.scale(act, c + 2)
                if latent:
                    act.wait_ge(l_ready, c + 1)
                    if c >= 2:
                        act.wait_ge(v_ready, c - 1)
                    nc.scalar.activation(gl[c % 2][:], l_bank[c % 2][0:64, :], ACT.Gelu,
                                         bias=latent["bkd"][:, 0:1]).then_inc(l_done, 1)
                for s in range(2):
                    n = 2 * c + s
                    act.wait_ge(qk_ready, n + 1)
                    if c >= 2:
                        act.wait_ge(stored[s][c % 2], 16 * STORES[s] * (c // 2))
                    b = bk if s else bq
                    if b is None:
                        nc.scalar.activation(parts[n % 4][:, 0, :], qk_bank[n % 2][:], ACT.Copy).then_inc(first_done, 1)
                    else:
                        nc.scalar.activation(parts[n % 4][:, 0, :], qk_bank[n % 2][:], ACT.Identity,
                                             bias=b).then_inc(first_done, 1)
                if c + 1 < N:
                    norm.copy(act, c + 1)
                for s in range(2):
                    n = 2 * c + s
                    act.wait_ge(rest_done, n + 1)
                    nc.scalar.activation(parts[n % 4][:, 1, :], rest[n % 2][:], ACT.Copy).then_inc(second_done, 1)
                if bv is None:
                    act.wait_ge(v_ready, c + 1)
                    nc.scalar.activation(*by_head_group(c), ACT.Copy).then_inc(v_copied, 1)

        @block.vector
        def _(dve):
            def normalise(c):
                if adder is None:
                    if c % 2 == 0:
                        dve.wait_ge(x_in[c // 2], 16)
                    norm.normalise(dve, c)
                    return
                if c == 0:
                    for i in range(4):
                        adder.add_second(dve, 0, i)
                dve.wait_ge(adder.added, 4 * (c + 1))
                def between(i):
                    if c + 1 < N and i >= 8:
                        adder.add_second(dve, c + 1, i - 8)

                norm.normalise(dve, c, between)

            normalise(0)
            for c in range(N):
                if c + 1 < N:
                    normalise(c + 1)
                for s in range(2):
                    n = 2 * c + s
                    b = bk if s else bq
                    dve.wait_ge(first_done, n + 1)
                    if n >= 2:
                        dve.wait_ge(third_done, n - 1)
                    nc.vector.scalar_tensor_tensor(out=rest[n % 2][:], in0=qk_bank[n % 2][:],
                                                   scalar=0.0 if b is None else b, in1=parts[n % 4][:, 0, :],
                                                   op0=ALU.add, op1=ALU.subtract).then_inc(rest_done, 1)
                if bv is not None:
                    dve.wait_ge(v_ready, c + 1)
                    dst, src = by_head_group(c)
                    by_group = bv[:].rearrange("p (g w) -> p g w", w=HG * HD).unsqueeze(1)
                    nc.vector.tensor_tensor(dst, src, by_group.broadcast_to([P, 4, H // HG, HG * HD]),
                                            ALU.add).then_inc(v_copied, 1)

        @block.gpsimd
        def _(pool):
            if adder:
                adder.add_first(pool, 0)
                adder.add_first(pool, 1)
            norm.help(pool, 0)
            for n in range(2 * N):
                c = n // 2
                if n % 2 == 0 and adder and c + 2 < N:
                    adder.add_first(pool, c + 2)
                if n % 2 == 0 and c + 1 < N:
                    norm.help(pool, c + 1)
                pool.wait_ge(second_done, n + 1)
                nc.gpsimd.tensor_tensor(parts[n % 4][:, 2, :], rest[n % 2][:], parts[n % 4][:, 1, :],
                                        ALU.subtract).then_inc(third_done, 1)

        @block.sync
        def _(sp):
            for c in range(adder.buffers if adder else 0):
                adder.load(sp, c)
            for c in range(N):
                if c == 4:
                    for s in range(2):
                        for i in range(2):
                            sp.wait_ge(stored[s][i], 16 * STORES[s])
                    for half in range(2):
                        load_group(nc, sp, k, loaded, q_dram, k_dram, 0, 0, half)
                if adder and c + adder.buffers < N:
                    adder.load(sp, c + adder.buffers)
                seq, half = divmod(c, S // CH)
                cols = slice(half * CH, (half + 1) * CH)
                sp.wait_ge(third_done, 2 * c + 1)
                sp.dma_start(q_dram[seq, :, :, cols], parts[2 * c % 4][:]).then_inc(stored[0][c % 2], 16)
                sp.wait_ge(third_done, 2 * c + 2)
                for x, part, n, place in K_STORES:
                    sp.dma_start(k_dram[x, seq, :, place:place + n, cols],
                                 parts[(2 * c + 1) % 4][:, part:part + n, :]).then_inc(stored[1][c % 2], 16)
            for s in range(2):
                for i in range(2):
                    sp.wait_ge(stored[s][i], 16 * STORES[s] * (N // 2))


def attention(nc, tag, v_sb, ctx_sb, q_dram, k_dram, k, loaded, later, later_in, spent):
    SCALE = float(HD) ** -0.5
    with ExitStack() as ctx:
        sb = lambda n, s, d: ctx.enter_context(nc.sbuf_tensor(f"{tag}_{n}", s, d))
        ps = lambda n, s: ctx.enter_context(nc.psum_tensor(f"{tag}_{n}", s, F32))
        sem = lambda n: ctx.enter_context(nc.semaphore(f"{tag}_{n}"))
        qT, kT, v = k["qT"], k["kT"], k["v"]
        prob = [sb(f"prob{i}", [P, HG, CH], F32) for i in range(PBUF)]
        mx = [sb(f"mx{i}", [P, HG, QB // 2], F32) for i in range(2)]
        mx2 = sb("mx2", [P, HG, QB // 2], F32)
        mneg = sb("mneg", [HG * QB // 2, PARTS, P], BF16)
        mrest = sb("mrest", [HG * QB // 2, P], F32)
        oT = sb("oT", [P, CH], F32)
        rec = sb("rec", [P, 4, HG], F32)
        st = [ps(f"st{i}", [P, 2, CH]) for i in range(2)]
        ring = [ps(f"ring{i}", [P, CH]) for i in range(RING)]
        pv = ps("pv", [P, CH])

        lo_loaded, hi_loaded = loaded
        v_set = sem("v_set")
        ring_ready, ring_free = sem("ring_ready"), sem("ring_free")
        mx_joined = sem("mx_joined")
        m_chain = sem("m_chain")
        m_cut, m_loaded = sem("m_cut"), sem("m_loaded")
        st_ready, exp_done, sel_done, pv_done = sem("st_ready"), sem("exp_done"), sem("sel_done"), sem("pv_done")
        o_copied, rec_done = sem("o_copied"), sem("rec_done")
        block = ctx.enter_context(nc.Block())

        NL = 2 * PARTS * 16

        def groups(eng, body):
            body(0, 0, 0, True, False)
            with eng.Fori(0, GROUPS // 2 - 1) as i:
                body(2 * i + 1, i, 1, False, False)
                body(2 * i + 2, i + 1, 0, False, False)
            body(GROUPS - 1, GROUPS // 2 - 1, 1, False, True)

        @block.sync
        def _(sp):
            def send(par, half):
                for a in range(PARTS):
                    dst = qT[par][MROW + a:MROW + a + 1, half, :, :]
                    sp.dma_start(dst.rearrange("o h (i q) -> o (h i) q", q=P),
                                 mneg[:, a, :]).then_inc(m_loaded, 16)

            def load(g, par, half):
                load_group(nc, sp, k, loaded, q_dram, k_dram, g, par, half)

            load(1, 1, 0)
            load(1, 1, 1)
            sp.wait_ge(m_cut, 1)
            send(0, 0)
            for dst, src in later:
                sp.dma_start(dst, src).then_inc(later_in, 16)

            def step(g, par):
                sp.wait_ge(m_cut, 2 * g + 2)
                send(par, 1)
                sp.wait_ge(m_cut, 2 * g + 3)
                send(1 - par, 0)
                sp.wait_ge(st_ready, 2 * NU * g + 2 * (UNITS.index((1, 3)) + 1))
                load(g + 2, par, 0)
                sp.wait_ge(st_ready, 2 * NU * (g + 1))
                load(g + 2, par, 1)

            with sp.Fori(0, GROUPS // 2 - 1) as i:
                step(2 * i, 0)
                step(2 * i + 1, 1)
            for g in (GROUPS - 2, GROUPS - 1):
                sp.wait_ge(m_cut, 2 * g + 2)
                send(g % 2, 1)
                if g == GROUPS - 2:
                    sp.wait_ge(m_cut, 2 * g + 3)
                    send(1, 0)
            sp.wait_ge(m_loaded, 2 * GROUPS * PARTS * 16)
            if later:
                sp.wait_ge(later_in, 16 * len(later))

        @block.gpsimd
        def _(pool):
            for s in spent:
                nc.gpsimd.sem_clear(s)
            spent[:] = [v_set, ring_ready, ring_free, mx_joined, m_chain, m_cut, m_loaded, st_ready, exp_done, sel_done,
                        pv_done, o_copied, rec_done]
            def values(g, par):
                nc.gpsimd.tensor_copy(v[par][:, :, :, 0:HD],
                                      v_sb[:, g, :, :].rearrange("p t (h d) -> p t h d", d=HD)).then_inc(v_set, 1)

            values(0, 0)
            fill = pool.alloc_register(f"{tag}_fill")
            pool.reg_mov(fill, 0)

            def body(g, nth, par, first, last):
                for u, (c, j) in enumerate(UNITS):
                    if u == 6 and not last:
                        if not first:
                            pool.wait_ge(pv_done, NU * g)
                        values(g + 1, 1 - par)
                    if j >= 4 * c:
                        pool.wait_ge(exp_done, 2 * NU * g + 2 * u + 2)
                        pool.reg_mul(fill, fill, 2)
                        diag = prob[u % PBUF][:, :, 0:P]
                        nc.gpsimd.affine_select(out=diag, in_=diag, compare_op=ALU.is_ge, fill=fill, base=0,
                                                pattern=[[0, HG], [1, P]], channel_multiplier=-1
                                                ).then_inc(sel_done, 1)

            groups(pool, body)

        @block.scalar
        def _(act):
            def copy_out(g, c, first, last):
                act.wait_ge(pv_done, NU * g + LAST[c] + 1)
                if c:
                    act.wait_ge(ring_free, out_index(g, 0, first, last) + 1)
                elif not first:
                    act.wait_ge(ring_free, out_index(g - 1, 1, False, last) + 1)
                nc.scalar.activation(oT[:], pv[:], ACT.Copy).then_inc(o_copied, 1)

            def body(g, nth, par, first, last):
                for u in range(NU):
                    _, n = unit_cols(u)
                    if not (first and u < PBUF):
                        act.wait_ge(pv_done, NU * g + u - PBUF + 1)
                    for pair in range(2):
                        act.wait_ge(st_ready, 2 * NU * g + 2 * u + pair + 1)
                        nc.scalar.activation(prob[u % PBUF][:, 2 * pair:2 * pair + 2, 0:n],
                                             st[pair][:, :, 0:n], ACT.Exp, scale=SCALE).then_inc(exp_done, 1)
                    if u == LAST[0] + LAG:
                        copy_out(g, 0, first, last)
                    if u == LAST[1] + LAG - NU and not first:
                        copy_out(g - 1, 1, False, False)
                if last:
                    copy_out(g, 1, first, last)

            groups(act, body)

        @block.tensor
        def _(pe):
            def ring_wait(n, at):
                if not (isinstance(n, int) and n < RING):
                    pe.wait_ge(ring_free, n - RING + 1)

            def scores_max(g, par, s, n, bank):
                i, h0, per, k0, keys, _ = STEPS[s]
                ring_wait(n, bank)
                for h in range(h0, h0 + per):
                    out = ring[bank][:, (h - h0) * keys:(h - h0 + 1) * keys]
                    last = nc.tensor.matmul(out, qT[par][0:MROW, i // 4, h, i % 4 * P:(i % 4 + 1) * P],
                                            kT[par][0:MROW, h, k0:k0 + keys], start=True, stop=True)
                    if k0 + keys == P * (i + 1):
                        last = nc.tensor.matmul(out[:, keys - P:keys], k["ident_bf"][:], k["mask"][:],
                                                start=False, stop=True, skip_group_check=True)
                last.then_inc(ring_ready, 1)

            def turn_max(g, half, n, bank, done):
                ring_wait(n, bank)
                if half:
                    pe.wait_ge(mx_joined, g + 1)
                else:
                    pe.wait_ge(ring_free, done)
                nc.tensor.transpose(ring[bank][0:HG * QB // 2, 0:P], mx[half][:].rearrange("p h i -> p (h i)"),
                                    k["ident"][:]).then_inc(ring_ready, 1)

            def turn_out(g, c, n, bank):
                ring_wait(n, bank)
                pe.wait_ge(o_copied, 2 * g + c + 1)
                for i in range(4):
                    last = nc.tensor.transpose(ring[bank][:, i * P:(i + 1) * P], oT[:, i * P:(i + 1) * P], k["ident"][:])
                last.then_inc(ring_ready, 1)

            def scores(g, par, u, pair, first):
                c, j = UNITS[u]
                q0, n = unit_cols(u)
                if not (first and u == 0):
                    pe.wait_ge(exp_done, 2 * NU * g + 2 * u + pair - 1)
                for h in range(2):
                    hh = 2 * pair + h
                    mm = nc.tensor.matmul(st[pair][:, h, 0:n], kT[par][0:MROW + PARTS, hh, j * P:(j + 1) * P],
                                          qT[par][0:MROW + PARTS, c, hh, q0 - c * CH:q0 - c * CH + n], start=True, stop=True)
                mm.then_inc(st_ready, 1)

            def product(g, par, u, very_first):
                c, j = UNITS[u]
                q0, n = unit_cols(u)
                off = q0 - c * CH
                if u == 0:
                    pe.wait_ge(v_set, g + 1)
                if u in (0, LAST[0] + 1) and not very_first:
                    pe.wait_ge(o_copied, 2 * g + (u > 0))
                if j >= 4 * c:
                    d = sum(jj >= 4 * cc for cc, jj in UNITS[:u + 1])
                    pe.wait_ge(sel_done, NDIAG * g + d)
                else:
                    pe.wait_ge(exp_done, 2 * NU * g + 2 * u + 2)
                for h in range(HG):
                    last = nc.tensor.matmul(pv[VW * h:VW * (h + 1), off:off + n], v[par][:, j, h, :],
                                            prob[u % PBUF][:, h, 0:n], start=(j == 0), stop=True,
                                            skip_group_check=True)
                last.then_inc(pv_done, 1)

            pe.wait_ge(lo_loaded[0], NL)
            pe.wait_ge(hi_loaded[0], NL)
            for n, (what, x, _) in enumerate(START):
                if what == "step":
                    scores_max(0, 0, x, n, n % RING)
                else:
                    turn_max(0, 0, n, n % RING, HALF_STEPS)

            def body(g, nth, par, first, last):
                base, at = ring_base(g, first)
                for u, (c, j) in enumerate(UNITS):
                    if u == 0:
                        pe.wait_ge(m_loaded, 16 * PARTS * (2 * g + 1))
                        if not last:
                            pe.wait_ge(lo_loaded[1 - par], NL * (nth + par + 1))
                    if u == LAST[0] + 1:
                        pe.wait_ge(m_loaded, 16 * PARTS * (2 * g + 2))
                    for what, x, y in ORDER[u]:
                        if what == "scores":
                            scores(g, par, u, x, first)
                        elif what == "product":
                            back = u < LAG
                            if not (first and back):
                                product(g - back, (1 - par) if back else par, (u - LAG) % NU, first and u == LAG)
                        elif not skipped(what, y, first, last):
                            n, bank = base + at, (ring_start(first) + at) % RING
                            if what == "step":
                                if x == FIRST_HI:
                                    pe.wait_ge(hi_loaded[1 - par], NL * (nth + par + 1))
                                scores_max(g + 1, 1 - par, x, n, bank)
                            elif what == "max":
                                turn_max(g + 1 - x, x, n, bank, base + HALF_STEPS_AT[first] + 1)
                            elif what == "out":
                                turn_out(g - y, x, n, bank)
                            at += 1
                if last:
                    for w in range(NU - LAG, NU):
                        product(g, par, w, False)
                    turn_out(g, 1, base + at, (ring_start(first) + at) % RING)

            groups(pe, body)

        @block.vector
        def _(dve):
            def row_max(s, n, bank):
                i, h0, per, _, keys, piece = STEPS[s]
                dve.wait_ge(ring_ready, n + 1)
                half = i // (QB // 2)
                dst = (mx2 if piece else mx[half])[:, h0:h0 + per, i % (QB // 2)]
                nc.vector.tensor_reduce(dst, ring[bank][:, 0:per * keys].rearrange("p (h k) -> p h k", k=keys),
                                        AX.X, ALU.max).then_inc(ring_free, 1)

            def join_max(n):
                dve.wait_ge(ring_free, n + 1)
                nc.vector.tensor_tensor(mx[1][:], mx[1][:], mx2[:], ALU.max).then_inc(mx_joined, 1)

            def cut_max(k, n, bank):
                dve.wait_ge(ring_ready, n + 1)
                if not (isinstance(k, int) and k == 0):
                    dve.wait_ge(m_loaded, 16 * PARTS * k)
                src = ring[bank][0:HG * QB // 2, 0:P]
                nc.vector.tensor_scalar(mneg[:, 0, :], src, -1.0, None, ALU.mult).then_inc(m_chain, 1)
                dve.wait_ge(m_chain, 2 * k + 1)
                nc.vector.scalar_tensor_tensor(out=mrest[:], in0=src, scalar=-1.0, in1=mneg[:, 0, :],
                                               op0=ALU.mult, op1=ALU.subtract).then_inc(ring_free, 1)
                dve.wait_ge(ring_free, n + 1)
                nc.vector.tensor_copy(mneg[:, 1, :], mrest[:]).then_inc(m_chain, 1)
                dve.wait_ge(m_chain, 2 * k + 2)
                nc.vector.tensor_tensor(mneg[:, 2, :], mrest[:], mneg[:, 1, :], ALU.subtract).then_inc(m_cut, 1)

            def norm_out(g, c, n, bank):
                dve.wait_ge(ring_ready, n + 1)
                o = ring[bank][:].rearrange("p (i h w) -> p i h w", i=4, w=VW)
                nc.vector.reciprocal(rec[:], o[:, :, :, HD]).then_inc(rec_done, 1)
                dve.wait_ge(rec_done, 2 * g + c + 1)
                dst = ctx_sb[:, g, 4 * c:4 * c + 4, :]
                nc.vector.tensor_tensor(dst.rearrange("p i (h d) -> p i h d", d=HD), o[:, :, :, 0:HD],
                                        rec[:].unsqueeze(3).broadcast_to([P, 4, HG, HD]),
                                        ALU.mult).then_inc(ring_free, 1)

            for n, (what, x, _) in enumerate(START):
                if what == "step":
                    row_max(x, n, n % RING)
                    if x == NSTEP - 1:
                        join_max(n)
                else:
                    cut_max(0, n, n % RING)

            def body(g, nth, par, first, last):
                base, at = ring_base(g, first)
                for u in range(NU):
                    for what, x, y in ORDER[u]:
                        if what in ("scores", "product") or skipped(what, y, first, last):
                            continue
                        n, bank = base + at, (ring_start(first) + at) % RING
                        if what == "step":
                            row_max(x, n, bank)
                            if x == NSTEP - 1:
                                join_max(n)
                        elif what == "max":
                            cut_max(2 * (g + 1 - x) + x, n, bank)
                        elif what == "out":
                            norm_out(g - y, x, n, bank)
                        at += 1
                if last:
                    norm_out(g, 1, base + at, (ring_start(first) + at) % RING)

            groups(dve, body)


def close_attention(nc, tag, ctx_sb, x, xn, xnT, xn_dram, wo, bo, router, top, at, ident):
    N = TILES // 4
    with ExitStack() as ctx:
        sem = lambda n: ctx.enter_context(nc.semaphore(f"{tag}_{n}"))
        ps = lambda n: [ctx.enter_context(nc.psum_tensor(f"{tag}_{n}{i}", [P, CH], F32)) for i in range(2)]
        t_bank, o_bank = ps("t"), ps("o")
        cT = [ctx.enter_context(nc.sbuf_tensor(f"{tag}_cT{i}", [P, CH], F32)) for i in range(2)]
        rows = [ctx.enter_context(nc.sbuf_tensor(f"{tag}_rows{i}", [P, 4, D], F32)) for i in range(2)]
        logit_bank = [ctx.enter_context(nc.psum_tensor(f"{tag}_logits{i}", [P, 4, E_N], F32)) for i in range(2)]
        logits = ctx.enter_context(nc.sbuf_tensor(f"{tag}_logits", [P, TILES, E_N], F32))
        norm = Norm(nc, ctx, tag, x, xn, xnT, ident)
        gathered = sem("gathered")
        turned, copied, made, added, biased = sem("ctx_turned"), sem("ctx_copied"), sem("made"), sem("added"), sem("biased")
        logits_made, logits_got, tops, at_done, xn_out = (sem("logits_made"), sem("logits_got"), sem("tops"),
                                                          sem("at_done"), sem("xn_out"))
        block = ctx.enter_context(nc.Block())
        LAGGING = 2

        @block.tensor
        def _(pe):
            for n in range(N + 3):
                if n < N:
                    pe.wait_ge(gathered, n + 1)
                    if n >= 2:
                        pe.wait_ge(copied, n - 1)
                    for i in range(4):
                        last = nc.tensor.transpose(t_bank[n % 2][:, i * P:(i + 1) * P], rows[n % 2][:, i, :],
                                                   ident[:])
                    last.then_inc(turned, 1)
                if 0 <= n - 1 < N:
                    m = n - 1
                    pe.wait_ge(copied, m + 1)
                    if m >= 2:
                        pe.wait_ge(added, m - 1)
                    for i in range(4):
                        last = nc.tensor.matmul(o_bank[m % 2][:, i * P:(i + 1) * P], cT[m % 2][:, i * P:(i + 1) * P],
                                                wo, start=True, stop=True)
                    last.then_inc(made, 1)
                if 0 <= n - 2 < N:
                    norm.turn(pe, n - 2)
                if 0 <= n - 3 < N:
                    m = n - 3
                    pe.wait_ge(norm.copied, m + 1)
                    if m >= 2:
                        pe.wait_ge(logits_got, m - 1)
                    for i in range(4):
                        t = 4 * m + i
                        last = nc.tensor.matmul(logit_bank[m % 2][:, i, :], xnT[:, t * P:(t + 1) * P], router,
                                                start=True, stop=True)
                    last.then_inc(logits_made, 1)

        @block.scalar
        def _(act):
            for n in range(N + 2):
                if n < N:
                    if n >= 2:
                        act.wait_ge(turned, n - 1)
                    seq, half = divmod(n, S // CH)
                    groups = ctx_sb[:, seq * (H // HG):(seq + 1) * (H // HG), 4 * half:4 * half + 4, :]
                    nc.scalar.activation(rows[n % 2][:].rearrange("p k (g w) -> p k g w", w=HG * HD),
                                         groups.rearrange("p g k w -> p k g w"), ACT.Copy).then_inc(gathered, 1)
                if 0 <= n - 2 < N:
                    norm.copy(act, n - 2)
                if n < N:
                    act.wait_ge(turned, n + 1)
                    if n >= 2:
                        act.wait_ge(made, n - 1)
                    nc.scalar.activation(cT[n % 2][:], t_bank[n % 2][:], ACT.Copy).then_inc(copied, 1)

        @block.gpsimd
        def _(pool):
            for n in range(N + 1):
                if bo is not None and n < N:
                    for t in range(4 * n, 4 * n + 4):
                        nc.gpsimd.tensor_tensor(x[:, t, :], x[:, t, :], bo[:], ALU.add).then_inc(biased, 1)
                if n >= 1:
                    norm.help(pool, n - 1)

        @block.vector
        def _(dve):
            def top_of(c, i):
                if i == 0:
                    dve.wait_ge(logits_made, c + 1)
                    nc.vector.tensor_copy(logits[:, 4 * c:4 * c + 4, :], logit_bank[c % 2][:]).then_inc(logits_got, 1)
                elif i < 5:
                    t = 4 * c + i - 1
                    dve.wait_ge(logits_got, c + 1)
                    nc.vector.max(top[:, t, :], logits[:, t, :]).then_inc(tops, 1)
                elif i < 9:
                    t = 4 * c + i - 5
                    dve.wait_ge(tops, t + 1)
                    nc.vector.max_index(at[:, t, :], top[:, t, :], logits[:, t, :]).then_inc(at_done, 1)

            for n in range(N + LAGGING):
                if n < N:
                    dve.wait_ge(made, n + 1)
                    if bo is not None:
                        dve.wait_ge(biased, 4 * n + 4)
                    xs = x[:, 4 * n:4 * n + 4, :]
                    nc.vector.tensor_tensor(xs, o_bank[n % 2][:].rearrange("p (i d) -> p i d", d=D), xs,
                                            ALU.add).then_inc(added, 1)
                    dve.wait_ge(added, n + 1)
                    norm.normalise(dve, n, (lambda i: top_of(n - LAGGING, i)) if n >= LAGGING else (lambda i: None))
                else:
                    for i in range(9):
                        top_of(n - LAGGING, i)

        @block.sync
        def _(sp):
            for c in range(B):
                norm.wait_xn(sp, 2 * (c + 1))
                sp.dma_start(xn_dram[c * S:(c + 1) * S, :].rearrange("(t p) d -> p t d", p=P),
                             xn[:, c * QB:(c + 1) * QB, :]).then_inc(xn_out, 16)
            sp.wait_ge(xn_out, 16 * B)


def route(nc, tag, top, at, k, gate, take, give, tile_expert):
    with ExitStack() as ctx:
        sb = lambda n, s, d=F32: ctx.enter_context(nc.sbuf_tensor(f"{tag}_{n}", s, d))
        ps = lambda n, s: ctx.enter_context(nc.psum_tensor(f"{tag}_{n}", s, F32))
        sem = lambda n: ctx.enter_context(nc.semaphore(f"{tag}_{n}"))
        before = ps("before", [P, E_N, PAIRS])
        total = ps("total", [P, E_N, PAIRS])
        inverse_parts = ps("inverse", [P, 2, XTILES])
        atf = sb("atf", [P, 2, TILES])
        den = sb("den", [P, TILES])
        hot = sb("hot", [P, E_N, PAIRS], BF16)
        run = sb("run", [P, E_N, PAIRS])
        pos = sb("pos", [P, E_N, PAIRS])
        sel = sb("sel", [P, E_N, PAIRS])
        count = sb("count", [P, E_N])
        more = sb("more", [P, E_N, TILES])
        ntile, end, shift = sb("ntile", [P, E_N]), sb("end", [P, E_N]), sb("shift", [P, E_N])
        past = sb("past", [1, XTILES, E_N])
        texp = sb("texp", [1, XTILES])
        slot = sb("slot", [P, PAIRS], U32)
        slot_tile_u, slot_row_u = sb("slot_tile_u", [P, PAIRS], U32), sb("slot_row_u", [P, PAIRS], U32)
        slots = sb("slots", [P, PAIRS])
        slot_tile, slot_row = sb("slot_tile", [P, PAIRS], BF16), sb("slot_row", [P, PAIRS], BF16)
        NB = 3
        row_hot = [sb(f"row_hot{i}", [P, P, STEP], BF16) for i in range(NB)]
        tile_hot = [sb(f"tile_hot{i}", [P, XTILES, STEP], BF16) for i in range(NB)]
        hot_id = [sb(f"hot_id{i}", [P, 2, XTILES, STEP], BF16) for i in range(NB)]
        inverse = sb("inverse_sum", [P, XTILES])
        spare, pair0, wrap = sb("spare", [P, XTILES]), sb("pair0", [P, XTILES]), sb("wrap", [P, XTILES])
        exp_done, small = sem("exp_done"), sem("small")
        hot_done, counted = sem("hot_done"), sem("counted")
        placed = sem("placed")
        rows_hot, tiles_hot, mixed = sem("rows_hot"), sem("tiles_hot"), sem("mixed")
        token_id = sem("token_id")
        tile_id = [sem("tile_id_pool"), sem("tile_id_dve")]
        block = ctx.enter_context(nc.Block())

        def times_tile(engine, m):
            tiles = k["count_up_bf"][:, STEP * m:STEP * (m + 1)].unsqueeze(1)
            engine.tensor_tensor(hot_id[m % NB][:, 1, :, :], tile_hot[m % NB][:],
                                 tiles.broadcast_to([P, XTILES, STEP]), ALU.mult).then_inc(tile_id[m % 2], 1)

        @block.tensor
        def _(pe):
            pe.wait_ge(hot_done, 1)
            nc.tensor.matmul(before[:], k["earlier"][:], hot[:], start=True, stop=True).then_inc(counted, 1)
            nc.tensor.matmul(total[:], k["all_ones"][:], hot[:], start=True, stop=True).then_inc(counted, 1)
            for m in range(PAIRS // STEP):
                pe.wait_ge(rows_hot, m + 1)
                pe.wait_ge(token_id, m + 1)
                pe.wait_ge(tile_id[m % 2], m // 2 + 1)
                for i in range(STEP):
                    last = nc.tensor.matmul(inverse_parts[:], row_hot[m % NB][:, :, i], hot_id[m % NB][:, :, :, i],
                                            start=(m == 0 and i == 0), stop=(m == PAIRS // STEP - 1 and i == STEP - 1))
                last.then_inc(mixed, 1)

        @block.scalar
        def _(act):
            act.wait_ge(small, 1)
            nc.scalar.activation(gate[:, 1, :], den[:], ACT.Exp).then_inc(exp_done, 1)
            for m in range(PAIRS // STEP):
                act.wait_ge(tiles_hot, m + 1)
                if m >= NB:
                    act.wait_ge(mixed, m - NB + 1)
                nc.scalar.activation(hot_id[m % NB][:, 0, :, :], tile_hot[m % NB][:], ACT.Copy,
                                     scale=k["token_no"][:, 0:1]).then_inc(token_id, 1)

        @block.gpsimd
        def _(pool):
            for m in range(0, PAIRS // STEP, 2):
                pool.wait_ge(tiles_hot, m + 1)
                if m >= NB:
                    pool.wait_ge(mixed, m - NB + 1)
                times_tile(nc.gpsimd, m)

        @block.vector
        def _(dve):
            nc.vector.tensor_tensor(den[:], top[:, :, 1], top[:, :, 0], ALU.subtract).then_inc(small, 1)
            nc.vector.tensor_copy(atf[:].rearrange("p k t -> p t k"), at[:, :, 0:2]).then_inc(small, 1)
            dve.wait_ge(small, 2)
            nc.vector.tensor_tensor(hot[:], atf[:].rearrange("p k t -> p (k t)").unsqueeze(1).broadcast_to([P, E_N, PAIRS]),
                                    k["count_up"][:, 0:E_N].unsqueeze(2).broadcast_to([P, E_N, PAIRS]),
                                    ALU.is_equal).then_inc(hot_done, 1)
            dve.wait_ge(exp_done, 1)
            nc.vector.tensor_scalar(den[:], gate[:, 1, :], 1.0, None, ALU.add).then_inc(small, 1)
            dve.wait_ge(small, 3)
            nc.vector.reciprocal(gate[:, 0, :], den[:]).then_inc(small, 1)
            dve.wait_ge(small, 4)
            nc.vector.tensor_tensor(gate[:, 1, :], gate[:, 1, :], gate[:, 0, :], ALU.mult).then_inc(small, 1)
            dve.wait_ge(counted, 2)
            flat = lambda m: m[:].rearrange("p e n -> p (e n)")
            nc.vector.tensor_tensor_scan(flat(run), k["ones_row"][:], flat(total), 0.0, ALU.mult,
                                         ALU.add).then_inc(small, 1)
            dve.wait_ge(small, 6)
            nc.vector.tensor_tensor(run[:], run[:], total[:], ALU.subtract).then_inc(small, 1)
            dve.wait_ge(small, 7)
            nc.vector.tensor_tensor(pos[:], run[:], before[:], ALU.add).then_inc(small, 1)
            nc.vector.tensor_reduce(count[:], total[:], AX.X, ALU.add).then_inc(small, 1)
            dve.wait_ge(small, 9)
            nc.vector.tensor_tensor(more[:], count[:].unsqueeze(2).broadcast_to([P, E_N, TILES]),
                                    k["by_tile"][:].unsqueeze(1).broadcast_to([P, E_N, TILES]),
                                    ALU.is_gt).then_inc(small, 1)
            dve.wait_ge(small, 10)
            nc.vector.tensor_reduce(ntile[:], more[:], AX.X, ALU.add).then_inc(small, 1)
            dve.wait_ge(small, 11)
            nc.vector.tensor_tensor_scan(end[:], k["ones_row"][:, 0:E_N], ntile[:], 0.0, ALU.mult,
                                         ALU.add).then_inc(small, 1)
            dve.wait_ge(small, 12)
            nc.vector.tensor_tensor(shift[:], end[:], ntile[:], ALU.subtract).then_inc(small, 1)
            dve.wait_ge(small, 13)
            nc.vector.scalar_tensor_tensor(out=shift[:], in0=shift[:], scalar=float(P), in1=run[:, :, 0],
                                           op0=ALU.mult, op1=ALU.subtract).then_inc(small, 1)
            dve.wait_ge(small, 14)
            nc.vector.tensor_tensor(pos[:], pos[:], shift[:].unsqueeze(2).broadcast_to([P, E_N, PAIRS]),
                                    ALU.add).then_inc(small, 1)
            dve.wait_ge(small, 15)
            nc.vector.tensor_tensor(sel[:], pos[:], hot[:], ALU.mult).then_inc(small, 1)
            dve.wait_ge(small, 16)
            nc.vector.tensor_reduce(slots[:], sel[:].rearrange("p e n -> p n e"), AX.X, ALU.add).then_inc(small, 1)
            dve.wait_ge(small, 17)
            nc.vector.tensor_copy(slot[:], slots[:]).then_inc(small, 1)
            dve.wait_ge(small, 18)
            nc.vector.tensor_scalar(slot_tile_u[:], slot[:], 7, None, ALU.logical_shift_right).then_inc(small, 1)
            nc.vector.tensor_scalar(slot_row_u[:], slot[:], P - 1, None, ALU.bitwise_and).then_inc(small, 1)
            dve.wait_ge(small, 20)
            nc.vector.tensor_copy(slot_tile[:], slot_tile_u[:]).then_inc(placed, 1)
            nc.vector.tensor_copy(slot_row[:], slot_row_u[:]).then_inc(placed, 1)
            dve.wait_ge(placed, 2)
            for m in range(PAIRS // STEP):
                if m >= NB:
                    dve.wait_ge(mixed, m - NB + 1)
                for width, dst, place, done in ((XTILES, tile_hot, slot_tile, tiles_hot), (P, row_hot, slot_row, rows_hot)):
                    here = place[:, STEP * m:STEP * (m + 1)].unsqueeze(1)
                    nc.vector.tensor_tensor(dst[m % NB][:], k["count_steps"][:, 0:width, :],
                                            here.broadcast_to([P, width, STEP]), ALU.is_equal).then_inc(done, 1)
                if m % 2:
                    dve.wait_ge(tiles_hot, m + 1)
                    times_tile(nc.vector, m)
            nc.vector.tensor_tensor(past[:], k["count_up"][0:1, 0:XTILES].unsqueeze(2).broadcast_to([1, XTILES, E_N]),
                                    end[0:1, :].unsqueeze(1).broadcast_to([1, XTILES, E_N]),
                                    ALU.is_ge).then_inc(small, 1)
            dve.wait_ge(small, 21)
            nc.vector.tensor_reduce(texp[:], past[:], AX.X, ALU.add).then_inc(small, 1)
            dve.wait_ge(small, 22)
            nc.vector.tensor_scalar(tile_expert[:], texp[:], float(E_N - 1), None, ALU.min).then_inc(small, 1)
            dve.wait_ge(mixed, PAIRS // STEP)
            nc.vector.tensor_scalar(wrap[:], inverse_parts[:, 1, :], float(P), None, ALU.mult).then_inc(small, 1)
            dve.wait_ge(small, 24)
            nc.vector.tensor_tensor(inverse[:], wrap[:], inverse_parts[:, 0, :], ALU.add).then_inc(small, 1)
            dve.wait_ge(small, 25)
            nc.vector.scalar_tensor_tensor(out=spare[:], in0=inverse[:], scalar=0.0, in1=k["spare_row"][:],
                                           op0=ALU.is_equal, op1=ALU.mult).then_inc(small, 1)
            nc.vector.tensor_scalar(pair0[:], inverse[:], -1.0, 0.0, ALU.add, ALU.max).then_inc(small, 1)
            dve.wait_ge(small, 27)
            nc.vector.scalar_tensor_tensor(out=give[:], in0=inverse[:], scalar=-1.0, in1=spare[:], op0=ALU.add,
                                           op1=ALU.add).then_inc(small, 1)
            nc.vector.tensor_scalar(wrap[:], pair0[:], float(NT), float(NT), ALU.is_ge, ALU.mult).then_inc(small, 1)
            dve.wait_ge(small, 29)
            nc.vector.tensor_tensor(take[:], pair0[:], wrap[:], ALU.subtract).then_inc(small, 1)


def experts(nc, tag, xn_dram, y_dram, take, give, tile_expert, w1, w2, ident, gathered, put, turn_no):
    XB, YB = len(gathered), len(put)
    N = XTILES // UNROLL
    G0, P0 = 2 * N * turn_no, N * turn_no
    with ExitStack() as ctx:
        sb = lambda n, s, d=F32: ctx.enter_context(nc.sbuf_tensor(f"{tag}_{n}", s, d))
        sem = lambda n: ctx.enter_context(nc.semaphore(f"{tag}_{n}"))
        ps = lambda n: [ctx.enter_context(nc.psum_tensor(f"{tag}_{n}{i}", [P, CH], F32)) for i in range(2)]
        t_bank, h_bank, y_bank = ps("t"), ps("h"), ps("y")
        xg = [sb(f"xg{i}", [P, D]) for i in range(XB)]
        xT = [sb(f"xT{i}", [P, P]) for i in range(2)]
        w1e = [sb(f"w1e{i}", [P, FF]) for i in range(2)]
        hs = [sb(f"hs{i}", [P, FC, P]) for i in range(2)]
        yo = [sb(f"yo{i}", [P, D]) for i in range(YB)]
        take4 = [sb(f"take4_{i}", [P, 4], U32) for i in range(2)]
        give4 = [sb(f"give4_{i}", [P, 4], U32) for i in range(2)]
        indexed, turned, xT_ready, w_ready = sem("indexed"), sem("turned"), sem("xT_ready"), sem("w_ready")
        passed = sem("passed")
        h_made, h_ready, y_made, y_ready = sem("h_made"), sem("h_ready"), sem("y_made"), sem("y_ready")
        block = ctx.enter_context(nc.Block())

        @block.gpsimd
        def _(pool):
            def take_waits():
                pool.sem_inc(passed, 1)

            def gather(j, r):
                t = UNROLL * j + r
                if not (isinstance(j, int) and t < XB):
                    pool.wait_ge(turned, t - XB + 1)
                take_waits()
                pool.indirect_dma_start(xg[r % XB][:], None, xn_dram,
                                        bass.IndirectOffsetOnAxis(take4[r // 4][:, r % 4:r % 4 + 1], 0)
                                        ).then_inc(gathered[r % XB], 16)

            def scatter(j, r):
                pool.wait_ge(y_ready, UNROLL * j + r + 1)
                take_waits()
                pool.indirect_dma_start(y_dram, bass.IndirectOffsetOnAxis(give4[r // 4][:, r % 4:r % 4 + 1], 0),
                                        yo[r][:], None).then_inc(put[r], 16)

            def give_index(j, half, first):
                if not first:
                    for r in range(4 * half, 4 * half + 4):
                        pool.wait_ge(put[r], 16 * (j + P0))
                    take_waits()
                nc.gpsimd.tensor_copy(give4[half][:], give[:, bass.ds(UNROLL * j + 4 * half, 4)]).then_inc(indexed, 1)

            def body(j, first, second):
                for r in range(UNROLL):
                    if r % 4 == 0:
                        nc.gpsimd.tensor_copy(take4[r // 4][:], take[:, bass.ds(UNROLL * j + r, 4)]).then_inc(indexed, 1)
                        if not first:
                            give_index(j - 1, r // 4, second)
                        pool.wait_ge(indexed, (r // 4 + 1) if first else 4 * j - 2 + 2 * (r // 4 + 1))
                    gather(j, r)
                    if not first:
                        scatter(j - 1, r)

            body(0, True, False)
            body(1, False, True)
            with pool.Fori(2, N) as j:
                body(j, False, False)
            for r in range(UNROLL):
                if r % 4 == 0:
                    give_index(N - 1, r // 4, False)
                    pool.wait_ge(indexed, 4 * N - 2 + r // 4 + 1)
                scatter(N - 1, r)
            for r in range(UNROLL):
                pool.wait_ge(put[r], 16 * (N + P0))

        @block.tensor
        def _(pe):
            def turn(j, r):
                t = UNROLL * j + r
                if not (isinstance(j, int) and t < 2):
                    pe.wait_ge(xT_ready, t - 1)
                pe.wait_ge(gathered[r % XB], 16 * (2 * j + r // XB + 1 + G0))
                nc.tensor.transpose(t_bank[r % 2][:, 0:P], xg[r % XB][:], ident[:]).then_inc(turned, 1)

            def up(t, r):
                pe.wait_ge(xT_ready, t + 1)
                pe.wait_ge(w_ready, t + 1)
                if not (isinstance(t, int) and t < 2):
                    pe.wait_ge(h_ready, t - 1)
                for f in range(FC):
                    last = nc.tensor.matmul(h_bank[r % 2][:, f * P:(f + 1) * P], w1e[r % 2][:, f * P:(f + 1) * P],
                                            xT[r % 2][:], start=True, stop=True)
                last.then_inc(h_made, 1)

            def down(t, r, e):
                pe.wait_ge(h_ready, t + 1)
                if not (isinstance(t, int) and t < 2):
                    pe.wait_ge(y_ready, t - 1)
                for f in range(FC):
                    last = nc.tensor.matmul(y_bank[r % 2][:, 0:D], hs[r % 2][:, f, :], w2[:, bass.ds(e, 1), f, :],
                                            start=(f == 0), stop=(f == FC - 1))
                last.then_inc(y_made, 1)

            def expert(t):
                return pe.value_load(tile_expert[0:1, bass.ds(t, 1)], min_val=0, max_val=E_N - 1)

            def body(j, first):
                for r in range(UNROLL):
                    t = UNROLL * j + r
                    turn(j, r)
                    if not (first and r < 1):
                        up(t - 1, r - 1)
                    if not (first and r < 2):
                        down(t - 2, r, expert(t - 2))

            body(0, True)
            with pe.Fori(1, N) as j:
                body(j, False)
            up(XTILES - 1, 1)
            down(XTILES - 2, 0, expert(XTILES - 2))
            down(XTILES - 1, 1, expert(XTILES - 1))

        @block.vector
        def _(dve):
            def body(j, first):
                for r in range(UNROLL):
                    t = UNROLL * j + r
                    if not (first and r < 2):
                        dve.wait_ge(h_made, t - 1)
                    e = dve.value_load(tile_expert[0:1, bass.ds(t, 1)], min_val=0, max_val=E_N - 1)
                    nc.vector.tensor_scalar(w1e[r % 2][:], w1[:, bass.ds(e, 1), :].rearrange("p e f -> p (e f)"), 1.0, None,
                                            ALU.mult).then_inc(w_ready, 1)
                    dve.wait_ge(turned, t + 1)
                    nc.vector.tensor_copy(xT[r % 2][:], t_bank[r % 2][:, 0:P]).then_inc(xT_ready, 1)

            body(0, True)
            with dve.Fori(1, N) as j:
                body(j, False)

        @block.scalar
        def _(act):
            def gelu(t, r):
                act.wait_ge(h_made, t + 1)
                if not (isinstance(t, int) and t < 2):
                    act.wait_ge(y_made, t - 1)
                nc.scalar.activation(hs[r % 2][:].rearrange("p f s -> p (f s)"), h_bank[r % 2][:],
                                     ACT.Gelu).then_inc(h_ready, 1)

            def results(j, r, first):
                act.wait_ge(y_made, UNROLL * j + r + 1)
                if not first:
                    act.wait_ge(put[r], 16 * (j + P0))
                nc.scalar.activation(yo[r][:], y_bank[r % 2][:, 0:D], ACT.Copy).then_inc(y_ready, 1)

            def body(j, first, second):
                for r in range(UNROLL):
                    gelu(UNROLL * j + r, r)
                    if r:
                        results(j, r - 1, first)
                    elif not first:
                        results(j - 1, UNROLL - 1, second)

            body(0, True, False)
            body(1, False, True)
            with act.Fori(2, N) as j:
                body(j, False, False)
            results(N - 1, UNROLL - 1, False)


def close(nc, x, gate, y_dram, out):
    N = TILES // 4
    with ExitStack() as ctx:
        adder = Adder(nc, ctx, "close", x, gate, y_dram, buffers=N)
        out_done = ctx.enter_context(nc.semaphore("out_done"))
        block = ctx.enter_context(nc.Block())

        @block.sync
        def _(sp):
            rows = out.rearrange("b (h t p) d -> (b h) p t d", t=4, p=P)
            for c in range(N):
                adder.load(sp, c)
            for c in range(N):
                sp.wait_ge(adder.added, 4 * (c + 1))
                sp.dma_start(rows[c], x[:, 4 * c:4 * c + 4, :]).then_inc(out_done, 16)
            sp.wait_ge(out_done, 16 * N)

        @block.scalar
        def _(act):
            for c in range(N):
                adder.scale(act, c)

        @block.gpsimd
        def _(pool):
            for c in range(N):
                adder.add_first(pool, c)

        @block.vector
        def _(dve):
            for c in range(N):
                for i in range(4):
                    adder.add_second(dve, c, i)


def hybrid_block(nc, a, out):
    with ExitStack() as ctx:
        sb = lambda n, s, d=F32: ctx.enter_context(nc.sbuf_tensor(n, s, d))
        x = sb("x", [P, TILES, D])
        xn = sb("xn", [P, TILES, D])
        xnT = sb("xnT", [P, NT])
        ident = sb("ident", [P, P])
        ident_bf = sb("ident_bf", [P, P], BF16)
        mask = sb("mask", [P, P], BF16)
        earlier = sb("earlier", [P, P], BF16)
        all_ones = sb("all_ones", [P, P], BF16)
        count_up = sb("count_up", [P, P])
        by_tile = sb("by_tile", [P, TILES])
        count_up_bf = sb("count_up_bf", [P, P], BF16)
        count_steps = sb("count_steps", [P, P, STEP], BF16)
        token_no = sb("token_no", [P, 1])
        spare_row = sb("spare_row", [P, XTILES])
        ones_row = sb("ones_row", [P, E_N * PAIRS])
        top, at = sb("top", [P, TILES, 8]), sb("at", [P, TILES, 8], U32)
        gate = sb("gate", [P, 2, TILES])
        take, give = sb("take", [P, XTILES], U32), sb("give", [P, XTILES], U32)
        tile_expert = sb("tile_expert", [1, XTILES], I32)
        w1 = sb("w1", [P, E_N, FF])
        w2 = sb("w2", [P, E_N, FC, D])
        router = sb("router", [P, E_N])
        wA = {n: sb(f"wA_{n}", [P, D]) for n in "qkvo"}
        lora_a = {n: sb(f"lora_a_{n}", [16, D]) for n in "qkvo"}
        lora_b = {n: sb(f"lora_b_{n}", [16, D]) for n in "qkvo"}
        b_wq, b_wo = sb("b_wq", [P, D]), sb("b_wo", [P, D])
        b_wkd, b_wku = sb("b_wkd", [P, 64]), sb("b_wku", [64, 2 * D])
        b_bq, b_bk, b_bkd = sb("b_bq", [P, 1]), sb("b_bk", [P, 1]), sb("b_bkd", [64, 1])
        b_bv, b_bo = sb("b_bv", [P, D]), sb("b_bo", [P, D])
        q_dram = nc.dram_tensor("q_parts", (B, D, PARTS, S), BF16).ap()
        k_dram = nc.dram_tensor("k_parts", (PARTS, B, D, PARTS, S), BF16).ap()
        by_group = xnT[:].rearrange("p (g t w) -> p g t w", g=GROUPS, t=QB)
        qT = [sb(f"qT{i}", [P, 2, HG, CH], BF16) for i in range(2)]
        kT = [sb(f"kT{i}", [P, HG, S], BF16) for i in range(2)]
        v = [sb(f"v{i}", [P, QB, HG, VW]) for i in range(2)]
        xn_dram = nc.dram_tensor("xn_rows", (NT, D), F32).ap()
        y_dram = nc.dram_tensor("expert_rows", (2 * NT + XTILES * P, D), F32).ap()
        x_in = [ctx.enter_context(nc.semaphore(f"x_in{c}")) for c in range(B)]
        loaded = [[[ctx.enter_context(nc.semaphore(f"loaded_{layer}{half}{par}")) for par in range(2)]
                   for half in range(2)] for layer in "ab"]
        later_in = ctx.enter_context(nc.semaphore("later_in"))
        bias = a["bku"]
        later = [(router[:], a["router"]), (b_wq[:], a["b_wq"]), (b_wo[:], a["b_wo"]),
                 (b_wkd[:], a["b_wkd"]), (b_wku[0:32, :], a["b_wku"]), (b_wku[32:64, :], a["b_wku"]),
                 (b_bq[:], a["bq"].unsqueeze(1)), (b_bk[:], bias[0:D].unsqueeze(1)),
                 (b_bkd[:], a["bkd"].unsqueeze(1)), (b_bv[:], bias[D:2 * D].partition_broadcast(P)),
                 (b_bo[:], a["bo"].partition_broadcast(P)), (w1[:], a["w1"]), (w2[:], a["w2"])]
        gathered = [ctx.enter_context(nc.semaphore(f"gathered{i}")) for i in range(4)]
        put = [ctx.enter_context(nc.semaphore(f"put{i}")) for i in range(UNROLL)]
        consts = {"ident": ident, "ident_bf": ident_bf, "mask": mask, "earlier": earlier, "all_ones": all_ones,
                  "count_up": count_up, "by_tile": by_tile, "count_up_bf": count_up_bf,
                  "count_steps": count_steps, "token_no": token_no, "spare_row": spare_row,
                  "ones_row": ones_row, "qT": qT, "kT": kT, "v": v}

        with ExitStack() as c2:
            sem = lambda n: c2.enter_context(nc.semaphore(n))
            w_in, c0, folded, lora_done = sem("w_in"), sem("c0"), sem("folded"), sem("lora_done")
            c1, padded = sem("c1"), sem("padded")
            spent = [w_in, c0, c1, padded, folded, lora_done]
            bank = c2.enter_context(nc.psum_tensor("fold", [P, 4, D], F32))
            block = c2.enter_context(nc.Block())

            @block.sync
            def _(sp):
                for c in range(B):
                    sp.dma_start(x[:, c * QB:(c + 1) * QB, :],
                                 a["x"][c].rearrange("(t p) d -> p t d", p=P)).then_inc(x_in[c], 16)

            @block.scalar
            def _(act):
                for m in "qkvo":
                    for dst, src in ((wA[m], a["wT_" + m]), (lora_a[m], a["la_" + m]), (lora_b[m], a["lb_" + m])):
                        act.dma_start(dst[:], src).then_inc(w_in, 16)

            @block.gpsimd
            def _(pool):
                nc.gpsimd.memset(ident[:], 0.0)
                nc.gpsimd.memset(mask[:], 0.0).then_inc(c0, 1)
                for dst, step, n, base, by_row in ((count_up, 1, P, 0, 0), (by_tile, P, TILES, 0, 0),
                                                   (token_no, 1, 1, 1, 1), (spare_row, P, XTILES, 2 * NT + 1, 1)):
                    nc.gpsimd.iota(dst[:], pattern=[[step, n]], base=base, channel_multiplier=by_row,
                                   allow_small_or_imprecise_dtypes=True).then_inc(c1, 1)
                nc.gpsimd.memset(ones_row[:], 1.0).then_inc(c1, 1)
                nc.gpsimd.memset(all_ones[:], 1.0).then_inc(c1, 1)
                nc.gpsimd.memset(earlier[:], 1.0).then_inc(c1, 1)
                pool.wait_ge(c1, 7)
                nc.gpsimd.affine_select(out=earlier[:], in_=earlier[:], compare_op=ALU.is_gt, fill=0.0, base=0,
                                        pattern=[[1, P]], channel_multiplier=-1).then_inc(c1, 1)
                pool.wait_ge(c0, 1)
                nc.gpsimd.affine_select(out=ident[:], in_=ident[:], compare_op=ALU.not_equal, fill=1.0, base=0,
                                        pattern=[[-1, P]], channel_multiplier=1).then_inc(c0, 1)
                nc.gpsimd.affine_select(out=mask[:], in_=mask[:], compare_op=ALU.is_ge, fill=NEG, base=0,
                                        pattern=[[-1, P]], channel_multiplier=1).then_inc(c0, 1)
                pool.wait_ge(c0, 3)
                nc.gpsimd.tensor_copy(ident_bf[:], ident[:]).then_inc(c0, 1)
                nc.gpsimd.tensor_copy(count_up_bf[:], count_up[:]).then_inc(c0, 1)
                nc.gpsimd.tensor_copy(count_steps[:], count_up[:].unsqueeze(2).broadcast_to([P, P, STEP])).then_inc(c0, 1)
                pool.wait_ge(c0, 6)
                for i in range(2):
                    nc.gpsimd.memset(kT[i][MROW:MROW + PARTS, :, :], 1.0).then_inc(c1, 1)
                pool.wait_ge(c1, 10)
                for i in range(2):
                    nc.gpsimd.memset(v[i][:, :, :, HD:HD + 1], 1.0).then_inc(padded, 1)
                    nc.gpsimd.memset(v[i][:, :, :, HD + 1:VW], 0.0).then_inc(padded, 1)

            @block.tensor
            def _(pe):
                pe.wait_ge(w_in, 16 * 12)
                for n, m in enumerate("qkvo"):
                    last = nc.tensor.matmul(bank[:, n, :], lora_a[m][:], lora_b[m][:], start=True, stop=True)
                last.then_inc(lora_done, 1)

            @block.vector
            def _(dve):
                for i in range(2):
                    for dst in (qT[i][64:96, :, :, :].rearrange("p a h c -> p (a h c)"),
                                kT[i][64:96, :, :].rearrange("p h s -> p (h s)")):
                        nc.vector.memset(dst.bitcast(F32), 0.0).then_inc(padded, 1)
                dve.wait_ge(lora_done, 1)
                for n, m in enumerate("qkvo"):
                    nc.vector.scalar_tensor_tensor(out=wA[m][:], in0=bank[:, n, :], scalar=1.0 / 16, in1=wA[m][:],
                                                   op0=ALU.mult, op1=ALU.add).then_inc(folded, 1)

        with nc.sbuf_tensor("v_sb", [P, GROUPS, QB, HG * HD], F32) as v_sb:
            project(nc, "pa", x, xn, xnT, ident, x_in, None, v_sb, q_dram, k_dram, consts, loaded[0],
                    wA["q"][:], wA["k"][:], wA["v"][:], None, None, None, None, spent)
            attention(nc, "aa", v_sb, by_group, q_dram, k_dram, consts, loaded[0], later, later_in, spent)
        close_attention(nc, "oa", by_group, x, xn, xnT, xn_dram, wA["o"][:], None, router[:], top, at, ident)
        route(nc, "ra", top, at, consts, gate, take, give, tile_expert)
        experts(nc, "ea", xn_dram, y_dram, take, give, tile_expert, w1, w2, ident, gathered, put, 0)
        with nc.sbuf_tensor("v_sb2", [P, GROUPS, QB, HG * HD], F32) as v_sb:
            project(nc, "pb", x, xn, xnT, ident, None, (gate, y_dram), v_sb, q_dram, k_dram, consts, loaded[1],
                    b_wq[:], b_wku[:, 0:D], b_wku[:, D:2 * D], b_bq[:, 0:1], b_bk[:, 0:1], b_bv, {"wkd": b_wkd, "bkd": b_bkd}, spent)
            attention(nc, "ab", v_sb, by_group, q_dram, k_dram, consts, loaded[1], [], later_in, spent)
        close_attention(nc, "ob", by_group, x, xn, xnT, xn_dram, b_wo[:], b_bo, router[:], top, at, ident)
        route(nc, "rb", top, at, consts, gate, take, give, tile_expert)
        experts(nc, "eb", xn_dram, y_dram, take, give, tile_expert, w1, w2, ident, gathered, put, 1)
        close(nc, x, gate, y_dram, out)


def kernel(**inputs):
    import numpy as np
    import concourse.bacc as bacc
    from concourse.bass_utils import run_bass_kernel_spmd

    def get(n):
        return np.asarray(inputs[n])

    w1 = get("L0_ffn_w1")
    w2 = get("L0_ffn_w2")
    arrays = {"x": get("L0_attn_a_x")}
    for m in "qkvo":
        arrays["wT_" + m] = get(f"L0_attn_a_w{m}").T
        arrays["la_" + m] = get(f"L0_attn_a_a{m}")
        arrays["lb_" + m] = get(f"L0_attn_a_b{m}").T
    arrays.update(
        w1=w1.transpose(2, 0, 1),
        w2=w2.reshape(w2.shape[0], w2.shape[1], 4, 128).transpose(3, 0, 2, 1),
        router=get("L0_ffn_router_w").T,
        b_wq=get("L0_attn_b_Wq"), b_wo=get("L0_attn_b_Wo"), b_wkd=get("L0_attn_b_Wkd"), b_wku=get("L0_attn_b_Wku"),
        bq=get("L0_attn_b_bq"), bkd=get("L0_attn_b_bkd"), bku=get("L0_attn_b_bku"), bo=get("L0_attn_b_bo"),
    )
    nc = bacc.Bacc("TRN2", target_bir_lowering=False, num_devices=1)
    fed, a = {}, {}
    for name, value in arrays.items():
        value = np.ascontiguousarray(value)
        fed[f"in_{name}"] = value
        a[name] = nc.dram_tensor(f"in_{name}", value.shape, mybir.dt.from_np(value.dtype), kind="ExternalInput").ap()
    out = nc.dram_tensor("out", (B, S, D), F32, kind="ExternalOutput").ap()
    hybrid_block(nc, a, out)
    r = run_bass_kernel_spmd(nc, [fed], core_ids=[0])
    return r.results[0]["out"]
```
